# Optimizing a Trainium2 kernel written in Bass

```python
import numpy as np
import jax
import jax.numpy as jnp

def _softmax(x, axis=-1):
    return jax.nn.softmax(x, axis=axis)

def _gelu(x):
    return jax.nn.gelu(x, approximate=True)

def _silu(x):
    return jax.nn.silu(x)

def _sigmoid(x):
    return jax.nn.sigmoid(x)

def _layernorm(x, axis=-1, eps=1e-05):
    m = jnp.mean(x, axis=axis, keepdims=True)
    v = jnp.var(x, axis=axis, keepdims=True)
    return (x - m) / jnp.sqrt(v + eps)

def _scatter_add(tgt, idx, src, axis=0):
    return tgt.at[idx].add(src)

def _segment_sum(src, seg, n):
    return jax.ops.segment_sum(src, seg, n)
kernel_name = 'mk_gnn_preln_d2_gnn_r64_dba9a5'

def setup_inputs(seed: int=0):
    np.random.seed(seed)
    _w = jnp.asarray

    def _rec_inputs():
        import jax
        import jax.numpy as jnp
        _gk = jax.random.key(seed)
        x = -0.0009044 + 1 * jax.random.normal(jax.random.fold_in(_gk, 1), (100000, 16), jnp.float32)
        src = jax.random.randint(jax.random.fold_in(_gk, 2), (50000,), 0, 100000, jnp.int32)
        dst = jnp.minimum((100000 * jax.random.uniform(jax.random.fold_in(_gk, 3), (50000,)) ** 2.0).astype(jnp.int32), 99999)
        _o = jnp.argsort(dst, stable=True)
        src = src[_o]
        dst = dst[_o]
        edge_attr_16 = -3.57403e-05 + 0.999761 * jax.random.normal(jax.random.fold_in(_gk, 12), (50000, 16), jnp.float32)
        edge_attr_8 = 0.000398945 + 1.00003 * jax.random.normal(jax.random.fold_in(_gk, 13), (50000, 8), jnp.float32)
        return (x, src, dst, edge_attr_16, edge_attr_8)
    x, src, dst, edge_attr_16, edge_attr_8 = _rec_inputs()

    def _L0_gnn_setup():
        import jax, jax.numpy as jnp
        import numpy as np
        N_NODES = 100000
        N_EDGES = 12500
        IN_C = 16
        OUT_C = 16
        EDGE_DIM = 8
        HIDDEN = 64

        def _layernorm(h, w, b, eps=1e-05):
            mu = jnp.mean(h, axis=-1, keepdims=True)
            var = jnp.mean(jnp.square(h - mu), axis=-1, keepdims=True)
            return (h - mu) * jax.lax.rsqrt(var + eps) * w + b
        key = jax.random.key(seed)
        ks = jax.random.split(key, 12)
        x = jax.random.normal(ks[0], (N_NODES, IN_C), dtype=jnp.float32)
        edge_index = jax.random.randint(ks[1], (2, N_EDGES), 0, N_NODES, dtype=jnp.int64)
        edge_attr = jax.random.normal(ks[2], (N_EDGES, EDGE_DIM), dtype=jnp.float32)
        s1 = 1.0 / np.sqrt(EDGE_DIM)
        s2 = 1.0 / np.sqrt(HIDDEN)
        s3 = 1.0 / np.sqrt(IN_C)
        W1 = jax.random.uniform(ks[3], (EDGE_DIM, HIDDEN), jnp.float32, -s1, s1)
        b1 = jax.random.uniform(ks[4], (HIDDEN,), jnp.float32, -s1, s1)
        W2 = jax.random.uniform(ks[5], (HIDDEN, OUT_C * IN_C), jnp.float32, -s2, s2)
        b2 = jax.random.uniform(ks[6], (OUT_C * IN_C,), jnp.float32, -s2, s2)
        root = jax.random.uniform(ks[7], (IN_C, OUT_C), jnp.float32, -s3, s3)
        bias = jnp.zeros((OUT_C,), jnp.float32)
        ln_w = jnp.ones((OUT_C,), jnp.float32)
        ln_b = jnp.zeros((OUT_C,), jnp.float32)
        return {'x': x, 'edge_index': edge_index, 'edge_attr': edge_attr, 'W1': W1, 'b1': b1, 'W2': W2, 'b2': b2, 'root': root, 'bias': bias, 'ln_w': ln_w, 'ln_b': ln_b}
    _L0_gnn_all = _L0_gnn_setup()
    _L0_gnn_in = {k: v for k, v in _L0_gnn_all.items() if k in ('W1', 'b1', 'W2', 'b2', 'root', 'bias', 'ln_w', 'ln_b')}
    del _L0_gnn_all

    def _L1_gnn_setup():
        import jax, jax.numpy as jnp
        import numpy as np
        N_NODES = 30000
        N_EDGES = 300000
        IN_FEATS = 16
        OUT_FEATS = 16
        EDGE_DIM = 16
        key = jax.random.key(seed)
        ks = jax.random.split(key, 8)
        feat = jax.random.normal(ks[0], (N_NODES, IN_FEATS), dtype=jnp.float32)
        efeat = jax.random.normal(ks[1], (N_EDGES, EDGE_DIM), dtype=jnp.float32)
        W_msg = jax.random.normal(ks[2], (EDGE_DIM, IN_FEATS * OUT_FEATS), dtype=jnp.float32) * 0.1
        b_msg = jnp.zeros((IN_FEATS * OUT_FEATS,), dtype=jnp.float32)
        W_attn = jax.random.normal(ks[3], (EDGE_DIM, IN_FEATS * OUT_FEATS), dtype=jnp.float32) * 0.1
        b_attn = jnp.zeros((IN_FEATS * OUT_FEATS,), dtype=jnp.float32)
        src = jax.random.randint(ks[4], (N_EDGES,), 0, N_NODES, dtype=jnp.int32)
        dst = jax.random.randint(ks[5], (N_EDGES,), 0, N_NODES, dtype=jnp.int32)
        return {'feat': feat, 'efeat': efeat, 'W_msg': W_msg, 'b_msg': b_msg, 'W_attn': W_attn, 'b_attn': b_attn, 'src': src, 'dst': dst}
    _L1_gnn_all = _L1_gnn_setup()
    _L1_gnn_in = {k: v for k, v in _L1_gnn_all.items() if k in ('W_msg', 'b_msg', 'W_attn', 'b_attn')}
    del _L1_gnn_all
    return {'x': x, 'src': src, 'dst': dst, 'edge_attr_16': edge_attr_16, 'edge_attr_8': edge_attr_8, 'L0_gnn_W1': _L0_gnn_in['W1'], 'L0_gnn_b1': _L0_gnn_in['b1'], 'L0_gnn_W2': _L0_gnn_in['W2'], 'L0_gnn_b2': _L0_gnn_in['b2'], 'L0_gnn_root': _L0_gnn_in['root'], 'L0_gnn_bias': _L0_gnn_in['bias'], 'L0_gnn_ln_w': _L0_gnn_in['ln_w'], 'L0_gnn_ln_b': _L0_gnn_in['ln_b'], 'L1_gnn_W_msg': _L1_gnn_in['W_msg'], 'L1_gnn_b_msg': _L1_gnn_in['b_msg'], 'L1_gnn_W_attn': _L1_gnn_in['W_attn'], 'L1_gnn_b_attn': _L1_gnn_in['b_attn']}

def reference(x, src, dst, edge_attr_16, edge_attr_8, L0_gnn_W1, L0_gnn_b1, L0_gnn_W2, L0_gnn_b2, L0_gnn_root, L0_gnn_bias, L0_gnn_ln_w, L0_gnn_ln_b, L1_gnn_W_msg, L1_gnn_b_msg, L1_gnn_W_attn, L1_gnn_b_attn):
    import jax
    import jax.numpy as jnp

    def _L0_gnn_ref(x, edge_index, edge_attr, W1, b1, W2, b2, root, bias, ln_w, ln_b):
        import jax, jax.numpy as jnp
        import numpy as np
        N_NODES = 100000
        N_EDGES = 12500
        IN_C = 16
        OUT_C = 16
        EDGE_DIM = 8
        HIDDEN = 64

        def _layernorm(h, w, b, eps=1e-05):
            mu = jnp.mean(h, axis=-1, keepdims=True)
            var = jnp.mean(jnp.square(h - mu), axis=-1, keepdims=True)
            return (h - mu) * jax.lax.rsqrt(var + eps) * w + b
        src = edge_index[0]
        dst = edge_index[1]
        h = jax.nn.silu(edge_attr @ W1 + b1)
        We = (h @ W2 + b2).reshape(-1, IN_C, OUT_C)
        msg = jnp.einsum('ei,eio->eo', x[src], We)
        summed = jax.ops.segment_sum(msg, dst, num_segments=N_NODES)
        cnt = jax.ops.segment_sum(jnp.ones_like(dst, dtype=x.dtype), dst, num_segments=N_NODES)
        aggr = summed / jnp.maximum(cnt, 1.0)[:, None]
        out = aggr + x @ root + bias
        out = _layernorm(out, ln_w, ln_b)
        return jax.nn.silu(out + x)

    def _L1_gnn_ref(feat, efeat, W_msg, b_msg, W_attn, b_attn, src, dst):
        import jax, jax.numpy as jnp
        import numpy as np
        N_NODES = 30000
        N_EDGES = 300000
        IN_FEATS = 16
        OUT_FEATS = 16
        EDGE_DIM = 16
        N, in_f = feat.shape
        E = efeat.shape[0]
        w_m = (efeat @ W_msg + b_msg).reshape(E, in_f, -1)
        w_a = (efeat @ W_attn + b_attn).reshape(E, in_f, -1)
        h_src = feat[src][:, :, None]
        e1 = w_m * h_src
        e2 = w_a * h_src
        seg_max = jax.ops.segment_max(e2, dst, num_segments=N)
        ex = jnp.exp(e2 - seg_max[dst])
        denom = jax.ops.segment_sum(ex, dst, num_segments=N)
        attn = ex / denom[dst]
        ft = jax.ops.segment_sum(e1 * attn, dst, num_segments=N)
        return ft.sum(axis=1)
    edge_index = jnp.stack([src, dst])
    h = jnp.maximum(_layernorm(x, axis=-1), 0.0)
    x = x + _L0_gnn_ref(h, edge_index, edge_attr_8, L0_gnn_W1, L0_gnn_b1, L0_gnn_W2, L0_gnn_b2, L0_gnn_root, L0_gnn_bias, L0_gnn_ln_w, L0_gnn_ln_b)
    h = jnp.maximum(_layernorm(x, axis=-1), 0.0)
    x = x + _L1_gnn_ref(h, edge_attr_16, L1_gnn_W_msg, L1_gnn_b_msg, L1_gnn_W_attn, L1_gnn_b_attn, src, dst)
    return x

_drawn_inputs = setup_inputs


def setup_inputs(seed=0):
    import zlib

    import numpy as np

    out = dict(_drawn_inputs(seed))
    spreads = {'L0_gnn_bias': (0.0, 0.1),
     'L0_gnn_ln_w': (1.0, 0.2),
     'L0_gnn_ln_b': (0.0, 0.1),
     'L1_gnn_b_msg': (0.0, 0.1),
     'L1_gnn_b_attn': (0.0, 0.686)}
    factors = {}
    for name, (base, spread) in spreads.items():
        noise = np.random.default_rng([zlib.crc32(name.encode()), seed]).standard_normal(out[name].shape)
        drawn = base * np.exp(spread * noise) if base else spread * noise
        out[name] = jnp.asarray(drawn.astype(out[name].dtype))
    for name, factor in factors.items():
        out[name] = (out[name] * factor).astype(out[name].dtype)
    return out
```

```python
from contextlib import ExitStack

import concourse.bass as bass
from concourse import mybir

F32 = mybir.dt.float32
I32 = mybir.dt.int32
BF16 = mybir.dt.bfloat16
ALU = mybir.AluOpType
ACT = mybir.ActivationFunctionType
X = mybir.AxisListType.X

N = 100000
E = 50000
C = 16
P = 125
T = E // P
CT = 8
CE = CT * P
NCH = T // CT
NP = N // P
NS = NP // NCH
W = C * C
HID = 64
K8 = 8
ENDS = 2 * T
EP = 100
EG = ENDS // EP
SPLITC = E // 8 // (NCH // 2)
NB = 10
NN = NP // NB
EPS = 1e-5
SKIP = float(1 << 20)
BIG = 3.0e38
LINKS1 = 52
STEPS = NCH * 4


class Chain:

    def __init__(self, sem):
        self.sem, self.count, self.loop = sem, 0, None

    def next(self):
        self.count += 1
        if self.loop is None:
            return self.count
        i, first, per = self.loop
        return i * per + (self.count - first * per)

    def enter(self, i, first, per):
        self.loop = (i, first, per)
        self.start = self.count

    def leave(self, times):
        per = self.loop[2]
        assert self.count - self.start == per, (self.count, self.start, per)
        self.count = self.start + times * per
        self.loop = None


def gnn_kernel(nc, x, src_cols, dst, dst_cols, ends, end_cols, ea16T, ea8T, W1, b1, W2, b2, root, bias, ln_w, ln_b,
               Wm, bm, Wa, ba, ident, fold, out, part=2):
    agg_tab = nc.dram_tensor("agg_tab", [N, C + 1], F32, kind="Internal").ap()
    ft_tab = nc.dram_tensor("ft_tab", [N, C], F32, kind="Internal").ap()
    x1_tab = nc.dram_tensor("x1_tab", [N, C], F32, kind="Internal").ap()
    stack_tab = nc.dram_tensor("stack_tab", [6 * C, E], BF16, kind="Internal").ap()
    flag_tab = nc.dram_tensor("flag_tab", [E], F32, kind="Internal").ap()

    with ExitStack() as ctx:
        def sb(name, shape, dt=F32):
            return ctx.enter_context(nc.sbuf_tensor(name, shape, dt))

        def sem(name):
            return ctx.enter_context(nc.semaphore(name))

        def sem2(name):
            return [sem(f"{name}_even"), sem(f"{name}_odd")]

        hb = sb("hb", [P, NP * C])
        ident_sb = sb("ident_sb", [128, 128])
        fold_sb = sb("fold_sb", [128, C])
        w1_sb = sb("w1_sb", [K8, HID])
        b1_sb = sb("b1_sb", [HID, 1])
        w2_sb = sb("w2_sb", [HID + 1, W])
        root_sb = sb("root_sb", [128, 128])
        bias_row = sb("bias_row", [1, 128])
        ones_row = sb("ones_row", [1, P])
        lnw_sb = sb("lnw_sb", [P, C])
        lnb_sb = sb("lnb_sb", [P, C])
        wf_sb = sb("wf_sb", [C + 1, 2 * W])
        wres = sb("wres", [C + 1, 2 * W])
        wpart = sb("wpart", [C + 1, 3, 2 * W], BF16)
        wstack = sb("wstack", [6 * C + 3, 2 * W], BF16)
        col_f = sb("col_f", [P, NCH, 2, CT])
        col_i = sb("col_i", [P, NCH, CT], I32)
        same_e = sb("same_e", [128, ENDS])
        live_e = sb("live_e", [128, ENDS])
        idx_e = sb("idx_e", [EP, EG], I32)
        bound0 = sb("bound0", [C + 1, ENDS])
        bound1 = sb("bound1", [128, 3, 2, ENDS])

        ARENA = 26000
        arena = sb("arena", [128, ARENA])
        place = [0]

        def carve(rows, cols, dt=F32):
            words = cols if dt != BF16 else cols // 2
            a = arena[0:rows, place[0]:place[0] + words]
            place[0] += words
            assert place[0] <= ARENA, place[0]
            return a if dt == F32 else a.bitcast(dt)

        rr = carve(P, NP * C)
        base = place[0]
        xin = [carve(P, (CT + NS) * C).rearrange("p (t c) -> p t c", c=C) for _ in range(2)]
        hx = carve(P, (CT + NS) * C).rearrange("p (t c) -> p t c", c=C)
        sq = carve(P, (CT + NS) * C).rearrange("p (t c) -> p t c", c=C)
        st = carve(P, 4 * (CT + NS)).rearrange("p (k t) -> p k t", k=4)
        src0 = [carve(P, CT, I32) for _ in range(2)]
        ea8 = [carve(K8, CE) for _ in range(2)]
        dstb = [carve(P, CE, I32) for _ in range(2)]
        hid = [carve(HID + 1, CE) for _ in range(2)]
        S0 = [carve(P, CT * P).rearrange("p (t e) -> p t e", t=CT) for _ in range(2)]
        prod = [carve(P, 2 * W) for _ in range(2)]
        msg = [carve(P, CT * (C + 1)).rearrange("p (t c) -> p t c", t=CT) for _ in range(2)]
        segs = [carve(P, CT * (C + 1)).rearrange("p (t c) -> p t c", t=CT) for _ in range(2)]
        sc0 = [carve(P, CT, I32) for _ in range(2)]
        dc0 = carve(P, CT)
        hT = carve(128, 2 * P).rearrange("p (g e) -> p g e", g=2)
        spx = carve(128, SPLITC)
        spr = carve(128, SPLITC)
        spb = carve(128, 3 * SPLITC, BF16).rearrange("p (k n) -> p k n", k=3)
        end_seg = carve(EP, EG * (C + 1)).rearrange("p (g c) -> p g c", g=EG)
        top0 = place[0]
        place[0] = 0
        d_i = carve(P, T, I32)
        d_next = carve(P, T, I32)
        d_first = carve(P, T, I32)
        d_last = carve(P, T, I32)
        c1, c2, c3, c4 = (carve(P, T) for _ in range(4))
        dn = carve(100, 500, I32)
        dq = carve(100, 500)
        e_b = carve(128, ENDS, I32)
        e_c = carve(EP, EG, I32)
        e_n = carve(EP, EG, I32)
        e_1 = carve(EP, EG)
        e_2 = carve(EP, EG)
        zero = carve(P, 17 * 400)
        assert place[0] <= base
        place[0] = base
        ag = [carve(P, NN * (C + 1)).rearrange("p (n c) -> p n c", n=NN) for _ in range(2)]
        xn = [carve(P, NN * C).rearrange("p (n c) -> p n c", n=NN) for _ in range(2)]
        nt = carve(P, NN * C).rearrange("p (n c) -> p n c", n=NN)
        nq = carve(P, NN * C).rearrange("p (n c) -> p n c", n=NN)
        nz = [carve(P, NN * C).rearrange("p (n c) -> p n c", n=NN) for _ in range(2)]
        ns = [carve(P, NN * C).rearrange("p (n c) -> p n c", n=NN) for _ in range(1)]
        nst = carve(P, 6 * NN).rearrange("p (k n) -> p k n", k=6)

        place[0] = 0
        src1 = [carve(P, CT, I32) for _ in range(2)]
        rows1 = [carve(P, CT * C).rearrange("p (t c) -> p t c", c=C) for _ in range(2)]
        h1 = [carve(P, CT * C).rearrange("p (t c) -> p t c", c=C) for _ in range(2)]
        sq1 = carve(P, CT * C).rearrange("p (t c) -> p t c", c=C)
        st1 = carve(P, 4 * CT).rearrange("p (k t) -> p k t", k=4)
        stk = [carve(6 * C + 3, CE, BF16) for _ in range(2)]
        flg = [carve(128, CE) for _ in range(2)]
        dsb = [carve(P, CE, I32) for _ in range(2)]
        dc1 = [carve(P, 2 * CT).rearrange("p (k t) -> p k t", k=2) for _ in range(2)]
        sc1 = [carve(P, CT, I32) for _ in range(2)]
        base1 = place[0]
        Sm = [carve(P, CT * P).rearrange("p (t e) -> p t e", t=CT) for _ in range(2)]
        Lm = [carve(P, CT * P).rearrange("p (t e) -> p t e", t=CT) for _ in range(2)]
        En = [carve(P, 4 * W).rearrange("p (t m w) -> p t m w", t=2, m=2) for _ in range(4)]
        Mx = [carve(128, 4 * P).rearrange("p (h e) -> p h e", h=2) for _ in range(2)]
        MT = [carve(P, 2 * W).rearrange("p (t w) -> p t w", t=2) for _ in range(2)]
        dd = [carve(P, 2 * W).rearrange("p (t w) -> p t w", t=2) for _ in range(2)]
        ex = [carve(P, 2 * W).rearrange("p (t w) -> p t w", t=2) for _ in range(2)]
        lnd = carve(P, 2 * W).rearrange("p (t w) -> p t w", t=2)
        Rd = [carve(P, 2 * W).rearrange("p (t w) -> p t w", t=2) for _ in range(2)]
        at = carve(P, 2 * W).rearrange("p (t w) -> p t w", t=2)
        wv = [carve(P, 2 * W).rearrange("p (t w) -> p t w", t=2) for _ in range(2)]
        vr = [carve(P, 2 * C).rearrange("p (t c) -> p t c", t=2) for _ in range(2)]
        fts = [carve(P, CT * C).rearrange("p (t c) -> p t c", t=CT) for _ in range(2)]
        top1, place[0] = place[0] - 2 * CT * C, base1
        bm_m, bm_x, bm_c, bm_w, bm_a, bm_r = (carve(128, 2 * ENDS).rearrange("p (h e) -> p h e", h=2) for _ in range(6))
        bm_nf, bm_sf = (carve(128, ENDS) for _ in range(2))
        end_ft = carve(EP, EG * C).rearrange("p (g c) -> p g c", g=EG)
        fin = [carve(P, NN * C) for _ in range(3)]
        assert place[0] <= top1

        bank = [ctx.enter_context(nc.psum_tensor(f"bank{i}", [128, 512], F32)) for i in range(8)]

        s_const = sem("s_const")
        s_dload = sem("s_dload")
        s_zero = sem("s_zero")
        s_zeroed = sem("s_zeroed")
        s_flag = sem("s_flag")
        s_flagst = sem("s_flagst")
        s_root0 = sem("s_root0")
        s_ones = sem("s_ones")
        s_pad = sem("s_pad")
        s_wsplit = sem("s_wsplit")
        s_wstack = sem("s_wstack")
        s_dve = sem("s_dve")
        s_act = sem("s_act")
        s_cols = sem("s_cols")
        l0_in = sem2("l0_in")
        l0_got = sem2("l0_got")
        l0_z = sem("l0_z")
        l0_h = sem("l0_h")
        l0_w = sem("l0_w")
        l0_prod = sem("l0_prod")
        l0_hx = sem("l0_hx")
        l0_ht = sem("l0_ht")
        l0_htc = sem("l0_htc")
        l0_root = sem("l0_root")
        l0_rootc = sem("l0_rootc")
        l0_msg = sem("l0_msg")
        l0_seg = sem("l0_seg")
        l0_segc = sem("l0_segc")
        l0_put = sem2("l0_put")
        l0_gate = sem("l0_gate")
        sp_in = sem("sp_in")
        sp_done = sem("sp_done")
        sp_out = sem("sp_out")
        l0_run = sem("l0_run")
        l0_runT = sem("l0_runT")
        l0_runc = sem("l0_runc")
        l0_end = sem("l0_end")
        n_in = sem2("n_in")
        n_sq = sem("n_sq")
        n_sqd = sem("n_sqd")
        n_z = sem("n_z")
        n_silu = sem("n_silu")
        n_x1 = sem("n_x1")
        n_out = sem("n_out")

        l1_in = sem2("l1_in")
        l1_got = sem2("l1_got")
        l1_gate = sem("l1_gate")
        l1_ones = sem("l1_ones")
        l1_pre = sem("l1_pre")
        l1_A = sem("l1_A")
        l1_e = sem("l1_e")
        l1_T = sem("l1_T")
        l1_M = sem("l1_M")
        l1_MT = sem("l1_MT")
        l1_MTc = sem("l1_MTc")
        l1_B = sem("l1_B")
        l1_d = sem("l1_d")
        l1_ex = sem("l1_ex")
        l1_D = sem("l1_D")
        l1_ln = sem("l1_ln")
        l1_R = sem("l1_R")
        l1_w = sem("l1_w")
        l1_F = sem("l1_F")
        l1_Fc = sem("l1_Fc")
        l1_put = sem2("l1_put")
        b_d = sem("b_d")
        b_x = sem("b_x")
        b_q = sem("b_q")
        b_f = sem("b_f")
        b_fc = sem("b_fc")
        b_put = sem("b_put")
        f_in = [sem(f"f_in{k}") for k in range(3)]
        f_sum = sem("f_sum")
        f_out = [sem(f"f_out{k}") for k in range(3)]

        def wait_pos(eng, s, value):
            if not (isinstance(value, int) and value <= 0):
                eng.wait_ge(s, value)

        def valid(i, k):
            return not isinstance(i, int) or 0 <= 8 * i + k < STEPS

        def run_slots(eng, slot):
            for k in range(8):
                slot(0, k)
            with eng.Fori(1, STEPS // 8) as i:
                for k in range(8):
                    slot(i, k)
            for k in range(4):
                slot(STEPS // 8, k)

        block = ctx.enter_context(nc.Block())

        def bcast_rows(ap, rows, cols):
            return ap.rearrange("(a n) -> a n", a=1).broadcast_to([rows, cols])

        x_part = x.rearrange("(p n) c -> p (n c)", p=P)

        @block.sync
        def _(sp):
            for dst_ap, src_ap in (
                (d_i, dst_cols), (d_first, bcast_rows(dst_cols[0, :], P, T)),
                (d_last, bcast_rows(dst_cols[P - 1, :], P, T)), (dn, dst.rearrange("(p n) -> p n", p=100)),
                (e_b, bcast_rows(ends[0:ENDS], 128, ENDS)), (e_c, end_cols[0:EP, :]),
                (e_n, end_cols[EP:2 * EP, :]),
            ):
                sp.dma_start(dst_ap, src_ap).then_inc(s_dload, 16)
            sp.wait_ge(s_pad, 1)
            sp.dma_start(d_next[0:P - 1, :], dst_cols[1:P, :]).then_inc(s_dload, 16)
            for dst_ap, src_ap in (
                (ident_sb[:, :], ident), (fold_sb[:, :], fold), (w1_sb[:, :], W1),
                (b1_sb[:, :], b1.rearrange("(h a) -> h a", a=1)), (w2_sb[0:HID, :], W2),
                (w2_sb[HID:HID + 1, :], b2.rearrange("(a n) -> a n", a=1)),
                (lnw_sb[:, :], bcast_rows(ln_w, P, C)), (lnb_sb[:, :], bcast_rows(ln_b, P, C)),
                (wf_sb[0:C, 0:W], Wm), (wf_sb[0:C, W:2 * W], Wa),
                (wf_sb[C:C + 1, 0:W], bm.rearrange("(a n) -> a n", a=1)),
                (wf_sb[C:C + 1, W:2 * W], ba.rearrange("(a n) -> a n", a=1)),
            ):
                sp.dma_start(dst_ap, src_ap).then_inc(s_const, 16)
            sp.wait_ge(s_root0, 1)
            for n in range(8):
                sp.dma_start(root_sb[n * C:(n + 1) * C, n * C:(n + 1) * C], root).then_inc(s_const, 16)
                sp.dma_start(bias_row[0:1, n * C:(n + 1) * C], bias.rearrange("(a n) -> a n", a=1)).then_inc(s_const, 16)

            def load(i, b):
                c = 2 * i + b
                if not (isinstance(i, int) and i == 0):
                    sp.wait_ge(l0_msg, c - 1)
                    sp.wait_ge(l0_seg, c - 1)
                sp.dma_start(src0[b], src_cols[:, bass.ds(c * CT, CT)]).then_inc(l0_in[b], 16)
                sp.dma_start(ea8[b], ea8T[:, bass.ds(c * CE, CE)]).then_inc(l0_in[b], 16)
                sp.dma_start(dstb[b], bcast_rows(dst[bass.ds(c * CE, CE)], P, CE)).then_inc(l0_in[b], 16)
                sp.dma_start(xin[b][:, CT:, :].rearrange("p t c -> p (t c)"),
                             x_part[:, bass.ds(c * NS * C, NS * C)]).then_inc(l0_in[b], 16)
                if b == 1:
                    if not (isinstance(i, int) and i == 0):
                        sp.wait_ge(sp_done, i)
                    sp.dma_start(spx, ea16T.rearrange("c (b n) -> (c b) n", b=8)[:, bass.ds(i * SPLITC, SPLITC)]
                                 ).then_inc(sp_in, 16)

            load(0, 0)
            load(0, 1)
            with sp.Fori(1, NCH // 2) as i:
                load(i, 0)
                load(i, 1)

            sp.wait_ge(l0_put[0], 128 * (NCH // 2))
            sp.wait_ge(l0_put[1], 128 * (NCH // 2))
            sp.wait_ge(l0_end, 16 * EG)
            sp.wait_ge(l0_rootc, NCH)
            sp.wait_ge(sp_out, 96 * (NCH // 2))
            for k in range(NB):
                if k >= 2:
                    sp.wait_ge(n_x1, k - 1)
                sp.dma_start(ag[k % 2].rearrange("p n c -> p (n c)"),
                             agg_tab.rearrange("(p n) c -> p (n c)", p=P)[:, k * NN * (C + 1):(k + 1) * NN * (C + 1)]
                             ).then_inc(n_in[k % 2], 16)
                sp.dma_start(xn[k % 2].rearrange("p n c -> p (n c)"), x_part[:, k * NN * C:(k + 1) * NN * C]
                             ).then_inc(n_in[k % 2], 16)

            if part == 1:
                return

            sp.wait_ge(n_x1, NB)
            sp.wait_ge(n_out, 16 * NB)

            def load1(i, b):
                c = 2 * i + b
                if not (isinstance(i, int) and i == 0):
                    sp.wait_ge(l1_F, 4 * (c - 1))
                sp.dma_start(src1[b], src_cols[:, bass.ds(c * CT, CT)]).then_inc(l1_in[b], 16)
                sp.dma_start(stk[b][0:6 * C, :], stack_tab[:, bass.ds(c * CE, CE)]).then_inc(l1_in[b], 16)
                sp.dma_start(flg[b], bcast_rows(flag_tab[bass.ds(c * CE, CE)], 128, CE)).then_inc(l1_in[b], 16)
                sp.dma_start(dsb[b], bcast_rows(dst[bass.ds(c * CE, CE)], P, CE)).then_inc(l1_in[b], 16)

            load1(0, 0)
            load1(0, 1)
            with sp.Fori(1, NCH // 2) as i:
                load1(i, 0)
                load1(i, 1)
            sp.wait_ge(l1_put[0], 128 * (NCH // 2))
            sp.wait_ge(l1_put[1], 128 * (NCH // 2))
            sp.wait_ge(b_put, 16 * EG)
            for k in range(NB + 2):
                if k < NB:
                    if k >= 3:
                        sp.wait_ge(f_out[k % 3], 16 * (k // 3))
                    sp.dma_start(fin[k % 3], ft_tab.rearrange("(p n) c -> p (n c)", p=P)[:, k * NN * C:(k + 1) * NN * C]
                                 ).then_inc(f_in[k % 3], 16)
                if k >= 2:
                    j = k - 2
                    sp.wait_ge(f_sum, j + 1)
                    sp.dma_start(out.rearrange("(p n) c -> p (n c)", p=P)[:, j * NN * C:(j + 1) * NN * C], fin[j % 3]
                                 ).then_inc(f_out[j % 3], 16)
            for k in range(3):
                sp.wait_ge(f_out[k], 16 * len(range(k, NB, 3)))

        @block.gpsimd
        def _(pool):
            pool.memset(root_sb[:, :], 0.0).then_inc(s_root0, 1)
            pool.memset(zero, 0.0).then_inc(s_zero, 1)

            def gather(i, b):
                pool.wait_ge(l0_in[b], 64 * (i + 1))
                pool.sem_inc(l0_gate, 1)
                for t in range(CT):
                    pool.indirect_dma_start(out=xin[b][:, t, :], out_offset=None, in_=x,
                                            in_offset=bass.IndirectOffsetOnAxis(ap=src0[b][:, t:t + 1], axis=0)
                                            ).then_inc(l0_got[b], 16)

            def scatter(i, b):
                pool.wait_ge(l0_segc, 2 * i + b + 1)
                pool.sem_inc(l0_gate, 1)
                for t in range(CT):
                    pool.indirect_dma_start(out=agg_tab, out_offset=bass.IndirectOffsetOnAxis(ap=sc0[b][:, t:t + 1], axis=0),
                                            in_=segs[b][:, t, :], in_offset=None,
                                            bounds_check=N - 1, oob_is_err=False).then_inc(l0_put[b], 16)

            gather(0, 0)
            gather(0, 1)
            pool.wait_ge(s_zeroed, 64)
            with pool.Fori(1, NCH // 2) as i:
                scatter(i - 1, 0)
                gather(i, 0)
                scatter(i - 1, 1)
                gather(i, 1)
            scatter(NCH // 2 - 1, 0)
            scatter(NCH // 2 - 1, 1)
            pool.wait_ge(l0_runc, 1)
            for g in range(EG):
                pool.indirect_dma_start(out=agg_tab, out_offset=bass.IndirectOffsetOnAxis(ap=idx_e[:, g:g + 1], axis=0),
                                        in_=end_seg[:, g, :], in_offset=None,
                                        bounds_check=N - 1, oob_is_err=False).then_inc(l0_end, 16)

            for k in range(NB):
                pool.wait_ge(n_silu, k + 1)
                pool.wait_ge(n_in[k % 2], 32 * (k // 2 + 1))
                pool.tensor_tensor(hb[:, k * NN * C:(k + 1) * NN * C], ns[0].rearrange("p n c -> p (n c)"),
                                   xn[k % 2].rearrange("p n c -> p (n c)"), ALU.add).then_inc(n_x1, 1)

            if part == 1:
                return

            pool.wait_ge(n_out, 16 * NB)

            def gather1(i, b):
                c = 2 * i + b
                pool.wait_ge(l1_in[b], 64 * (i + 1))
                if not (isinstance(i, int) and i == 0):
                    pool.wait_ge(l1_pre, c - 1)
                pool.sem_inc(l1_gate, 1)
                for t in range(CT):
                    pool.indirect_dma_start(out=rows1[b][:, t, :], out_offset=None, in_=x1_tab,
                                            in_offset=bass.IndirectOffsetOnAxis(ap=src1[b][:, t:t + 1], axis=0)
                                            ).then_inc(l1_got[b], 16)

            def scatter1(i, b):
                pool.wait_ge(l1_Fc, 2 * i + b + 1)
                pool.sem_inc(l1_gate, 1)
                for t in range(CT):
                    pool.indirect_dma_start(out=ft_tab, out_offset=bass.IndirectOffsetOnAxis(ap=sc1[b][:, t:t + 1], axis=0),
                                            in_=fts[b][:, t, :], in_offset=None,
                                            bounds_check=N - 1, oob_is_err=False).then_inc(l1_put[b], 16)

            gather1(0, 0)
            gather1(0, 1)
            with pool.Fori(1, NCH // 2) as i:
                scatter1(i - 1, 0)
                gather1(i, 0)
                scatter1(i - 1, 1)
                gather1(i, 1)
            scatter1(NCH // 2 - 1, 0)
            scatter1(NCH // 2 - 1, 1)
            pool.wait_ge(b_fc, 1)
            for g in range(EG):
                pool.indirect_dma_start(out=ft_tab, out_offset=bass.IndirectOffsetOnAxis(ap=idx_e[:, g:g + 1], axis=0),
                                        in_=end_ft[:, g, :], in_offset=None,
                                        bounds_check=N - 1, oob_is_err=False).then_inc(b_put, 16)

        @block.tensor
        def _(pe):
            pe.wait_ge(s_const, 16 * 28)
            pe.wait_ge(s_ones, 1)

            def weights(i, b, s):
                c = 2 * i + b
                if not (isinstance(i, int) and i == 0 and b == 0 and s < 2):
                    pe.wait_ge(l0_prod, 4 * c + s - 1)
                for k in range(2):
                    t = 2 * s + k
                    ins = pe.matmul(bank[s % 2][0:P, k * W:(k + 1) * W], hid[b][:, t * P:(t + 1) * P], w2_sb[:, :],
                                    start=True, stop=True)
                ins.then_inc(l0_w, 1)

            def chunk(i, b):
                c = 2 * i + b
                pe.wait_ge(l0_in[b], 64 * (i + 1))
                if not (isinstance(i, int) and i == 0 and b == 0):
                    pe.wait_ge(l0_h, c)
                for k in range(2):
                    ins = pe.matmul(bank[2 + k][0:HID, 0:CE // 2], w1_sb[:, :], ea8[b][:, k * CE // 2:(k + 1) * CE // 2],
                                    start=True, stop=True)
                ins.then_inc(l0_z, 1)
                pe.wait_ge(l0_h, c + 1)
                weights(i, b, 0)
                weights(i, b, 1)
                pe.wait_ge(l0_hx, c + 1)
                if not (isinstance(i, int) and i == 0 and b == 0):
                    pe.wait_ge(l0_htc, c)
                for g in range(2):
                    ins = pe.transpose(bank[4][:, g * 128:g * 128 + P],
                                       hx[:, CT + 8 * g:CT + 8 * g + 8, :].rearrange("p t c -> p (t c)"),
                                       ident_sb[0:P, 0:P])
                ins.then_inc(l0_ht, 1)
                weights(i, b, 2)
                weights(i, b, 3)
                pe.wait_ge(l0_htc, c + 1)
                if not (isinstance(i, int) and i == 0 and b == 0):
                    pe.wait_ge(l0_rootc, c)
                for g in range(2):
                    pe.matmul(bank[5][0:P, g * 128:(g + 1) * 128], hT[:, g, :], root_sb[:, :], start=True, stop=False)
                    ins = pe.matmul(bank[5][0:P, g * 128:(g + 1) * 128], ones_row[:, :], bias_row[:, :],
                                    start=False, stop=True)
                ins.then_inc(l0_root, 1)
                pe.wait_ge(l0_msg, c + 1)
                if not (isinstance(i, int) and i == 0 and b == 0):
                    pe.wait_ge(l0_segc, c)
                for t in range(CT):
                    pe.matmul(bank[6][0:P, t * (C + 1):(t + 1) * (C + 1)], S0[b][:, t, :], msg[b][:, t, :],
                              start=True, stop=True)
                    ins = pe.matmul(bank[7][0:C + 1, 2 * t:2 * t + 2], msg[b][:, t, :], S0[b][:, t, 0:P:P - 1],
                                    start=True, stop=True)
                ins.then_inc(l0_seg, 1)

            chunk(0, 0)
            chunk(0, 1)
            with pe.Fori(1, NCH // 2) as i:
                chunk(i, 0)
                chunk(i, 1)
            pe.wait_ge(l0_run, 1)
            for g in range(EG):
                ins = pe.transpose(bank[6][0:EP, g * (C + 1):(g + 1) * (C + 1)], bound0[:, g * EP:(g + 1) * EP],
                                   ident_sb[0:C + 1, 0:C + 1])
            ins.then_inc(l0_runT, 1)

            if part == 1:
                return

            pe.wait_ge(s_wstack, 16 * 9)
            pe.wait_ge(l1_ones, 1)
            pe.wait_ge(l0_runc, 1)

            def edge_weights(i, k):
                b, s = (k % 8) // 4, k % 4
                n = 8 * i + k
                if s == 0:
                    if isinstance(i, int):
                        pe.wait_ge(l1_in[b], 64 * (n // 8 + 1))
                    else:
                        pe.wait_ge(l1_in[b], 64 * (i + k // 8 + 1))
                for t in range(2):
                    wait_pos(pe, l1_e, 2 * n + t - 1)
                    pe.matmul(bank[t][0:P, :], stk[b][:, (2 * s + t) * P:(2 * s + t + 1) * P], wstack[:, :],
                              start=True, stop=True).then_inc(l1_A, 1)

            def slot(i, k):
                if valid(i, k):
                    edge_weights(i, k)
                k -= 1
                if valid(i, k):
                    n = 8 * i + k
                    pe.wait_ge(l1_e, 2 * n + 2)
                    wait_pos(pe, l1_M, n)
                    for t in range(2):
                        for h in range(2):
                            ins = pe.transpose(bank[2][:, (2 * h + t) * P:(2 * h + t + 1) * P],
                                               En[k % 4][:, t, 1, h * 128:(h + 1) * 128], ident_sb[0:P, 0:P])
                    ins.then_inc(l1_T, 1)
                if valid(i, k - 1):
                    n, q, b, s = 8 * i + k - 1, (k - 1) % 2, ((k - 1) % 8) // 4, (k - 1) % 4
                    pe.wait_ge(l1_M, n + 1)
                    wait_pos(pe, l1_MTc, n)
                    for t in range(2):
                        for h in range(2):
                            ins = pe.transpose(bank[3][0:P, (2 * t + h) * 128:(2 * t + h + 1) * 128],
                                               Mx[q][:, h, t * P:(t + 1) * P], ident_sb[:, :])
                    ins.then_inc(l1_MT, 1)
                    pe.wait_ge(l1_MTc, n + 1)
                    wait_pos(pe, l1_d, n)
                    if s == 0:
                        wait_pos(pe, l1_Fc, (n // 4 if isinstance(n, int) else 2 * i + (k - 1) // 4) - 1)
                    for t in range(2):
                        tt = 2 * s + t
                        pe.matmul(bank[4][0:P, t * W:(t + 1) * W], Lm[b][:, tt, :], MT[q][:, t, :], start=True, stop=True)
                        for h in range(2):
                            ins = pe.matmul(bank[7][:, b * 96 + h * 16 + 2 * tt:b * 96 + h * 16 + 2 * tt + 2],
                                            MT[q][:, t, h * 128:(h + 1) * 128], Lm[b][:, tt, 0:P:P - 1],
                                            start=True, stop=True)
                    ins.then_inc(l1_B, 1)
                if valid(i, k - 2):
                    n, q, b, s = 8 * i + k - 2, k % 2, ((k - 2) % 8) // 4, (k - 2) % 4
                    pe.wait_ge(l1_ex, n + 1)
                    wait_pos(pe, l1_ln, n)
                    for t in range(2):
                        tt = 2 * s + t
                        pe.matmul(bank[5][0:P, t * W:(t + 1) * W], Sm[b][:, tt, :], ex[q][:, t, :], start=True, stop=True)
                        for h in range(2):
                            ins = pe.matmul(bank[7][:, b * 96 + 32 + h * 16 + 2 * tt:b * 96 + 32 + h * 16 + 2 * tt + 2],
                                            ex[q][:, t, h * 128:(h + 1) * 128], Sm[b][:, tt, 0:P:P - 1],
                                            start=True, stop=True)
                    ins.then_inc(l1_D, 1)
                if valid(i, k - 3):
                    n, q, b, s = 8 * i + k - 3, (k - 3) % 2, ((k - 3) % 8) // 4, (k - 3) % 4
                    pe.wait_ge(l1_w, n + 1)
                    for t in range(2):
                        tt = 2 * s + t
                        pe.matmul(bank[6][0:P, b * 128 + tt * C:b * 128 + (tt + 1) * C], Sm[b][:, tt, :], vr[q][:, t, :],
                                  start=True, stop=True)
                        for h in range(2):
                            ins = pe.matmul(bank[7][:, b * 96 + 64 + h * 16 + 2 * tt:b * 96 + 64 + h * 16 + 2 * tt + 2],
                                            wv[q][:, t, h * 128:(h + 1) * 128], Sm[b][:, tt, 0:P:P - 1],
                                            start=True, stop=True)
                    ins.then_inc(l1_F, 1)

            run_slots(pe, slot)
            pe.wait_ge(b_q, 1)
            for g in range(EG):
                for h in range(2):
                    ins = pe.matmul(bank[0][0:EP, g * C:(g + 1) * C], bm_a[:, h, g * EP:(g + 1) * EP], fold_sb[:, :],
                                    start=(h == 0), stop=(h == 1))
            ins.then_inc(b_f, 1)

        @block.scalar
        def _(act):
            act.wait_ge(s_zero, 1)
            for tab, w in ((agg_tab, C + 1), (ft_tab, C)):
                flat = tab.rearrange("(p n) c -> p (n c)", p=P)
                for k in range(2):
                    half = NP * w // 2
                    act.dma_start(flat[:, k * half:(k + 1) * half], zero[:, 0:half]).then_inc(s_zeroed, 16)
            act.wait_ge(s_flag, 1)
            act.dma_start(flag_tab.rearrange("(p n) -> p n", p=100), dq).then_inc(s_flagst, 16)
            act.wait_ge(s_wsplit, 1)
            for j, k in enumerate((0, 1, 0, 1, 2, 0)):
                act.dma_start(wstack[j * C:(j + 1) * C, :], wpart[0:C, k, :]).then_inc(s_wstack, 16)
            for k in range(3):
                act.dma_start(wstack[6 * C + k:6 * C + k + 1, :], wpart[C:C + 1, k, :]).then_inc(s_wstack, 16)
            act.wait_ge(s_const, 16 * 28)
            act.wait_ge(s_cols, 1)
            act.wait_ge(s_zeroed, 64)
            act.wait_ge(s_flagst, 16)

            def chunk(i, b):
                c = 2 * i + b
                act.wait_ge(l0_z, c + 1)
                if not (isinstance(i, int) and i == 0):
                    act.wait_ge(l0_w, 4 * (c - 1))
                z = [bank[2 + k][0:HID, 0:CE // 2] for k in range(2)]
                for k in range(2):
                    ins = nc.scalar.activation(hid[b][0:HID, k * CE // 2:(k + 1) * CE // 2], z[k], ACT.Silu,
                                               bias=b1_sb[:, 0:1])
                ins.then_inc(l0_h, 1)
                act.wait_ge(l0_ht, c + 1)
                if not (isinstance(i, int) and i == 0 and b == 0):
                    act.wait_ge(l0_root, c)
                nc.scalar.activation(hT, bank[4][:, 0:256].rearrange("p (g e) -> p g e", g=2)[:, :, 0:P],
                                     ACT.Copy).then_inc(l0_htc, 1)
                act.wait_ge(l0_root, c + 1)
                nc.scalar.activation(rr[:, bass.ds(c * NS * C, NS * C)], bank[5][0:P, 0:NS * C],
                                     ACT.Copy).then_inc(l0_rootc, 1)
                act.wait_ge(l0_seg, c + 1)
                if not (isinstance(i, int) and i == 0):
                    act.wait_ge(l0_put[b], 128 * i)
                nc.scalar.activation(bound0[:, bass.ds(c * 2 * CT, 2 * CT)], bank[7][0:C + 1, 0:2 * CT], ACT.Copy)
                nc.scalar.activation(segs[b].rearrange("p t c -> p (t c)"), bank[6][0:P, 0:CT * (C + 1)],
                                     ACT.Copy).then_inc(l0_segc, 1)
                if b == 1:
                    act.wait_ge(sp_done, i + 1)
                    for j, k in enumerate((0, 0, 1, 1, 0, 2)):
                        act.dma_start(stack_tab[j * C:(j + 1) * C, :].rearrange("c (b n) -> (c b) n", b=8)
                                      [:, bass.ds(i * SPLITC, SPLITC)], spb[:, k, :]).then_inc(sp_out, 16)

            chunk(0, 0)
            chunk(0, 1)
            with act.Fori(1, NCH // 2) as i:
                chunk(i, 0)
                chunk(i, 1)
            act.wait_ge(l0_runT, 1)
            nc.scalar.activation(end_seg.rearrange("p g c -> p (g c)"), bank[6][0:EP, 0:EG * (C + 1)],
                                 ACT.Copy).then_inc(l0_runc, 1)

            for k in range(NB):
                act.wait_ge(n_sq, k + 1)
                nc.scalar.activation(nq, nt, ACT.Square).then_inc(n_sqd, 1)
                act.wait_ge(n_z, k + 1)
                if k:
                    act.wait_ge(n_x1, k)
                nc.scalar.activation(ns[0], nz[k % 2], ACT.Silu).then_inc(n_silu, 1)
                if k:
                    act.dma_start(x1_tab.rearrange("(p n) c -> p (n c)", p=P)[:, (k - 1) * NN * C:k * NN * C],
                                  hb[:, (k - 1) * NN * C:k * NN * C]).then_inc(n_out, 16)
            act.wait_ge(n_x1, NB)
            act.dma_start(x1_tab.rearrange("(p n) c -> p (n c)", p=P)[:, (NB - 1) * NN * C:],
                          hb[:, (NB - 1) * NN * C:]).then_inc(n_out, 16)
            if part == 1:
                act.dma_start(out.rearrange("(p n) c -> p (n c)", p=P), hb[:, :]).then_inc(n_out, 16)
                act.wait_ge(n_out, 16 * (NB + 1))

            if part == 1:
                return

            def slot(i, k):
                if valid(i, k - 1):
                    n, q = 8 * i + k - 1, (k - 1) % 2
                    act.wait_ge(l1_MT, n + 1)
                    wait_pos(act, l1_B, n - 1)
                    nc.scalar.activation(MT[q], bank[3][0:P, :].rearrange("p (t w) -> p t w", t=2),
                                         ACT.Copy).then_inc(l1_MTc, 1)
                if valid(i, k - 2):
                    n, q = 8 * i + k - 2, k % 2
                    act.wait_ge(l1_d, n + 1)
                    wait_pos(act, l1_w, n - 1)
                    nc.scalar.activation(ex[q], dd[q], ACT.Exp).then_inc(l1_ex, 1)
                    act.wait_ge(l1_D, n + 1)
                    nc.scalar.activation(lnd, bank[5][0:P, :].rearrange("p (t w) -> p t w", t=2),
                                         ACT.Ln).then_inc(l1_ln, 1)
                    act.wait_ge(l1_ln, n + 1)
                    nc.scalar.activation(Rd[q], lnd, ACT.Exp, scale=-1.0).then_inc(l1_R, 1)
                if valid(i, k - 3) and (k - 3) % 4 == 3:
                    b = ((k - 3) % 8) // 4
                    c = 2 * i + (k - 3) // 4
                    act.wait_ge(l1_F, 4 * c + 4)
                    wait_pos(act, l1_put[b], 128 * (i + (k - 3) // 8))
                    nc.scalar.activation(bound1[:, :, :, bass.ds(c * 2 * CT, 2 * CT)],
                                         bank[7][:, b * 96:(b + 1) * 96].rearrange("p (m h e) -> p m h e", m=3, h=2),
                                         ACT.Copy)
                    nc.scalar.activation(fts[b].rearrange("p t c -> p (t c)"), bank[6][0:P, b * 128:(b + 1) * 128],
                                         ACT.Copy).then_inc(l1_Fc, 1)

            run_slots(act, slot)
            act.wait_ge(b_d, 1)
            nc.scalar.activation(bm_c[:, :, :], bm_c[:, :, :], ACT.Exp).then_inc(b_x, 1)
            nc.scalar.activation(bm_w[:, :, :], bm_w[:, :, :], ACT.Exp).then_inc(b_x, 1)
            act.wait_ge(b_f, 1)
            nc.scalar.activation(end_ft.rearrange("p g c -> p (g c)"), bank[0][0:EP, 0:EG * C],
                                 ACT.Copy).then_inc(b_fc, 1)

        @block.vector
        def _(dve):
            ch = Chain(s_dve)
            V = nc.vector

            def link(ins):
                ins.then_inc(s_dve, 1)
                dve.wait_ge(s_dve, ch.next())

            def rstd(y, v, t, total):
                link(V.tensor_scalar(v, total, 1.0 / C, EPS, ALU.mult, ALU.add))
                link(V.tensor_scalar(y.bitcast(I32), v.bitcast(I32), -0.5, 1597463007.0, ALU.mult, ALU.add))
                for _ in range(3):
                    link(V.scalar_tensor_tensor(t, y, -0.5, v, ALU.mult, ALU.mult))
                    link(V.tensor_tensor(t, t, y, ALU.mult))
                    link(V.scalar_tensor_tensor(y, t, 1.5, y, ALU.add, ALU.mult))

            def wide(a, rows):
                return a.rearrange("p (n a) -> p n a", a=1).broadcast_to([P, rows, C])

            V.memset(d_next, -1).then_inc(s_pad, 1)
            for b in range(2):
                V.memset(hid[b][HID:HID + 1, :], 1.0)
                V.memset(msg[b][:, :, C:C + 1], 1.0)
            V.memset(ones_row[:, :], 1.0).then_inc(s_ones, 1)
            dve.wait_ge(s_dload, 16 * 8)
            link(V.tensor_copy(c1, d_i))
            link(V.tensor_copy(col_f[:, :, 0, :], c1.rearrange("p (c t) -> p c t", t=CT)))
            link(V.tensor_tensor(c2, d_i, d_next, ALU.not_equal))
            link(V.tensor_copy(col_f[:, :, 1, :], c2.rearrange("p (c t) -> p c t", t=CT)))
            V.tensor_tensor(c3, d_i, d_first, ALU.not_equal)
            link(V.tensor_tensor(c4, d_i, d_last, ALU.not_equal))
            link(V.tensor_tensor(c3, c3, c4, ALU.mult))
            link(V.tensor_tensor(c3, c3, c2, ALU.mult))
            link(V.scalar_tensor_tensor(c4, c1, -SKIP, c3, ALU.add, ALU.mult))
            link(V.tensor_scalar(col_i.rearrange("p c t -> p (c t)"), c4, SKIP, None, ALU.add))
            V.memset(same_e[:, 0:1], 0.0)
            V.memset(live_e[:, :], 1.0)
            link(V.tensor_tensor(same_e[:, 1:], e_b[:, 1:], e_b[:, :-1], ALU.is_equal))
            pairs = same_e[:, :].rearrange("p (t q) -> p t q", q=2)
            link(V.tensor_scalar(live_e[:, :].rearrange("p (t q) -> p t q", q=2)[:, :, 1:2], pairs[:, :, 1:2],
                                 -1.0, 1.0, ALU.mult, ALU.add))
            link(V.tensor_tensor(e_1, e_c, e_n, ALU.not_equal))
            link(V.tensor_copy(e_2, e_c))
            link(V.scalar_tensor_tensor(e_2, e_2, -SKIP, e_1, ALU.add, ALU.mult))
            link(V.tensor_scalar(idx_e[:, :], e_2, SKIP, None, ALU.add))
            V.memset(dq.rearrange("p (t e) -> p t e", e=P)[:, :, 0:1], 0.0)
            d3 = dn.rearrange("p (t e) -> p t e", e=P)
            link(V.tensor_tensor(dq.rearrange("p (t e) -> p t e", e=P)[:, :, 1:], d3[:, :, 1:], d3[:, :, :-1],
                                 ALU.is_equal))
            link(V.tensor_scalar(dq, dq, 2.0, -1.0, ALU.mult, ALU.add))
            V.tensor_scalar(dq, dq, BIG, None, ALU.mult).then_inc(s_flag, 1)
            dve.wait_ge(s_const, 16 * 28)
            link(V.tensor_copy(wpart[:, 0, :], wf_sb[:, :]))
            link(V.tensor_tensor(wres[:, :], wf_sb[:, :], wpart[:, 0, :], ALU.subtract))
            link(V.tensor_copy(wpart[:, 1, :], wres[:, :]))
            link(V.tensor_tensor(wres[:, :], wres[:, :], wpart[:, 1, :], ALU.subtract))
            V.tensor_copy(wpart[:, 2, :], wres[:, :]).then_inc(s_wsplit, 1)
            V.memset(sc0[0], 0).then_inc(s_cols, 1)

            R = CT + NS

            def layernorm(xi, b_c):
                tot, v, y, t = (st[:, k, :] for k in range(4))
                link(V.tensor_reduce(tot, xi, X, ALU.add))
                link(V.tensor_scalar(tot, tot, -1.0 / C, None, ALU.mult))
                link(V.tensor_tensor(xi, xi, wide(tot, R), ALU.add))
                link(V.tensor_tensor(sq, xi, xi, ALU.mult))
                link(V.tensor_reduce(tot, sq, X, ALU.add))
                rstd(y, v, t, tot)
                link(V.tensor_tensor(sq, xi, wide(y, R), ALU.mult))

            def chunk(i, b):
                c = 2 * i + b
                dve.wait_ge(l0_got[b], 128 * (i + 1))
                dve.wait_ge(l0_in[b], 64 * (i + 1))
                layernorm(xin[b], c)
                if not (isinstance(i, int) and i == 0 and b == 0):
                    dve.wait_ge(l0_ht, c)
                ins = V.tensor_scalar(hx, sq, 0.0, None, ALU.max)
                ins.then_inc(l0_hx, 1)
                dve.wait_ge(l0_hx, c + 1)
                V.tensor_tensor(hb[:, bass.ds(c * NS * C, NS * C)].rearrange("p (n c) -> p n c", c=C), hx[:, CT:, :],
                                lnb_sb[:, :].rearrange("p (a c) -> p a c", a=1).broadcast_to([P, NS, C]), ALU.add)
                link(V.tensor_copy(dc0, col_f[:, bass.ds(c, 1), 0, :].rearrange("p a t -> p (a t)")))
                if not (isinstance(i, int) and i == 0):
                    dve.wait_ge(l0_seg, c - 1)
                    dve.wait_ge(l0_put[b], 128 * i)
                V.tensor_copy(sc0[b], col_i[:, bass.ds(c, 1), :].rearrange("p a t -> p (a t)"))
                for t in range(CT):
                    V.tensor_scalar(S0[b][:, t, :], dstb[b][:, t * P:(t + 1) * P], dc0[:, t:t + 1], None, ALU.is_equal)
                for s in range(4):
                    dve.wait_ge(l0_w, 4 * c + s + 1)
                    V.tensor_tensor(prod[s % 2].rearrange("p (r o) -> p r o", o=C),
                                    bank[s % 2][0:P, :].rearrange("p (r o) -> p r o", o=C),
                                    hx[:, 2 * s:2 * s + 2, :].rearrange("p t (c a) -> p (t c) a", a=1)
                                    .broadcast_to([P, 2 * C, C]), ALU.mult).then_inc(l0_prod, 1)
                    dve.wait_ge(l0_prod, 4 * c + s + 1)
                    ins = V.tensor_reduce(msg[b][:, 2 * s:2 * s + 2, 0:C],
                                          prod[s % 2].rearrange("p (t i o) -> p t o i", t=2, i=C), X, ALU.add)
                ins.then_inc(l0_msg, 1)
                if b == 1:
                    dve.wait_ge(sp_in, 16 * (i + 1))
                    if not (isinstance(i, int) and i == 0):
                        dve.wait_ge(sp_out, 96 * i)
                    link(V.tensor_copy(spb[:, 0, :], spx))
                    link(V.tensor_tensor(spr, spx, spb[:, 0, :], ALU.subtract))
                    link(V.tensor_copy(spb[:, 1, :], spr))
                    link(V.tensor_tensor(spr, spr, spb[:, 1, :], ALU.subtract))
                    V.tensor_copy(spb[:, 2, :], spr).then_inc(sp_done, 1)

            before = ch.count
            chunk(0, 0)
            chunk(0, 1)
            per = ch.count - before
            with dve.Fori(1, NCH // 2) as i:
                ch.enter(i, 1, per)
                chunk(i, 0)
                chunk(i, 1)
            ch.leave(NCH // 2 - 1)
            dve.wait_ge(l0_segc, NCH)
            link(V.tensor_tensor(bound0[:, :], bound0[:, :], live_e[0:C + 1, :], ALU.mult))
            V.tensor_tensor_scan(bound0[:, :], same_e[0:C + 1, :], bound0[:, :], 0.0, ALU.mult, ALU.add
                                 ).then_inc(l0_run, 1)

            for k in range(NB):
                a, z = ag[k % 2], nz[k % 2]
                tot, v, y, t, cnt, rc = (nst[:, j, :] for j in range(6))
                dve.wait_ge(n_in[k % 2], 32 * (k // 2 + 1))
                link(V.tensor_scalar(cnt, a[:, :, C:C + 1].rearrange("p n a -> p (n a)"), 1.0, None, ALU.max))
                link(V.reciprocal(rc, cnt))
                link(V.tensor_tensor(nt, a[:, :, 0:C], wide(rc, NN), ALU.mult))
                link(V.tensor_tensor(nt, nt, rr[:, k * NN * C:(k + 1) * NN * C].rearrange("p (n c) -> p n c", c=C),
                                     ALU.add))
                link(V.tensor_reduce(tot, nt, X, ALU.add))
                link(V.tensor_scalar(tot, tot, -1.0 / C, None, ALU.mult))
                V.tensor_tensor(nt, nt, wide(tot, NN), ALU.add).then_inc(n_sq, 1)
                dve.wait_ge(n_sqd, k + 1)
                link(V.tensor_reduce(tot, nq, X, ALU.add))
                rstd(y, v, t, tot)
                link(V.tensor_tensor(nt, nt, wide(y, NN), ALU.mult))
                link(V.tensor_tensor(nt, nt, lnw_sb[:, :].rearrange("p (a c) -> p a c", a=1)
                                     .broadcast_to([P, NN, C]), ALU.mult))
                if k >= 2:
                    dve.wait_ge(n_silu, k - 1)
                V.tensor_tensor(z, nt, hb[:, k * NN * C:(k + 1) * NN * C].rearrange("p (n c) -> p n c", c=C),
                                ALU.add).then_inc(n_z, 1)
                dve.wait_ge(n_z, k + 1)

            if part == 1:
                return

            dve.wait_ge(n_x1, NB)
            for b in range(2):
                ins = V.memset(stk[b][6 * C:6 * C + 3, :], 1.0)
            ins.then_inc(l1_ones, 1)

            def prelude(i, b):
                c = 2 * i + b
                xi = rows1[b]
                dve.wait_ge(l1_got[b], 128 * (i + 1))
                tot, v, y, t = (st1[:, j, :] for j in range(4))
                link(V.tensor_reduce(tot, xi, X, ALU.add))
                link(V.tensor_scalar(tot, tot, -1.0 / C, None, ALU.mult))
                link(V.tensor_tensor(xi, xi, wide(tot, CT), ALU.add))
                link(V.tensor_tensor(sq1, xi, xi, ALU.mult))
                link(V.tensor_reduce(tot, sq1, X, ALU.add))
                rstd(y, v, t, tot)
                link(V.tensor_tensor(sq1, xi, wide(y, CT), ALU.mult))
                V.tensor_scalar(h1[b], sq1, 0.0, None, ALU.max)
                link(V.tensor_copy(dc1[b], col_f[:, bass.ds(c, 1), :, :].rearrange("p a k t -> p (a k) t")))
                wait_pos(dve, l1_F, 4 * (c - 1))
                wait_pos(dve, l1_put[b], 128 * i)
                V.tensor_copy(sc1[b], col_i[:, bass.ds(c, 1), :].rearrange("p a t -> p (a t)"))
                for t in range(CT):
                    d = dsb[b][:, t * P:(t + 1) * P]
                    V.tensor_scalar(Sm[b][:, t, :], d, dc1[b][:, 0, t:t + 1], None, ALU.is_equal)
                    ins = V.tensor_scalar(Lm[b][:, t, :], d, dc1[b][:, 0, t:t + 1], dc1[b][:, 1, t:t + 1],
                                          ALU.is_equal, ALU.mult)
                ins.then_inc(l1_pre, 1)
                dve.wait_ge(l1_pre, c + 1)

            def slot(i, k):
                if valid(i, k) and k % 4 == 0:
                    if isinstance(i, int):
                        prelude((2 * i + k // 4) // 2, k // 4)
                    else:
                        prelude(i, k // 4)
                if valid(i, k):
                    n, b, s = 8 * i + k, k // 4, k % 4
                    for t in range(2):
                        dve.wait_ge(l1_A, 2 * n + t + 1)
                        V.tensor_tensor(En[k % 4][:, t, :, :].rearrange("p m (i o) -> p m i o", o=C),
                                        bank[t][0:P, :].rearrange("p (m i o) -> p m i o", m=2, o=C),
                                        h1[b][:, 2 * s + t, :].rearrange("p (m i o) -> p m i o", m=1, o=1)
                                        .broadcast_to([P, 2, C, C]), ALU.mult).then_inc(l1_e, 1)
                if valid(i, k - 1):
                    n, b, s, q = 8 * i + k - 1, ((k - 1) % 8) // 4, (k - 1) % 4, (k - 1) % 2
                    dve.wait_ge(l1_T, n + 1)
                    wait_pos(dve, l1_MT, n - 1)
                    for h in range(2):
                        ins = V.tensor_tensor_scan(Mx[q][:, h, :], flg[b][:, 2 * s * P:(2 * s + 2) * P],
                                                   bank[2][:, h * 2 * P:(h + 1) * 2 * P], 0.0, ALU.min, ALU.max)
                    ins.then_inc(l1_M, 1)
                if valid(i, k - 2):
                    n, q = 8 * i + k - 2, k % 2
                    dve.wait_ge(l1_B, n + 1)
                    wait_pos(dve, l1_ex, n - 1)
                    V.tensor_tensor(dd[q], En[(k - 2) % 4][:, :, 1, :],
                                    bank[4][0:P, :].rearrange("p (t w) -> p t w", t=2), ALU.subtract).then_inc(l1_d, 1)
                if valid(i, k - 3):
                    n, q = 8 * i + k - 3, (k - 3) % 2
                    dve.wait_ge(l1_R, n + 1)
                    wait_pos(dve, l1_F, n - 1)
                    link(V.tensor_tensor(at, ex[q], Rd[q], ALU.mult))
                    link(V.tensor_tensor(wv[q], at, En[(k - 3) % 4][:, :, 0, :], ALU.mult))
                    V.tensor_reduce(vr[q], wv[q].rearrange("p t (i o) -> p t o i", i=C), X, ALU.add).then_inc(l1_w, 1)

            for k in range(8):
                slot(0, k)
            with dve.Fori(1, STEPS // 8) as i:
                ch.enter(i, 1, LINKS1)
                for k in range(8):
                    slot(i, k)
            ch.leave(STEPS // 8 - 1)
            for k in range(4):
                slot(STEPS // 8, k)

            dve.wait_ge(l1_Fc, NCH)
            V.tensor_scalar(bm_nf, live_e[:, :], 2.0, -1.0, ALU.mult, ALU.add)
            link(V.tensor_scalar(bm_sf, same_e[:, :], 2.0, -1.0, ALU.mult, ALU.add))
            V.tensor_scalar(bm_nf, bm_nf, BIG, None, ALU.mult)
            V.memset(bm_c[:, :, 0:1], 0.0)
            link(V.tensor_scalar(bm_sf, bm_sf, BIG, None, ALU.mult))
            for h in range(2):
                link(V.tensor_tensor(bm_m[:, h, :], bound1[:, 0, h, :], bm_nf, ALU.min))
                link(V.tensor_tensor_scan(bm_x[:, h, :], bm_sf, bm_m[:, h, :], 0.0, ALU.min, ALU.max))
                link(V.tensor_tensor(bm_c[:, h, 1:], bm_x[:, h, :-1], bm_x[:, h, 1:], ALU.subtract))
                link(V.tensor_scalar(bm_c[:, h, :], bm_c[:, h, :], 0.0, None, ALU.min))
                ins = V.tensor_tensor(bm_w[:, h, :], bm_m[:, h, :], bm_x[:, h, :], ALU.subtract)
            ins.then_inc(b_d, 1)
            dve.wait_ge(b_x, 2)
            for h in range(2):
                link(V.tensor_tensor(bm_c[:, h, :], bm_c[:, h, :], same_e[:, :], ALU.mult))
                link(V.tensor_tensor(bm_w[:, h, :], bm_w[:, h, :], bound1[:, 1, h, :], ALU.mult))
                link(V.tensor_tensor(bm_a[:, h, :], bm_w[:, h, :], bound1[:, 2, h, :], ALU.mult))
                link(V.tensor_tensor_scan(bm_x[:, h, :], bm_c[:, h, :], bm_w[:, h, :], 0.0, ALU.mult, ALU.add))
                link(V.tensor_tensor_scan(bm_m[:, h, :], bm_c[:, h, :], bm_a[:, h, :], 0.0, ALU.mult, ALU.add))
                link(V.reciprocal(bm_r[:, h, :], bm_x[:, h, :]))
                ins = V.tensor_tensor(bm_a[:, h, :], bm_m[:, h, :], bm_r[:, h, :], ALU.mult)
            ins.then_inc(b_q, 1)
            for k in range(NB):
                dve.wait_ge(f_in[k % 3], 16 * (k // 3 + 1))
                V.tensor_tensor(fin[k % 3], fin[k % 3], hb[:, k * NN * C:(k + 1) * NN * C], ALU.add).then_inc(f_sum, 1)


_OUTS = [((N, C), 'float32')]
PART = 2


def kernel(**inputs):
    import numpy as _np
    import concourse.bacc as _bacc
    from concourse import mybir as _mybir
    from concourse.bass_utils import run_bass_kernel_spmd as _run

    nc = _bacc.Bacc("TRN2", target_bir_lowering=False, num_devices=1)
    a = {k: _np.asarray(v) for k, v in inputs.items()}
    dst_tiles = a["dst"].reshape(T, P)
    ends = _np.concatenate([dst_tiles[:, [0, P - 1]].reshape(-1), _np.full(1, -1, a["dst"].dtype)])
    sent = {
        "x": a["x"], "src_cols": a["src"].reshape(T, P).T, "dst": a["dst"], "dst_cols": dst_tiles.T,
        "ends": ends,
        "end_cols": _np.concatenate([ends[:-1].reshape(EG, EP).T, ends[1:].reshape(EG, EP).T]),
        "ea16T": a["edge_attr_16"].T, "ea8T": a["edge_attr_8"].T,
        "W1": a["L0_gnn_W1"], "b1": a["L0_gnn_b1"], "W2": a["L0_gnn_W2"], "b2": a["L0_gnn_b2"],
        "root": a["L0_gnn_root"], "bias": a["L0_gnn_bias"], "ln_w": a["L0_gnn_ln_w"], "ln_b": a["L0_gnn_ln_b"],
        "Wm": a["L1_gnn_W_msg"], "bm": a["L1_gnn_b_msg"], "Wa": a["L1_gnn_W_attn"], "ba": a["L1_gnn_b_attn"],
        "ident": _np.eye(128, dtype=_np.float32),
        "fold": _np.tile(_np.eye(C, dtype=_np.float32), (8, 1)),
    }
    arrays, args = {}, []
    for name, value in sent.items():
        value = _np.ascontiguousarray(value)
        arrays[f"in_{name}_dram"] = value
        args.append(nc.dram_tensor(f"in_{name}_dram", value.shape, _mybir.dt.from_np(value.dtype),
                                   kind="ExternalInput").ap())
    for i, (shape, dtype) in enumerate(_OUTS):
        args.append(nc.dram_tensor(f"out_{i}_dram", shape, _mybir.dt.from_np(_np.dtype(dtype)),
                                   kind="ExternalOutput").ap())
    gnn_kernel(nc, *args, part=PART)
    r = _run(nc, [arrays], core_ids=[0])
    return r.results[0]["out_0_dram"]
```

```python
from contextlib import ExitStack

import concourse.bass as bass
from concourse import mybir

F32 = mybir.dt.float32
I32 = mybir.dt.int32
BF16 = mybir.dt.bfloat16
ALU = mybir.AluOpType
ACT = mybir.ActivationFunctionType
X = mybir.AxisListType.X

N = 100000
E = 50000
C = 16
P = 125
T = E // P
CT = 8
CE = CT * P
NCH = T // CT
NP = N // P
NS = NP // NCH
W = C * C
HID = 64
K8 = 8
ENDS = 2 * T
EP = 100
EG = ENDS // EP
SPLITC = E // 8 // (NCH // 2)
NB = 10
NN = NP // NB
EPS = 1e-5
SKIP = float(1 << 20)
BIG = 3.0e38
LINKS1 = 52
STEPS = NCH * 4


class Chain:

    def __init__(self, sem):
        self.sem, self.count, self.loop = sem, 0, None

    def next(self):
        self.count += 1
        if self.loop is None:
            return self.count
        i, first, per = self.loop
        return i * per + (self.count - first * per)

    def enter(self, i, first, per):
        self.loop = (i, first, per)
        self.start = self.count

    def leave(self, times):
        per = self.loop[2]
        assert self.count - self.start == per, (self.count, self.start, per)
        self.count = self.start + times * per
        self.loop = None


def gnn_kernel(nc, x, src_cols, dst, dst_cols, ends, end_cols, ea16T, ea8T, W1, b1, W2, b2, root, bias, ln_w, ln_b,
               Wm, bm, Wa, ba, ident, fold, out, part=2):
    agg_tab = nc.dram_tensor("agg_tab", [N, C + 1], F32, kind="Internal").ap()
    ft_tab = nc.dram_tensor("ft_tab", [N, C], F32, kind="Internal").ap()
    x1_tab = nc.dram_tensor("x1_tab", [N, C], F32, kind="Internal").ap()
    stack_tab = nc.dram_tensor("stack_tab", [6 * C, E], BF16, kind="Internal").ap()
    flag_tab = nc.dram_tensor("flag_tab", [E], F32, kind="Internal").ap()
    row_tab = nc.dram_tensor("row_tab", [4, T, 2, W], F32, kind="Internal").ap()

    with ExitStack() as ctx:
        def sb(name, shape, dt=F32):
            return ctx.enter_context(nc.sbuf_tensor(name, shape, dt))

        def sem(name):
            return ctx.enter_context(nc.semaphore(name))

        def sem2(name):
            return [sem(f"{name}_even"), sem(f"{name}_odd")]

        hb = sb("hb", [P, NP * C])
        ident_sb = sb("ident_sb", [128, 128])
        fold_sb = sb("fold_sb", [128, C])
        w1_sb = sb("w1_sb", [K8, HID])
        b1_sb = sb("b1_sb", [HID, 1])
        w2_sb = sb("w2_sb", [HID + 1, W])
        root_sb = sb("root_sb", [128, 128])
        bias_row = sb("bias_row", [1, 128])
        ones_row = sb("ones_row", [1, P])
        lnw_sb = sb("lnw_sb", [P, C])
        lnb_sb = sb("lnb_sb", [P, C])
        wf_sb = sb("wf_sb", [C + 1, 2 * W])
        wres = sb("wres", [C + 1, 2 * W])
        wpart = sb("wpart", [C + 1, 3, 2 * W], BF16)
        wstack = sb("wstack", [6 * C + 3, 2 * W], BF16)
        col_f = sb("col_f", [P, NCH, 2, CT])
        col_i = sb("col_i", [P, NCH, CT], I32)
        same_e = sb("same_e", [128, ENDS])
        live_e = sb("live_e", [128, ENDS])
        idx_e = sb("idx_e", [EP, EG], I32)
        bound0 = sb("bound0", [C + 1, ENDS])

        ARENA = 27400
        arena = sb("arena", [128, ARENA])
        place = [0]

        def carve(rows, cols, dt=F32):
            words = cols if dt != BF16 else cols // 2
            a = arena[0:rows, place[0]:place[0] + words]
            place[0] += words
            assert place[0] <= ARENA, place[0]
            return a if dt == F32 else a.bitcast(dt)

        rr = carve(P, NP * C)
        base = place[0]
        xin = [carve(P, (CT + NS) * C).rearrange("p (t c) -> p t c", c=C) for _ in range(2)]
        hx = carve(P, (CT + NS) * C).rearrange("p (t c) -> p t c", c=C)
        sq = carve(P, (CT + NS) * C).rearrange("p (t c) -> p t c", c=C)
        st = carve(P, 4 * (CT + NS)).rearrange("p (k t) -> p k t", k=4)
        src0 = [carve(P, CT, I32) for _ in range(2)]
        ea8 = [carve(K8, CE) for _ in range(2)]
        dstb = [carve(P, CE, I32) for _ in range(2)]
        hid = [carve(HID + 1, CE) for _ in range(2)]
        S0 = [carve(P, CT * P).rearrange("p (t e) -> p t e", t=CT) for _ in range(2)]
        prod = [carve(P, 2 * W) for _ in range(2)]
        msg = [carve(P, CT * (C + 1)).rearrange("p (t c) -> p t c", t=CT) for _ in range(2)]
        segs = [carve(P, CT * (C + 1)).rearrange("p (t c) -> p t c", t=CT) for _ in range(2)]
        sc0 = [carve(P, CT, I32) for _ in range(2)]
        dc0 = carve(P, CT)
        hT = carve(128, 2 * P).rearrange("p (g e) -> p g e", g=2)
        spx = carve(128, SPLITC)
        spr = carve(128, SPLITC)
        spb = carve(128, 3 * SPLITC, BF16).rearrange("p (k n) -> p k n", k=3)
        end_seg = carve(EP, EG * (C + 1)).rearrange("p (g c) -> p g c", g=EG)
        top0 = place[0]
        place[0] = 0
        d_i = carve(P, T, I32)
        d_next = carve(P, T, I32)
        d_first = carve(P, T, I32)
        d_last = carve(P, T, I32)
        c1, c2, c3, c4 = (carve(P, T) for _ in range(4))
        dn = carve(100, 500, I32)
        dq = carve(100, 500)
        e_b = carve(128, ENDS, I32)
        e_c = carve(EP, EG, I32)
        e_n = carve(EP, EG, I32)
        e_1 = carve(EP, EG)
        e_2 = carve(EP, EG)
        assert place[0] <= base
        place[0] = top0
        zero = carve(P, NP * (C + 1) // 8)
        place[0] = base
        ag = [carve(P, NN * (C + 1)).rearrange("p (n c) -> p n c", n=NN) for _ in range(2)]
        xn = [carve(P, NN * C).rearrange("p (n c) -> p n c", n=NN) for _ in range(2)]
        nt = carve(P, NN * C).rearrange("p (n c) -> p n c", n=NN)
        nq = carve(P, NN * C).rearrange("p (n c) -> p n c", n=NN)
        nz = [carve(P, NN * C).rearrange("p (n c) -> p n c", n=NN) for _ in range(2)]
        ns = [carve(P, NN * C).rearrange("p (n c) -> p n c", n=NN) for _ in range(1)]
        nst = carve(P, 6 * NN).rearrange("p (k n) -> p k n", k=6)

        place[0] = 0
        src1 = [carve(P, CT, I32) for _ in range(2)]
        rows1 = [carve(P, CT * C).rearrange("p (t c) -> p t c", c=C) for _ in range(2)]
        h1 = [carve(P, CT * C).rearrange("p (t c) -> p t c", c=C) for _ in range(2)]
        sq1 = carve(P, CT * C).rearrange("p (t c) -> p t c", c=C)
        st1 = carve(P, 4 * CT).rearrange("p (k t) -> p k t", k=4)
        stk = [carve(6 * C + 3, CE, BF16) for _ in range(2)]
        flg = [carve(128, CE) for _ in range(2)]
        dsb = [carve(P, CE, I32) for _ in range(2)]
        dc1 = [carve(P, 2 * CT).rearrange("p (k t) -> p k t", k=2) for _ in range(2)]
        sc1 = [carve(P, CT, I32) for _ in range(2)]
        base1 = place[0]
        Sm = [carve(P, CT * P).rearrange("p (t e) -> p t e", t=CT) for _ in range(2)]
        Lm = [carve(P, CT * P).rearrange("p (t e) -> p t e", t=CT) for _ in range(2)]
        En = [carve(P, 4 * W).rearrange("p (t m w) -> p t m w", t=2, m=2) for _ in range(8)]
        Mx = [carve(128, 4 * P).rearrange("p (h e) -> p h e", h=2) for _ in range(2)]
        MT = [carve(P, 2 * W).rearrange("p (t w) -> p t w", t=2) for _ in range(2)]
        dd = [carve(P, 2 * W).rearrange("p (t w) -> p t w", t=2) for _ in range(2)]
        ex = [carve(P, 2 * W).rearrange("p (t w) -> p t w", t=2) for _ in range(2)]
        lnd = [carve(P, 2 * W).rearrange("p (t w) -> p t w", t=2) for _ in range(2)]
        Rd = [carve(P, 2 * W).rearrange("p (t w) -> p t w", t=2) for _ in range(2)]
        at = carve(P, 2 * W).rearrange("p (t w) -> p t w", t=2)
        wv = [carve(P, 2 * W).rearrange("p (t w) -> p t w", t=2) for _ in range(2)]
        arow = [carve(2, 2 * W) for _ in range(2)]
        vr = [carve(P, 2 * C).rearrange("p (t c) -> p t c", t=2) for _ in range(2)]
        fts = [carve(P, CT * C).rearrange("p (t c) -> p t c", t=CT) for _ in range(2)]
        top1, place[0] = place[0] - 2 * CT * C, base1
        rows4 = [carve(EP, EG * W).rearrange("p (g w) -> p g w", g=EG) for _ in range(4)]
        bound1 = carve(128, 6 * ENDS).rearrange("p (m h e) -> p m h e", m=3, h=2)
        bm_r = carve(128, 2 * ENDS).rearrange("p (h e) -> p h e", h=2)
        bm_nf, bm_sf = (carve(128, ENDS) for _ in range(2))
        end_ft = carve(EP, EG * C).rearrange("p (g c) -> p g c", g=EG)
        assert place[0] <= top1
        place[0] = base1
        bm_m, bm_x, bm_c, bm_w, bm_a = (carve(128, 2 * ENDS).rearrange("p (h e) -> p h e", h=2) for _ in range(5))
        assert place[0] <= base1 + 4 * EG * W
        place[0] = base1
        fin = [carve(P, NN * C) for _ in range(3)]

        bank = [ctx.enter_context(nc.psum_tensor(f"bank{i}", [128, 512], F32)) for i in range(8)]

        s_const = sem("s_const")
        s_dload = sem("s_dload")
        s_zero = sem("s_zero")
        s_zeroed = sem("s_zeroed")
        s_zeroed_ft = sem("s_zeroed_ft")
        s_flag = sem("s_flag")
        s_flagst = sem("s_flagst")
        s_root0 = sem("s_root0")
        s_ones = sem("s_ones")
        s_pad = sem("s_pad")
        s_wsplit = sem("s_wsplit")
        s_wstack = sem("s_wstack")
        s_dve = sem("s_dve")
        s_act = sem("s_act")
        s_cols = sem("s_cols")
        l0_in = sem2("l0_in")
        l0_got = sem2("l0_got")
        l0_z = sem("l0_z")
        l0_h = sem("l0_h")
        l0_w = sem("l0_w")
        l0_prod = sem("l0_prod")
        l0_hx = sem("l0_hx")
        l0_ht = sem("l0_ht")
        l0_htc = sem("l0_htc")
        l0_root = sem("l0_root")
        l0_rootc = sem("l0_rootc")
        l0_msg = sem("l0_msg")
        l0_seg = sem("l0_seg")
        l0_segc = sem("l0_segc")
        l0_sc = sem("l0_sc")
        l0_put = sem2("l0_put")
        l0_gate = sem("l0_gate")
        sp_in = sem("sp_in")
        sp_done = sem("sp_done")
        sp_out = sem("sp_out")
        l0_run = sem("l0_run")
        l0_runT = sem("l0_runT")
        l0_runc = sem("l0_runc")
        l0_end = sem("l0_end")
        n_in = sem2("n_in")
        n_sq = sem("n_sq")
        n_sqd = sem("n_sqd")
        n_z = sem("n_z")
        n_silu = sem("n_silu")
        n_x1 = sem("n_x1")
        n_out = sem("n_out")

        l1_in = sem2("l1_in")
        l1_got = sem2("l1_got")
        l1_gate = sem("l1_gate")
        l1_sp = sem("l1_sp")
        l1_ones = sem("l1_ones")
        l1_pre = sem("l1_pre")
        l1_A = sem("l1_A")
        l1_e = sem("l1_e")
        l1_T = sem("l1_T")
        l1_M = sem("l1_M")
        l1_MT = sem("l1_MT")
        l1_MTc = sem("l1_MTc")
        l1_B = sem("l1_B")
        l1_d = sem("l1_d")
        l1_ex = sem("l1_ex")
        l1_D = sem("l1_D")
        l1_ln = sem("l1_ln")
        l1_R = sem("l1_R")
        l1_w = sem("l1_w")
        l1_F = sem("l1_F")
        l1_idx = sem2("l1_idx")
        l1_sc = sem("l1_sc")
        l1_S = sem("l1_S")
        l1_L = sem("l1_L")
        l1_ac = sem("l1_ac")
        l1_rowd = sem2("l1_rowd")
        l1_rowl = sem2("l1_rowl")
        l1_rowa = sem2("l1_rowa")
        b_in = sem("b_in")
        b_row = sem("b_row")
        b_T = sem("b_T")
        b_Tc = sem("b_Tc")
        l1_Fc = sem("l1_Fc")
        l1_put = sem2("l1_put")
        b_d = sem("b_d")
        b_x = sem("b_x")
        b_q = sem("b_q")
        b_f = sem("b_f")
        b_fc = sem("b_fc")
        b_put = sem("b_put")
        f_in = [sem(f"f_in{k}") for k in range(3)]
        f_sum = sem("f_sum")
        f_out = [sem(f"f_out{k}") for k in range(3)]

        def wait_pos(eng, s, value):
            if not (isinstance(value, int) and value <= 0):
                eng.wait_ge(s, value)

        def valid(i, k):
            return not isinstance(i, int) or 0 <= 8 * i + k < STEPS

        def run_slots(eng, slot, chain=None, links=0):
            turns = STEPS // 8
            for k in range(16):
                slot(k // 8, k % 8)
            with eng.Fori(2, turns - 1) as i:
                if chain:
                    chain.enter(i, 2, links)
                for k in range(8):
                    slot(i, k)
            if chain:
                chain.leave(turns - 3)
            for k in range(8):
                slot(turns - 1, k)
            for k in range(6):
                slot(turns, k)

        def both(a):
            return a.rearrange("p (t w) -> p t w", t=2)

        block = ctx.enter_context(nc.Block())

        def bcast_rows(ap, rows, cols):
            return ap.rearrange("(a n) -> a n", a=1).broadcast_to([rows, cols])

        x_part = x.rearrange("(p n) c -> p (n c)", p=P)

        @block.sync
        def _(sp):
            def load(i, b):
                c = 2 * i + b
                if not (isinstance(i, int) and i == 0):
                    sp.wait_ge(l0_msg, c - 1)
                    sp.wait_ge(l0_seg, c - 1)
                sp.dma_start(src0[b], src_cols[:, bass.ds(c * CT, CT)]).then_inc(l0_in[b], 16)
                sp.dma_start(ea8[b], ea8T[:, bass.ds(c * CE, CE)]).then_inc(l0_in[b], 16)
                sp.dma_start(dstb[b], bcast_rows(dst[bass.ds(c * CE, CE)], P, CE)).then_inc(l0_in[b], 16)
                sp.dma_start(xin[b][:, CT:, :].rearrange("p t c -> p (t c)"),
                             x_part[:, bass.ds(c * NS * C, NS * C)]).then_inc(l0_in[b], 16)
                if b == 1:
                    if not (isinstance(i, int) and i == 0):
                        sp.wait_ge(sp_done, i)
                    sp.dma_start(spx, ea16T.rearrange("c (b n) -> (c b) n", b=8)[:, bass.ds(i * SPLITC, SPLITC)]
                                 ).then_inc(sp_in, 16)

            load(0, 0)
            for dst_ap, src_ap in (
                (d_i, dst_cols), (d_first, bcast_rows(dst_cols[0, :], P, T)),
                (d_last, bcast_rows(dst_cols[P - 1, :], P, T)), (dn, dst.rearrange("(p n) -> p n", p=100)),
                (e_b, bcast_rows(ends[0:ENDS], 128, ENDS)), (e_c, end_cols[0:EP, :]),
                (e_n, end_cols[EP:2 * EP, :]),
            ):
                sp.dma_start(dst_ap, src_ap).then_inc(s_dload, 16)
            sp.wait_ge(s_pad, 1)
            sp.dma_start(d_next[0:P - 1, :], dst_cols[1:P, :]).then_inc(s_dload, 16)
            for dst_ap, src_ap in (
                (ident_sb[:, :], ident), (fold_sb[:, :], fold), (w1_sb[:, :], W1),
                (b1_sb[:, :], b1.rearrange("(h a) -> h a", a=1)), (w2_sb[0:HID, :], W2),
                (w2_sb[HID:HID + 1, :], b2.rearrange("(a n) -> a n", a=1)),
                (lnw_sb[:, :], bcast_rows(ln_w, P, C)), (lnb_sb[:, :], bcast_rows(ln_b, P, C)),
                (wf_sb[0:C, 0:W], Wm), (wf_sb[0:C, W:2 * W], Wa),
                (wf_sb[C:C + 1, 0:W], bm.rearrange("(a n) -> a n", a=1)),
                (wf_sb[C:C + 1, W:2 * W], ba.rearrange("(a n) -> a n", a=1)),
            ):
                sp.dma_start(dst_ap, src_ap).then_inc(s_const, 16)
            sp.wait_ge(s_root0, 1)
            for n in range(8):
                sp.dma_start(root_sb[n * C:(n + 1) * C, n * C:(n + 1) * C], root).then_inc(s_const, 16)
                sp.dma_start(bias_row[0:1, n * C:(n + 1) * C], bias.rearrange("(a n) -> a n", a=1)).then_inc(s_const, 16)

            load(0, 1)
            with sp.Fori(1, NCH // 2) as i:
                load(i, 0)
                load(i, 1)

            sp.wait_ge(l0_put[0], 128 * (NCH // 2))
            sp.wait_ge(l0_put[1], 128 * (NCH // 2))
            sp.wait_ge(l0_end, 16 * EG)
            sp.wait_ge(l0_rootc, NCH)
            sp.wait_ge(sp_out, 96 * (NCH // 2))
            for k in range(NB):
                if k >= 2:
                    sp.wait_ge(n_x1, k - 1)
                sp.dma_start(ag[k % 2].rearrange("p n c -> p (n c)"),
                             agg_tab.rearrange("(p n) c -> p (n c)", p=P)[:, k * NN * (C + 1):(k + 1) * NN * (C + 1)]
                             ).then_inc(n_in[k % 2], 16)
                sp.dma_start(xn[k % 2].rearrange("p n c -> p (n c)"), x_part[:, k * NN * C:(k + 1) * NN * C]
                             ).then_inc(n_in[k % 2], 16)

            if part == 1:
                return

            sp.wait_ge(n_x1, NB)
            sp.wait_ge(n_out, 16 * NB)

            def load1(i, k):
                c, b = 2 * i + k // 4, (k % 8) // 4
                wait_pos(sp, l1_A, 8 * (c - 1))
                sp.sem_inc(l1_sp, 1)
                wait_pos(sp, l1_M, 4 * (c - 1))
                sp.sem_inc(l1_sp, 1)
                sp.dma_start(stk[b][0:6 * C, :], stack_tab[:, bass.ds(c * CE, CE)]).then_inc(l1_in[b], 16)
                sp.dma_start(flg[b], bcast_rows(flag_tab[bass.ds(c * CE, CE)], 128, CE)).then_inc(l1_in[b], 16)
                sp.dma_start(dsb[b], bcast_rows(dst[bass.ds(c * CE, CE)], P, CE)).then_inc(l1_in[b], 16)

            def load_idx(i, k):
                c, b = 2 * i + k // 4, (k % 8) // 4
                wait_pos(sp, l1_pre, c - 1)
                sp.sem_inc(l1_sp, 1)
                sp.dma_start(src1[b], src_cols[:, bass.ds(c * CT, CT)]).then_inc(l1_idx[b], 16)

            def rows_of(m, i, k):
                return row_tab[m, bass.ds(16 * i + 2 * k, 2), :, :].rearrange("t q w -> q t w")

            def slot(i, k):
                if k % 4 == 1 and valid(i, k + 3):
                    load1(i, k + 3)
                if k % 4 == 2 and valid(i, k + 6):
                    load_idx(i, k + 6)
                if valid(i, k - 3):
                    n, q = 8 * i + k - 3, (k - 3) % 2
                    sp.wait_ge(l1_d, n + 1)
                    sp.sem_inc(l1_sp, 1)
                    sp.dma_start(rows_of(0, i, k - 3), En[(k - 3) % 8][0:P:P - 1, :, 1, :]).then_inc(l1_rowd[q], 16)
                    sp.dma_start(rows_of(1, i, k - 3), dd[q][0:P:P - 1, :, :]).then_inc(l1_rowd[q], 16)
                if valid(i, k - 4):
                    n, q = 8 * i + k - 4, k % 2
                    sp.wait_ge(l1_ln, n + 1)
                    sp.sem_inc(l1_sp, 1)
                    sp.dma_start(rows_of(2, i, k - 4), lnd[q][0:P:P - 1, :, :]).then_inc(l1_rowl[q], 16)
                if valid(i, k - 5):
                    n, q = 8 * i + k - 5, (k - 5) % 2
                    sp.wait_ge(l1_ac, n + 1)
                    sp.sem_inc(l1_sp, 1)
                    sp.dma_start(rows_of(3, i, k - 5), both(arow[q])).then_inc(l1_rowa[q], 16)

            load_idx(0, 0)
            load_idx(0, 4)
            load1(0, 0)
            run_slots(sp, slot)
            for q in range(2):
                sp.wait_ge(l1_rowd[q], 16 * STEPS)
                sp.wait_ge(l1_rowl[q], 8 * STEPS)
                sp.wait_ge(l1_rowa[q], 8 * STEPS)
            sp.wait_ge(l1_F, STEPS)
            for m in range(4):
                sp.dma_start(rows4[m], row_tab[m, :, :, :].rearrange("t q w -> (t q) w")
                             .rearrange("(g p) w -> p g w", p=EP)).then_inc(b_in, 16)
            sp.wait_ge(l1_put[0], 128 * (NCH // 2))
            sp.wait_ge(l1_put[1], 128 * (NCH // 2))
            sp.wait_ge(b_put, 16 * EG)
            for k in range(NB + 2):
                if k < NB:
                    if k >= 3:
                        sp.wait_ge(f_out[k % 3], 16 * (k // 3))
                    sp.dma_start(fin[k % 3], ft_tab.rearrange("(p n) c -> p (n c)", p=P)[:, k * NN * C:(k + 1) * NN * C]
                                 ).then_inc(f_in[k % 3], 16)
                if k >= 2:
                    j = k - 2
                    sp.wait_ge(f_sum, j + 1)
                    sp.dma_start(out.rearrange("(p n) c -> p (n c)", p=P)[:, j * NN * C:(j + 1) * NN * C], fin[j % 3]
                                 ).then_inc(f_out[j % 3], 16)
            for k in range(3):
                sp.wait_ge(f_out[k], 16 * len(range(k, NB, 3)))

        @block.gpsimd
        def _(pool):
            pool.memset(root_sb[:, :], 0.0).then_inc(s_root0, 1)
            pool.memset(zero, 0.0).then_inc(s_zero, 1)

            def gather(i, b):
                pool.wait_ge(l0_in[b], 64 * (i + 1))
                pool.sem_inc(l0_gate, 1)
                for t in range(CT):
                    pool.indirect_dma_start(out=xin[b][:, t, :], out_offset=None, in_=x,
                                            in_offset=bass.IndirectOffsetOnAxis(ap=src0[b][:, t:t + 1], axis=0)
                                            ).then_inc(l0_got[b], 16)

            def scatter(i, b):
                pool.wait_ge(l0_segc, 2 * i + b + 1)
                pool.wait_ge(l0_sc, 2 * i + b + 1)
                pool.sem_inc(l0_gate, 1)
                for t in range(CT):
                    pool.indirect_dma_start(out=agg_tab, out_offset=bass.IndirectOffsetOnAxis(ap=sc0[b][:, t:t + 1], axis=0),
                                            in_=segs[b][:, t, :], in_offset=None,
                                            bounds_check=N - 1, oob_is_err=False).then_inc(l0_put[b], 16)

            gather(0, 0)
            gather(0, 1)
            pool.wait_ge(s_zeroed, 128)
            with pool.Fori(1, NCH // 2) as i:
                gather(i, 0)
                scatter(i - 1, 0)
                gather(i, 1)
                scatter(i - 1, 1)
            scatter(NCH // 2 - 1, 0)
            scatter(NCH // 2 - 1, 1)
            pool.wait_ge(l0_runc, 1)
            for g in range(EG):
                pool.indirect_dma_start(out=agg_tab, out_offset=bass.IndirectOffsetOnAxis(ap=idx_e[:, g:g + 1], axis=0),
                                        in_=end_seg[:, g, :], in_offset=None,
                                        bounds_check=N - 1, oob_is_err=False).then_inc(l0_end, 16)

            for k in range(NB):
                pool.wait_ge(n_silu, k + 1)
                pool.wait_ge(n_in[k % 2], 32 * (k // 2 + 1))
                pool.tensor_tensor(hb[:, k * NN * C:(k + 1) * NN * C], ns[0].rearrange("p n c -> p (n c)"),
                                   xn[k % 2].rearrange("p n c -> p (n c)"), ALU.add).then_inc(n_x1, 1)

            if part == 1:
                return

            pool.wait_ge(s_zeroed_ft, 128)
            pool.wait_ge(n_out, 16 * NB)

            def gather1(i, d):
                b = d % 2
                pool.wait_ge(l1_idx[b], 16 * (i + d // 2 + 1))
                wait_pos(pool, l1_pre, 2 * i + d - 1)
                pool.sem_inc(l1_gate, 1)
                for t in range(CT):
                    pool.indirect_dma_start(out=rows1[b][:, t, :], out_offset=None, in_=x1_tab,
                                            in_offset=bass.IndirectOffsetOnAxis(ap=src1[b][:, t:t + 1], axis=0)
                                            ).then_inc(l1_got[b], 16)

            def scatter1(i, d):
                b = d % 2
                pool.wait_ge(l1_Fc, 2 * i + d + 1)
                pool.wait_ge(l1_sc, 2 * i + d + 1)
                pool.sem_inc(l1_gate, 1)
                for t in range(CT):
                    pool.indirect_dma_start(out=ft_tab, out_offset=bass.IndirectOffsetOnAxis(ap=sc1[b][:, t:t + 1], axis=0),
                                            in_=fts[b][:, t, :], in_offset=None,
                                            bounds_check=N - 1, oob_is_err=False).then_inc(l1_put[b], 16)

            for c in range(3):
                gather1(0, c)
            with pool.Fori(1, NCH // 2 - 1) as i:
                gather1(i, 1)
                scatter1(i, -2)
                gather1(i, 2)
                scatter1(i, -1)
            gather1(0, NCH - 1)
            for c in range(NCH - 4, NCH):
                scatter1(0, c)
            pool.wait_ge(b_fc, 1)
            for g in range(EG):
                pool.indirect_dma_start(out=ft_tab, out_offset=bass.IndirectOffsetOnAxis(ap=idx_e[:, g:g + 1], axis=0),
                                        in_=end_ft[:, g, :], in_offset=None,
                                        bounds_check=N - 1, oob_is_err=False).then_inc(b_put, 16)

        @block.tensor
        def _(pe):
            pe.wait_ge(s_const, 16 * 28)
            pe.wait_ge(s_ones, 1)

            def weights(i, b, s):
                c = 2 * i + b
                if not (isinstance(i, int) and i == 0 and b == 0 and s < 2):
                    pe.wait_ge(l0_prod, 4 * c + s - 1)
                for k in range(2):
                    t = 2 * s + k
                    ins = pe.matmul(bank[s % 2][0:P, k * W:(k + 1) * W], hid[b][:, t * P:(t + 1) * P], w2_sb[:, :],
                                    start=True, stop=True)
                ins.then_inc(l0_w, 1)

            def chunk(i, b):
                c = 2 * i + b
                pe.wait_ge(l0_in[b], 64 * (i + 1))
                if not (isinstance(i, int) and i == 0 and b == 0):
                    pe.wait_ge(l0_h, c)
                for k in range(2):
                    ins = pe.matmul(bank[2 + k][0:HID, 0:CE // 2], w1_sb[:, :], ea8[b][:, k * CE // 2:(k + 1) * CE // 2],
                                    start=True, stop=True)
                ins.then_inc(l0_z, 1)
                pe.wait_ge(l0_h, c + 1)
                weights(i, b, 0)
                weights(i, b, 1)
                pe.wait_ge(l0_hx, c + 1)
                if not (isinstance(i, int) and i == 0 and b == 0):
                    pe.wait_ge(l0_htc, c)
                for g in range(2):
                    ins = pe.transpose(bank[4][:, g * 128:g * 128 + P],
                                       hx[:, CT + 8 * g:CT + 8 * g + 8, :].rearrange("p t c -> p (t c)"),
                                       ident_sb[0:P, 0:P])
                ins.then_inc(l0_ht, 1)
                weights(i, b, 2)
                weights(i, b, 3)
                pe.wait_ge(l0_htc, c + 1)
                if not (isinstance(i, int) and i == 0 and b == 0):
                    pe.wait_ge(l0_rootc, c)
                for g in range(2):
                    pe.matmul(bank[5][0:P, g * 128:(g + 1) * 128], hT[:, g, :], root_sb[:, :], start=True, stop=False)
                    ins = pe.matmul(bank[5][0:P, g * 128:(g + 1) * 128], ones_row[:, :], bias_row[:, :],
                                    start=False, stop=True)
                ins.then_inc(l0_root, 1)
                pe.wait_ge(l0_msg, c + 1)
                if not (isinstance(i, int) and i == 0 and b == 0):
                    pe.wait_ge(l0_segc, c)
                for t in range(CT):
                    pe.matmul(bank[6][0:P, t * (C + 1):(t + 1) * (C + 1)], S0[b][:, t, :], msg[b][:, t, :],
                              start=True, stop=True)
                    ins = pe.matmul(bank[7][0:C + 1, 2 * t:2 * t + 2], msg[b][:, t, :], S0[b][:, t, 0:P:P - 1],
                                    start=True, stop=True)
                ins.then_inc(l0_seg, 1)

            chunk(0, 0)
            chunk(0, 1)
            with pe.Fori(1, NCH // 2) as i:
                chunk(i, 0)
                chunk(i, 1)
            pe.wait_ge(l0_run, 1)
            for g in range(EG):
                ins = pe.transpose(bank[6][0:EP, g * (C + 1):(g + 1) * (C + 1)], bound0[:, g * EP:(g + 1) * EP],
                                   ident_sb[0:C + 1, 0:C + 1])
            ins.then_inc(l0_runT, 1)

            if part == 1:
                return

            pe.wait_ge(s_wstack, 16 * 9)
            pe.wait_ge(l1_ones, 1)
            pe.wait_ge(l0_runc, 1)

            def edge_weights(i, k):
                b, s = (k % 8) // 4, k % 4
                n = 8 * i + k
                if s == 0:
                    if isinstance(i, int):
                        pe.wait_ge(l1_in[b], 48 * (n // 8 + 1))
                    else:
                        pe.wait_ge(l1_in[b], 48 * (i + k // 8 + 1))
                for t in range(2):
                    wait_pos(pe, l1_e, 2 * n + t - 1)
                    pe.matmul(bank[t][0:P, :], stk[b][:, (2 * s + t) * P:(2 * s + t + 1) * P], wstack[:, :],
                              start=True, stop=True).then_inc(l1_A, 1)

            def slot(i, k):
                if valid(i, k):
                    edge_weights(i, k)
                if valid(i, k - 4):
                    n, q, b, s = 8 * i + k - 4, k % 2, ((k - 4) % 8) // 4, k % 4
                    pe.wait_ge(l1_ex, n + 1)
                    wait_pos(pe, l1_ln, n)
                    for t in range(2):
                        ins = pe.matmul(bank[5][0:P, t * W:(t + 1) * W], Sm[b][:, 2 * s + t, :], ex[q][:, t, :],
                                        start=True, stop=True)
                    ins.then_inc(l1_D, 1)
                if valid(i, k - 1):
                    n = 8 * i + k - 1
                    pe.wait_ge(l1_e, 2 * n + 2)
                    wait_pos(pe, l1_M, n)
                    for t in range(2):
                        for h in range(2):
                            ins = pe.transpose(bank[2][:, (2 * h + t) * P:(2 * h + t + 1) * P],
                                               En[(k - 1) % 8][:, t, 1, h * 128:(h + 1) * 128], ident_sb[0:P, 0:P])
                    ins.then_inc(l1_T, 1)
                if valid(i, k - 2):
                    n, q = 8 * i + k - 2, k % 2
                    pe.wait_ge(l1_M, n + 1)
                    wait_pos(pe, l1_MTc, n)
                    for t in range(2):
                        for h in range(2):
                            ins = pe.transpose(bank[3][0:P, (2 * t + h) * 128:(2 * t + h + 1) * 128],
                                               Mx[q][:, h, t * P:(t + 1) * P], ident_sb[:, :])
                    ins.then_inc(l1_MT, 1)
                if valid(i, k - 5):
                    n, q, b, s = 8 * i + k - 5, (k - 5) % 2, ((k - 5) % 8) // 4, (k - 5) % 4
                    pe.wait_ge(l1_w, n + 1)
                    wait_pos(pe, l1_ac, n)
                    if s == 0:
                        wait_pos(pe, l1_Fc, 2 * i + (k - 5) // 4)
                    for t in range(2):
                        tt = 2 * s + t
                        pe.matmul(bank[6][0:P, b * 128 + tt * C:b * 128 + (tt + 1) * C], Sm[b][:, tt, :], vr[q][:, t, :],
                                  start=True, stop=True)
                        ins = pe.matmul(bank[7][0:2, t * W:(t + 1) * W], Sm[b][:, tt, 0:P:P - 1], wv[q][:, t, :],
                                        start=True, stop=True)
                    ins.then_inc(l1_F, 1)
                if valid(i, k - 2):
                    n, q, b, s = 8 * i + k - 2, k % 2, ((k - 2) % 8) // 4, (k - 2) % 4
                    pe.wait_ge(l1_MTc, n + 1)
                    wait_pos(pe, l1_d, n)
                    if s == 0:
                        pe.wait_ge(l1_L, 2 * i + (k - 2) // 4 + 1)
                    for t in range(2):
                        ins = pe.matmul(bank[4][0:P, t * W:(t + 1) * W], Lm[b][:, 2 * s + t, :], MT[q][:, t, :],
                                        start=True, stop=True)
                    ins.then_inc(l1_B, 1)

            run_slots(pe, slot)
            pe.wait_ge(b_row, 2)
            pe.wait_ge(l1_Fc, NCH)
            for j in range(12):
                m, h, r = j // 4, j // 2 % 2, j % 2
                if j >= 8:
                    pe.wait_ge(b_Tc, j - 7)
                for g in range(4):
                    ins = pe.transpose(bank[j % 8][:, g * EP:(g + 1) * EP],
                                       rows4[(0, 2, 3)[m]][:, 4 * r + g, h * 128:(h + 1) * 128], ident_sb[0:EP, 0:EP])
                ins.then_inc(b_T, 1)
            pe.wait_ge(b_q, 1)
            for g in range(EG):
                for h in range(2):
                    ins = pe.matmul(bank[0][0:EP, g * C:(g + 1) * C], bm_a[:, h, g * EP:(g + 1) * EP], fold_sb[:, :],
                                    start=(h == 0), stop=(h == 1))
            ins.then_inc(b_f, 1)

        @block.scalar
        def _(act):
            def clear(tab, w, zeroed):
                eighth = NP * w // 8
                for k in range(8):
                    act.dma_start(tab.rearrange("(p n) c -> p (n c)", p=P)[:, k * eighth:(k + 1) * eighth],
                                  zero[:, 0:eighth]).then_inc(zeroed, 16)

            act.wait_ge(s_zero, 1)
            act.wait_ge(s_dload, 16 * 8)
            clear(agg_tab, C + 1, s_zeroed)
            act.wait_ge(s_flag, 1)
            act.dma_start(flag_tab.rearrange("(p n) -> p n", p=100), dq).then_inc(s_flagst, 16)
            act.wait_ge(s_wsplit, 1)
            for j, k in enumerate((0, 1, 0, 1, 2, 0)):
                act.dma_start(wstack[j * C:(j + 1) * C, :], wpart[0:C, k, :]).then_inc(s_wstack, 16)
            for k in range(3):
                act.dma_start(wstack[6 * C + k:6 * C + k + 1, :], wpart[C:C + 1, k, :]).then_inc(s_wstack, 16)
            act.wait_ge(s_const, 16 * 28)
            act.wait_ge(s_cols, 1)
            act.wait_ge(s_flagst, 16)

            def chunk(i, b):
                c = 2 * i + b
                act.wait_ge(l0_z, c + 1)
                if not (isinstance(i, int) and i == 0):
                    act.wait_ge(l0_w, 4 * (c - 1))
                z = [bank[2 + k][0:HID, 0:CE // 2] for k in range(2)]
                for k in range(2):
                    ins = nc.scalar.activation(hid[b][0:HID, k * CE // 2:(k + 1) * CE // 2], z[k], ACT.Silu,
                                               bias=b1_sb[:, 0:1])
                ins.then_inc(l0_h, 1)
                act.wait_ge(l0_ht, c + 1)
                if not (isinstance(i, int) and i == 0 and b == 0):
                    act.wait_ge(l0_root, c)
                nc.scalar.activation(hT, bank[4][:, 0:256].rearrange("p (g e) -> p g e", g=2)[:, :, 0:P],
                                     ACT.Copy).then_inc(l0_htc, 1)
                act.wait_ge(l0_root, c + 1)
                nc.scalar.activation(rr[:, bass.ds(c * NS * C, NS * C)], bank[5][0:P, 0:NS * C],
                                     ACT.Copy).then_inc(l0_rootc, 1)
                act.wait_ge(l0_seg, c + 1)
                if not (isinstance(i, int) and i == 0):
                    act.wait_ge(l0_put[b], 128 * i)
                nc.scalar.activation(bound0[:, bass.ds(c * 2 * CT, 2 * CT)], bank[7][0:C + 1, 0:2 * CT], ACT.Copy)
                nc.scalar.activation(segs[b].rearrange("p t c -> p (t c)"), bank[6][0:P, 0:CT * (C + 1)],
                                     ACT.Copy).then_inc(l0_segc, 1)
                if b == 1:
                    act.wait_ge(sp_done, i + 1)
                    for j, k in enumerate((0, 0, 1, 1, 0, 2)):
                        act.dma_start(stack_tab[j * C:(j + 1) * C, :].rearrange("c (b n) -> (c b) n", b=8)
                                      [:, bass.ds(i * SPLITC, SPLITC)], spb[:, k, :]).then_inc(sp_out, 16)

            chunk(0, 0)
            chunk(0, 1)
            clear(ft_tab, C, s_zeroed_ft)
            with act.Fori(1, NCH // 2) as i:
                chunk(i, 0)
                chunk(i, 1)
            act.wait_ge(l0_runT, 1)
            nc.scalar.activation(end_seg.rearrange("p g c -> p (g c)"), bank[6][0:EP, 0:EG * (C + 1)],
                                 ACT.Copy).then_inc(l0_runc, 1)

            for k in range(NB):
                act.wait_ge(n_sq, k + 1)
                nc.scalar.activation(nq, nt, ACT.Square).then_inc(n_sqd, 1)
                act.wait_ge(n_z, k + 1)
                if k:
                    act.wait_ge(n_x1, k)
                nc.scalar.activation(ns[0], nz[k % 2], ACT.Silu).then_inc(n_silu, 1)
                if k:
                    act.dma_start(x1_tab.rearrange("(p n) c -> p (n c)", p=P)[:, (k - 1) * NN * C:k * NN * C],
                                  hb[:, (k - 1) * NN * C:k * NN * C]).then_inc(n_out, 16)
            act.wait_ge(n_x1, NB)
            act.dma_start(x1_tab.rearrange("(p n) c -> p (n c)", p=P)[:, (NB - 1) * NN * C:],
                          hb[:, (NB - 1) * NN * C:]).then_inc(n_out, 16)
            if part == 1:
                act.dma_start(out.rearrange("(p n) c -> p (n c)", p=P), hb[:, :]).then_inc(n_out, 16)
                act.wait_ge(n_out, 16 * (NB + 1))

            if part == 1:
                return

            act.preload_act_table_set("natural_log_exp_and_others")

            def slot(i, k):
                if k == 0:
                    act.preload_act_table_set("natural_log_exp_and_others")
                if valid(i, k - 4):
                    n, q = 8 * i + k - 4, k % 2
                    act.wait_ge(l1_D, n + 1)
                    wait_pos(act, l1_rowl[q], 8 * (n - k % 2))
                    wait_pos(act, l1_w, n - 1)
                    nc.scalar.activation(lnd[q], both(bank[5][0:P, :]), ACT.Ln).then_inc(l1_ln, 1)
                    act.wait_ge(l1_ln, n + 1)
                    nc.scalar.activation(Rd[q], lnd[q], ACT.Exp, scale=-1.0).then_inc(l1_R, 1)
                if valid(i, k - 2):
                    n, q = 8 * i + k - 2, k % 2
                    act.wait_ge(l1_MT, n + 1)
                    wait_pos(act, l1_B, n - 1)
                    nc.scalar.activation(MT[q], both(bank[3][0:P, :]), ACT.Copy).then_inc(l1_MTc, 1)
                if k % 4 == 1 and valid(i, k - 1):
                    b, c = (k % 8) // 4, 2 * i + k // 4
                    act.wait_ge(l1_S, c + 1)
                    wait_pos(act, l1_B, 4 * (c - 1))
                    for t in range(CT):
                        ins = nc.scalar.activation(Lm[b][:, t, :], Sm[b][:, t, :], ACT.Copy,
                                                   scale=dc1[b][:, 1, t:t + 1])
                    ins.then_inc(l1_L, 1)
                if valid(i, k - 5):
                    n, q = 8 * i + k - 5, (k - 5) % 2
                    act.wait_ge(l1_F, n + 1)
                    wait_pos(act, l1_rowa[q], 8 * (n - (k - 5) % 2))
                    nc.scalar.activation(arow[q], bank[7][0:2, :], ACT.Copy).then_inc(l1_ac, 1)
                    if (k - 5) % 4 == 3:
                        b, c = ((k - 5) % 8) // 4, 2 * i + (k - 5) // 4
                        wait_pos(act, l1_put[b], 128 * (i + (k - 5) // 8))
                        nc.scalar.activation(fts[b].rearrange("p t c -> p (t c)"), bank[6][0:P, b * 128:(b + 1) * 128],
                                             ACT.Copy).then_inc(l1_Fc, 1)
                if valid(i, k - 2):
                    n, q = 8 * i + k - 2, k % 2
                    act.wait_ge(l1_d, n + 1)
                    wait_pos(act, l1_w, n - 1)
                    nc.scalar.activation(ex[q], dd[q], ACT.Exp).then_inc(l1_ex, 1)

            run_slots(act, slot)
            act.wait_ge(b_in, 64)
            nc.scalar.activation(rows4[2], rows4[2], ACT.Exp).then_inc(b_row, 1)
            for j in range(12):
                m, h, r = j // 4, j // 2 % 2, j % 2
                act.wait_ge(b_T, j + 1)
                nc.scalar.activation(bound1[:, m, h, r * 4 * EP:(r + 1) * 4 * EP], bank[j % 8][:, 0:4 * EP],
                                     ACT.Copy).then_inc(b_Tc, 1)
            act.wait_ge(b_d, 1)
            nc.scalar.activation(bm_c[:, :, :], bm_c[:, :, :], ACT.Exp).then_inc(b_x, 1)
            nc.scalar.activation(bm_w[:, :, :], bm_w[:, :, :], ACT.Exp).then_inc(b_x, 1)
            act.wait_ge(b_f, 1)
            nc.scalar.activation(end_ft.rearrange("p g c -> p (g c)"), bank[0][0:EP, 0:EG * C],
                                 ACT.Copy).then_inc(b_fc, 1)

        @block.vector
        def _(dve):
            ch = Chain(s_dve)
            V = nc.vector

            def link(ins):
                ins.then_inc(s_dve, 1)
                dve.wait_ge(s_dve, ch.next())

            def rstd(y, v, t, total):
                link(V.tensor_scalar(v, total, 1.0 / C, EPS, ALU.mult, ALU.add))
                link(V.tensor_scalar(y.bitcast(I32), v.bitcast(I32), -0.5, 1597463007.0, ALU.mult, ALU.add))
                for _ in range(3):
                    link(V.scalar_tensor_tensor(t, y, -0.5, v, ALU.mult, ALU.mult))
                    link(V.tensor_tensor(t, t, y, ALU.mult))
                    link(V.scalar_tensor_tensor(y, t, 1.5, y, ALU.add, ALU.mult))

            def wide(a, rows):
                return a.rearrange("p (n a) -> p n a", a=1).broadcast_to([P, rows, C])

            V.memset(d_next, -1).then_inc(s_pad, 1)
            for b in range(2):
                V.memset(hid[b][HID:HID + 1, :], 1.0)
                V.memset(msg[b][:, :, C:C + 1], 1.0)
            V.memset(ones_row[:, :], 1.0).then_inc(s_ones, 1)
            dve.wait_ge(s_dload, 16 * 8)
            link(V.tensor_copy(c1, d_i))
            link(V.tensor_copy(col_f[:, :, 0, :], c1.rearrange("p (c t) -> p c t", t=CT)))
            link(V.tensor_tensor(c2, d_i, d_next, ALU.not_equal))
            link(V.tensor_copy(col_f[:, :, 1, :], c2.rearrange("p (c t) -> p c t", t=CT)))
            V.tensor_tensor(c3, d_i, d_first, ALU.not_equal)
            link(V.tensor_tensor(c4, d_i, d_last, ALU.not_equal))
            link(V.tensor_tensor(c3, c3, c4, ALU.mult))
            link(V.tensor_tensor(c3, c3, c2, ALU.mult))
            link(V.scalar_tensor_tensor(c4, c1, -SKIP, c3, ALU.add, ALU.mult))
            link(V.tensor_scalar(col_i.rearrange("p c t -> p (c t)"), c4, SKIP, None, ALU.add))
            V.memset(same_e[:, 0:1], 0.0)
            V.memset(live_e[:, :], 1.0)
            link(V.tensor_tensor(same_e[:, 1:], e_b[:, 1:], e_b[:, :-1], ALU.is_equal))
            pairs = same_e[:, :].rearrange("p (t q) -> p t q", q=2)
            link(V.tensor_scalar(live_e[:, :].rearrange("p (t q) -> p t q", q=2)[:, :, 1:2], pairs[:, :, 1:2],
                                 -1.0, 1.0, ALU.mult, ALU.add))
            link(V.tensor_tensor(e_1, e_c, e_n, ALU.not_equal))
            link(V.tensor_copy(e_2, e_c))
            link(V.scalar_tensor_tensor(e_2, e_2, -SKIP, e_1, ALU.add, ALU.mult))
            link(V.tensor_scalar(idx_e[:, :], e_2, SKIP, None, ALU.add))
            V.memset(dq.rearrange("p (t e) -> p t e", e=P)[:, :, 0:1], 0.0)
            d3 = dn.rearrange("p (t e) -> p t e", e=P)
            link(V.tensor_tensor(dq.rearrange("p (t e) -> p t e", e=P)[:, :, 1:], d3[:, :, 1:], d3[:, :, :-1],
                                 ALU.is_equal))
            link(V.tensor_scalar(dq, dq, 2.0, -1.0, ALU.mult, ALU.add))
            V.tensor_scalar(dq, dq, BIG, None, ALU.mult).then_inc(s_flag, 1)
            dve.wait_ge(s_const, 16 * 28)
            link(V.tensor_copy(wpart[:, 0, :], wf_sb[:, :]))
            link(V.tensor_tensor(wres[:, :], wf_sb[:, :], wpart[:, 0, :], ALU.subtract))
            link(V.tensor_copy(wpart[:, 1, :], wres[:, :]))
            link(V.tensor_tensor(wres[:, :], wres[:, :], wpart[:, 1, :], ALU.subtract))
            V.tensor_copy(wpart[:, 2, :], wres[:, :]).then_inc(s_wsplit, 1)
            V.memset(sc0[0], 0).then_inc(s_cols, 1)

            R = CT + NS

            def layernorm(xi, b_c):
                tot, v, y, t = (st[:, k, :] for k in range(4))
                link(V.tensor_reduce(tot, xi, X, ALU.add))
                link(V.tensor_scalar(tot, tot, -1.0 / C, None, ALU.mult))
                link(V.tensor_tensor(xi, xi, wide(tot, R), ALU.add))
                link(V.tensor_tensor(sq, xi, xi, ALU.mult))
                link(V.tensor_reduce(tot, sq, X, ALU.add))
                rstd(y, v, t, tot)
                link(V.tensor_tensor(sq, xi, wide(y, R), ALU.mult))

            def chunk(i, b):
                c = 2 * i + b
                dve.wait_ge(l0_got[b], 128 * (i + 1))
                dve.wait_ge(l0_in[b], 64 * (i + 1))
                layernorm(xin[b], c)
                if not (isinstance(i, int) and i == 0 and b == 0):
                    dve.wait_ge(l0_ht, c)
                ins = V.tensor_scalar(hx, sq, 0.0, None, ALU.max)
                ins.then_inc(l0_hx, 1)
                dve.wait_ge(l0_hx, c + 1)
                V.tensor_tensor(hb[:, bass.ds(c * NS * C, NS * C)].rearrange("p (n c) -> p n c", c=C), hx[:, CT:, :],
                                lnb_sb[:, :].rearrange("p (a c) -> p a c", a=1).broadcast_to([P, NS, C]), ALU.add)
                link(V.tensor_copy(dc0, col_f[:, bass.ds(c, 1), 0, :].rearrange("p a t -> p (a t)")))
                if not (isinstance(i, int) and i == 0):
                    dve.wait_ge(l0_seg, c - 1)
                V.tensor_tensor(S0[b], dstb[b].rearrange("p (t e) -> p t e", e=P),
                                dc0.rearrange("p (t a) -> p t a", a=1).broadcast_to([P, CT, P]), ALU.is_equal)
                for s in range(4):
                    dve.wait_ge(l0_w, 4 * c + s + 1)
                    V.tensor_tensor(prod[s % 2].rearrange("p (r o) -> p r o", o=C),
                                    bank[s % 2][0:P, :].rearrange("p (r o) -> p r o", o=C),
                                    hx[:, 2 * s:2 * s + 2, :].rearrange("p t (c a) -> p (t c) a", a=1)
                                    .broadcast_to([P, 2 * C, C]), ALU.mult).then_inc(l0_prod, 1)
                    dve.wait_ge(l0_prod, 4 * c + s + 1)
                    ins = V.tensor_reduce(msg[b][:, 2 * s:2 * s + 2, 0:C],
                                          prod[s % 2].rearrange("p (t i o) -> p t o i", t=2, i=C), X, ALU.add)
                ins.then_inc(l0_msg, 1)
                if not (isinstance(i, int) and i == 0):
                    dve.wait_ge(l0_put[b], 128 * i)
                V.tensor_copy(sc0[b], col_i[:, bass.ds(c, 1), :].rearrange("p a t -> p (a t)")).then_inc(l0_sc, 1)
                if b == 1:
                    dve.wait_ge(sp_in, 16 * (i + 1))
                    if not (isinstance(i, int) and i == 0):
                        dve.wait_ge(sp_out, 96 * i)
                    link(V.tensor_copy(spb[:, 0, :], spx))
                    link(V.tensor_tensor(spr, spx, spb[:, 0, :], ALU.subtract))
                    link(V.tensor_copy(spb[:, 1, :], spr))
                    link(V.tensor_tensor(spr, spr, spb[:, 1, :], ALU.subtract))
                    V.tensor_copy(spb[:, 2, :], spr).then_inc(sp_done, 1)

            before = ch.count
            chunk(0, 0)
            chunk(0, 1)
            per = ch.count - before
            with dve.Fori(1, NCH // 2) as i:
                ch.enter(i, 1, per)
                chunk(i, 0)
                chunk(i, 1)
            ch.leave(NCH // 2 - 1)
            dve.wait_ge(l0_segc, NCH)
            link(V.tensor_tensor(bound0[:, :], bound0[:, :], live_e[0:C + 1, :], ALU.mult))
            V.tensor_tensor_scan(bound0[:, :], same_e[0:C + 1, :], bound0[:, :], 0.0, ALU.mult, ALU.add
                                 ).then_inc(l0_run, 1)

            for k in range(NB):
                a, z = ag[k % 2], nz[k % 2]
                tot, v, y, t, cnt, rc = (nst[:, j, :] for j in range(6))
                dve.wait_ge(n_in[k % 2], 32 * (k // 2 + 1))
                link(V.tensor_scalar(cnt, a[:, :, C:C + 1].rearrange("p n a -> p (n a)"), 1.0, None, ALU.max))
                link(V.reciprocal(rc, cnt))
                link(V.tensor_tensor(nt, a[:, :, 0:C], wide(rc, NN), ALU.mult))
                link(V.tensor_tensor(nt, nt, rr[:, k * NN * C:(k + 1) * NN * C].rearrange("p (n c) -> p n c", c=C),
                                     ALU.add))
                link(V.tensor_reduce(tot, nt, X, ALU.add))
                link(V.tensor_scalar(tot, tot, -1.0 / C, None, ALU.mult))
                V.tensor_tensor(nt, nt, wide(tot, NN), ALU.add).then_inc(n_sq, 1)
                dve.wait_ge(n_sqd, k + 1)
                link(V.tensor_reduce(tot, nq, X, ALU.add))
                rstd(y, v, t, tot)
                link(V.tensor_tensor(nt, nt, wide(y, NN), ALU.mult))
                link(V.tensor_tensor(nt, nt, lnw_sb[:, :].rearrange("p (a c) -> p a c", a=1)
                                     .broadcast_to([P, NN, C]), ALU.mult))
                if k >= 2:
                    dve.wait_ge(n_silu, k - 1)
                V.tensor_tensor(z, nt, hb[:, k * NN * C:(k + 1) * NN * C].rearrange("p (n c) -> p n c", c=C),
                                ALU.add).then_inc(n_z, 1)
                dve.wait_ge(n_z, k + 1)

            if part == 1:
                return

            dve.wait_ge(n_x1, NB)
            for b in range(2):
                ins = V.memset(stk[b][6 * C:6 * C + 3, :], 1.0)
            ins.then_inc(l1_ones, 1)

            def prelude(i, b):
                c = 2 * i + b
                xi = rows1[b]
                dve.wait_ge(l1_got[b], 128 * (i + 1))
                tot, v, y, t = (st1[:, j, :] for j in range(4))
                link(V.tensor_reduce(tot, xi, X, ALU.add))
                link(V.tensor_scalar(tot, tot, -1.0 / C, None, ALU.mult))
                link(V.tensor_tensor(xi, xi, wide(tot, CT), ALU.add))
                link(V.tensor_tensor(sq1, xi, xi, ALU.mult))
                link(V.tensor_reduce(tot, sq1, X, ALU.add))
                rstd(y, v, t, tot)
                link(V.tensor_tensor(sq1, xi, wide(y, CT), ALU.mult))
                wait_pos(dve, l1_L, c - 1)
                V.tensor_scalar(h1[b], sq1, 0.0, None, ALU.max).then_inc(l1_pre, 1)
                link(V.tensor_copy(dc1[b], col_f[:, bass.ds(c, 1), :, :].rearrange("p a k t -> p (a k) t")))

            def same_segment(i, b):
                c = 2 * i + b
                wait_pos(dve, l1_F, 4 * (c - 1))
                V.tensor_tensor(Sm[b], dsb[b].rearrange("p (t e) -> p t e", e=P),
                                dc1[b][:, 0, :].rearrange("p (t a) -> p t a", a=1).broadcast_to([P, CT, P]),
                                ALU.is_equal).then_inc(l1_S, 1)

            def slot(i, k):
                if valid(i, k) and k % 4 == 0:
                    prelude(i, k // 4)
                if valid(i, k):
                    n, b, s = 8 * i + k, k // 4, k % 4
                    wait_pos(dve, l1_rowd[k % 2], 16 * (n - 6 - k % 2))
                    for t in range(2):
                        dve.wait_ge(l1_A, 2 * n + t + 1)
                        V.tensor_tensor(En[k % 8][:, t, :, :].rearrange("p m (i o) -> p m i o", o=C),
                                        bank[t][0:P, :].rearrange("p (m i o) -> p m i o", m=2, o=C),
                                        h1[b][:, 2 * s + t, :].rearrange("p (m i o) -> p m i o", m=1, o=1)
                                        .broadcast_to([P, 2, C, C]), ALU.mult).then_inc(l1_e, 1)
                if valid(i, k) and k % 4 == 1:
                    same_segment(i, k // 4)
                if k % 4 == 1 and valid(i, k - 9):
                    c, b = 2 * i + (k - 9) // 4, ((k - 9) % 8) // 4
                    wait_pos(dve, l1_put[b], 128 * (i + (k - 9) // 8))
                    V.tensor_copy(sc1[b], col_i[:, bass.ds(c, 1), :].rearrange("p a t -> p (a t)")).then_inc(l1_sc, 1)
                if valid(i, k - 1):
                    n, b, s, q = 8 * i + k - 1, ((k - 1) % 8) // 4, (k - 1) % 4, (k - 1) % 2
                    dve.wait_ge(l1_T, n + 1)
                    wait_pos(dve, l1_MT, n - 1)
                    for h in range(2):
                        ins = V.tensor_tensor_scan(Mx[q][:, h, :], flg[b][:, 2 * s * P:(2 * s + 2) * P],
                                                   bank[2][:, h * 2 * P:(h + 1) * 2 * P], 0.0, ALU.min, ALU.max)
                    ins.then_inc(l1_M, 1)
                if valid(i, k - 4):
                    n, q = 8 * i + k - 4, k % 2
                    dve.wait_ge(l1_R, n + 1)
                    wait_pos(dve, l1_F, n - 1)
                    link(V.tensor_tensor(at, ex[q], Rd[q], ALU.mult))
                    link(V.tensor_tensor(wv[q], at, En[(k - 4) % 8][:, :, 0, :], ALU.mult))
                    V.tensor_reduce(vr[q], wv[q].rearrange("p t (i o) -> p t o i", i=C), X, ALU.add).then_inc(l1_w, 1)
                if valid(i, k - 2):
                    n, q = 8 * i + k - 2, k % 2
                    dve.wait_ge(l1_B, n + 1)
                    wait_pos(dve, l1_ex, n - 1)
                    wait_pos(dve, l1_rowd[q], 16 * (n - k % 2))
                    V.tensor_tensor(dd[q], En[(k - 2) % 8][:, :, 1, :], both(bank[4][0:P, :]),
                                    ALU.subtract).then_inc(l1_d, 1)

            run_slots(dve, slot, ch, LINKS1)

            dve.wait_ge(b_in, 64)
            V.tensor_tensor(rows4[0], rows4[0], rows4[1], ALU.subtract).then_inc(b_row, 1)
            dve.wait_ge(b_Tc, 12)
            dve.wait_ge(l1_Fc, NCH)
            V.tensor_scalar(bm_nf, live_e[:, :], 2.0, -1.0, ALU.mult, ALU.add)
            link(V.tensor_scalar(bm_sf, same_e[:, :], 2.0, -1.0, ALU.mult, ALU.add))
            V.tensor_scalar(bm_nf, bm_nf, BIG, None, ALU.mult)
            V.memset(bm_c[:, :, 0:1], 0.0)
            link(V.tensor_scalar(bm_sf, bm_sf, BIG, None, ALU.mult))
            for h in range(2):
                link(V.tensor_tensor(bm_m[:, h, :], bound1[:, 0, h, :], bm_nf, ALU.min))
                link(V.tensor_tensor_scan(bm_x[:, h, :], bm_sf, bm_m[:, h, :], 0.0, ALU.min, ALU.max))
                link(V.tensor_tensor(bm_c[:, h, 1:], bm_x[:, h, :-1], bm_x[:, h, 1:], ALU.subtract))
                link(V.tensor_scalar(bm_c[:, h, :], bm_c[:, h, :], 0.0, None, ALU.min))
                ins = V.tensor_tensor(bm_w[:, h, :], bm_m[:, h, :], bm_x[:, h, :], ALU.subtract)
            ins.then_inc(b_d, 1)
            dve.wait_ge(b_x, 2)
            for h in range(2):
                link(V.tensor_tensor(bm_c[:, h, :], bm_c[:, h, :], same_e[:, :], ALU.mult))
                link(V.tensor_tensor(bm_w[:, h, :], bm_w[:, h, :], bound1[:, 1, h, :], ALU.mult))
                link(V.tensor_tensor(bm_a[:, h, :], bm_w[:, h, :], bound1[:, 2, h, :], ALU.mult))
                link(V.tensor_tensor_scan(bm_x[:, h, :], bm_c[:, h, :], bm_w[:, h, :], 0.0, ALU.mult, ALU.add))
                link(V.tensor_tensor_scan(bm_m[:, h, :], bm_c[:, h, :], bm_a[:, h, :], 0.0, ALU.mult, ALU.add))
                link(V.reciprocal(bm_r[:, h, :], bm_x[:, h, :]))
                ins = V.tensor_tensor(bm_a[:, h, :], bm_m[:, h, :], bm_r[:, h, :], ALU.mult)
            ins.then_inc(b_q, 1)
            for k in range(NB):
                dve.wait_ge(f_in[k % 3], 16 * (k // 3 + 1))
                V.tensor_tensor(fin[k % 3], fin[k % 3], hb[:, k * NN * C:(k + 1) * NN * C], ALU.add).then_inc(f_sum, 1)


_OUTS = [((N, C), 'float32')]
PART = 2


def kernel(**inputs):
    import numpy as _np
    import concourse.bacc as _bacc
    from concourse import mybir as _mybir
    from concourse.bass_utils import run_bass_kernel_spmd as _run

    nc = _bacc.Bacc("TRN2", target_bir_lowering=False, num_devices=1)
    a = {k: _np.asarray(v) for k, v in inputs.items()}
    dst_tiles = a["dst"].reshape(T, P)
    ends = _np.concatenate([dst_tiles[:, [0, P - 1]].reshape(-1), _np.full(1, -1, a["dst"].dtype)])
    sent = {
        "x": a["x"], "src_cols": a["src"].reshape(T, P).T, "dst": a["dst"], "dst_cols": dst_tiles.T,
        "ends": ends,
        "end_cols": _np.concatenate([ends[:-1].reshape(EG, EP).T, ends[1:].reshape(EG, EP).T]),
        "ea16T": a["edge_attr_16"].T, "ea8T": a["edge_attr_8"].T,
        "W1": a["L0_gnn_W1"], "b1": a["L0_gnn_b1"], "W2": a["L0_gnn_W2"], "b2": a["L0_gnn_b2"],
        "root": a["L0_gnn_root"], "bias": a["L0_gnn_bias"], "ln_w": a["L0_gnn_ln_w"], "ln_b": a["L0_gnn_ln_b"],
        "Wm": a["L1_gnn_W_msg"], "bm": a["L1_gnn_b_msg"], "Wa": a["L1_gnn_W_attn"], "ba": a["L1_gnn_b_attn"],
        "ident": _np.eye(128, dtype=_np.float32),
        "fold": _np.tile(_np.eye(C, dtype=_np.float32), (8, 1)),
    }
    arrays, args = {}, []
    for name, value in sent.items():
        value = _np.ascontiguousarray(value)
        arrays[f"in_{name}_dram"] = value
        args.append(nc.dram_tensor(f"in_{name}_dram", value.shape, _mybir.dt.from_np(value.dtype),
                                   kind="ExternalInput").ap())
    for i, (shape, dtype) in enumerate(_OUTS):
        args.append(nc.dram_tensor(f"out_{i}_dram", shape, _mybir.dt.from_np(_np.dtype(dtype)),
                                   kind="ExternalOutput").ap())
    gnn_kernel(nc, *args, part=PART)
    r = _run(nc, [arrays], core_ids=[0])
    return r.results[0]["out_0_dram"]
```

```python
from contextlib import ExitStack

import concourse.bass as bass
from concourse import mybir

F32 = mybir.dt.float32
I32 = mybir.dt.int32
BF16 = mybir.dt.bfloat16
ALU = mybir.AluOpType
ACT = mybir.ActivationFunctionType
X = mybir.AxisListType.X

N = 100000
E = 50000
C = 16
P = 125
T = E // P
CT = 8
CE = CT * P
NCH = T // CT
NP = N // P
NS = NP // NCH
W = C * C
HID = 64
K8 = 8
ENDS = 2 * T
EP = 100
EG = ENDS // EP
SPLITC = E // 8 // (NCH // 2)
NB = 10
NN = NP // NB
EPS = 1e-5
SKIP = float(1 << 20)
BIG = 3.0e38
LINKS1 = 12
DVE_SUB = (2,)
STEPS = NCH * 4


class Chain:

    def __init__(self, sem):
        self.sem, self.count, self.loop = sem, 0, None

    def next(self):
        self.count += 1
        return self.now()

    def now(self):
        if self.loop is None:
            return self.count
        i, first, per = self.loop
        return i * per + (self.count - first * per)

    def enter(self, i, first, per):
        self.loop = (i, first, per)
        self.start = self.count

    def leave(self, times):
        per = self.loop[2]
        assert self.count - self.start == per, (self.count, self.start, per)
        self.count = self.start + times * per
        self.loop = None


def gnn_kernel(nc, x, src_cols, dst, dst_cols, ends, end_cols, ea16T, ea8T, W1, b1, W2, b2, root, bias, ln_w, ln_b,
               Wm, bm, Wa, ba, ident, fold, out):
    agg_tab = nc.dram_tensor("agg_tab", [N, C + 1], F32, kind="Internal").ap()
    ft_tab = nc.dram_tensor("ft_tab", [N, C], F32, kind="Internal").ap()
    x1_tab = nc.dram_tensor("x1_tab", [N, C], F32, kind="Internal").ap()
    stack_tab = nc.dram_tensor("stack_tab", [6 * C, E], BF16, kind="Internal").ap()
    flag_tab = nc.dram_tensor("flag_tab", [E], F32, kind="Internal").ap()
    row_tab = nc.dram_tensor("row_tab", [4, T, 2, W], F32, kind="Internal").ap()

    with ExitStack() as ctx:
        def sb(name, shape, dt=F32):
            return ctx.enter_context(nc.sbuf_tensor(name, shape, dt))

        def sem(name):
            return ctx.enter_context(nc.semaphore(name))

        def sem2(name):
            return [sem(f"{name}_even"), sem(f"{name}_odd")]

        hb = sb("hb", [P, NP * C])
        ident_sb = sb("ident_sb", [128, 128])
        fold_sb = sb("fold_sb", [128, C])
        w1_sb = sb("w1_sb", [K8, HID])
        b1_sb = sb("b1_sb", [HID, 1])
        w2_sb = sb("w2_sb", [HID + 1, W])
        root_sb = sb("root_sb", [128, 128])
        bias_row = sb("bias_row", [1, 128])
        ones_row = sb("ones_row", [1, P])
        lnw_sb = sb("lnw_sb", [P, C])
        lnb_sb = sb("lnb_sb", [P, C])
        wf_sb = sb("wf_sb", [C + 1, 2 * W])
        wres = sb("wres", [C + 1, 2 * W])
        wpart = sb("wpart", [C + 1, 3, 2 * W], BF16)
        wstack = sb("wstack", [6 * C + 3, 2 * W], BF16)
        col_f = sb("col_f", [P, NCH, 2, CT])
        col_i = sb("col_i", [P, NCH, CT], I32)
        same_e = sb("same_e", [128, ENDS])
        live_e = sb("live_e", [128, ENDS])
        idx_e = sb("idx_e", [EP, EG], I32)
        idx_x = sb("idx_x", [EP, EG], I32)
        bound0 = sb("bound0", [C + 1, ENDS])

        ARENA = 27400
        arena = sb("arena", [128, ARENA])
        place = [0]

        def carve(rows, cols, dt=F32):
            words = cols if dt != BF16 else cols // 2
            a = arena[0:rows, place[0]:place[0] + words]
            place[0] += words
            assert place[0] <= ARENA, place[0]
            return a if dt == F32 else a.bitcast(dt)

        rr = carve(P, NP * C)
        base = place[0]
        xin = [carve(P, (CT + NS) * C).rearrange("p (t c) -> p t c", c=C) for _ in range(2)]
        hx = carve(P, (CT + NS) * C).rearrange("p (t c) -> p t c", c=C)
        sq = carve(P, (CT + NS) * C).rearrange("p (t c) -> p t c", c=C)
        st = carve(P, 4 * (CT + NS)).rearrange("p (k t) -> p k t", k=4)
        src0 = [carve(P, CT, I32) for _ in range(2)]
        ea8 = [carve(K8, CE) for _ in range(2)]
        dstb = [carve(P, CE, I32) for _ in range(2)]
        hid = [carve(HID + 1, CE) for _ in range(2)]
        S0 = [carve(P, CT * P).rearrange("p (t e) -> p t e", t=CT) for _ in range(2)]
        prod = [carve(P, 2 * W) for _ in range(2)]
        msg = [carve(P, CT * (C + 1)).rearrange("p (t c) -> p t c", t=CT) for _ in range(2)]
        segs = [carve(P, CT * (C + 1)).rearrange("p (t c) -> p t c", t=CT) for _ in range(2)]
        sc0 = [carve(P, CT, I32) for _ in range(2)]
        dc0 = carve(P, CT)
        hT = carve(128, 2 * P).rearrange("p (g e) -> p g e", g=2)
        spx = carve(128, SPLITC)
        spr = carve(128, SPLITC)
        spb = carve(128, 3 * SPLITC, BF16).rearrange("p (k n) -> p k n", k=3)
        end_seg = carve(EP, EG * (C + 1)).rearrange("p (g c) -> p g c", g=EG)
        cen = carve(128, C)
        top0 = place[0]
        place[0] = 0
        d_i = carve(P, T, I32)
        d_next = carve(P, T, I32)
        d_first = carve(P, T, I32)
        d_last = carve(P, T, I32)
        c1, c2, c3, c4 = (carve(P, T) for _ in range(4))
        dn = carve(100, 500, I32)
        dq = carve(100, 500)
        e_b = carve(128, ENDS, I32)
        e_c = carve(EP, EG, I32)
        e_n = carve(EP, EG, I32)
        e_1 = carve(EP, EG)
        e_2 = carve(EP, EG)
        assert place[0] <= base
        place[0] = top0
        zero = carve(P, NP * (C + 1) // 8)
        place[0] = base
        ag = [carve(P, NN * (C + 1)).rearrange("p (n c) -> p n c", n=NN) for _ in range(2)]
        xn = [carve(P, NN * C).rearrange("p (n c) -> p n c", n=NN) for _ in range(2)]
        nt = [carve(P, NN * C).rearrange("p (n c) -> p n c", n=NN) for _ in range(3)]
        nq = carve(P, NN * C).rearrange("p (n c) -> p n c", n=NN)
        ns = [carve(P, NN * C) for _ in range(2)]
        nst = carve(P, 6 * NN).rearrange("p (k n) -> p k n", k=6)

        place[0] = 0
        src1 = [carve(P, CT, I32) for _ in range(2)]
        rows1 = [carve(P, CT * C).rearrange("p (t c) -> p t c", c=C) for _ in range(2)]
        h1 = [carve(P, CT * C).rearrange("p (t c) -> p t c", c=C) for _ in range(2)]
        sq1 = carve(P, CT * C).rearrange("p (t c) -> p t c", c=C)
        st1 = carve(P, 5 * CT).rearrange("p (k t) -> p k t", k=5)
        stk = [carve(6 * C + 3, CE, BF16) for _ in range(2)]
        flg = [carve(128, CE) for _ in range(2)]
        dsb = [carve(P, CE, I32) for _ in range(2)]
        dc1 = [carve(P, 2 * CT).rearrange("p (k t) -> p k t", k=2) for _ in range(2)]
        sc1 = [carve(P, CT, I32) for _ in range(2)]
        base1 = place[0]
        Sm = [carve(P, CT * P).rearrange("p (t e) -> p t e", t=CT) for _ in range(2)]
        Lm = [carve(P, CT * P).rearrange("p (t e) -> p t e", t=CT) for _ in range(2)]
        En = [carve(P, 4 * W).rearrange("p (t m w) -> p t m w", t=2, m=2) for _ in range(8)]
        Mx = [carve(128, 4 * P).rearrange("p (h e) -> p h e", h=2) for _ in range(2)]
        MT = [carve(P, 2 * W).rearrange("p (t w) -> p t w", t=2) for _ in range(2)]
        dd = [carve(P, 2 * W).rearrange("p (t w) -> p t w", t=2) for _ in range(2)]
        ex = [carve(P, 2 * W).rearrange("p (t w) -> p t w", t=2) for _ in range(2)]
        lnd = [carve(P, 2 * W).rearrange("p (t w) -> p t w", t=2) for _ in range(2)]
        Rd = [carve(P, 2 * W).rearrange("p (t w) -> p t w", t=2) for _ in range(2)]
        at = carve(P, 2 * W).rearrange("p (t w) -> p t w", t=2)
        wv = [carve(P, 2 * W).rearrange("p (t w) -> p t w", t=2) for _ in range(2)]
        asum = [carve(P, 2 * W) for _ in range(2)]
        fts = [carve(P, CT * C).rearrange("p (t c) -> p t c", t=CT) for _ in range(2)]
        top1, place[0] = place[0] - 2 * CT * C, base1
        rows4 = [carve(EP, EG * W).rearrange("p (g w) -> p g w", g=EG) for _ in range(4)]
        bound1 = carve(128, 6 * ENDS).rearrange("p (m h e) -> p m h e", m=3, h=2)
        bm_r = carve(128, 2 * ENDS).rearrange("p (h e) -> p h e", h=2)
        bm_nf, bm_sf = (carve(128, ENDS) for _ in range(2))
        end_ft = carve(EP, EG * C).rearrange("p (g c) -> p g c", g=EG)
        end_x1 = carve(EP, EG * C).rearrange("p (g c) -> p g c", g=EG)
        fin = [carve(P, NN * C) for _ in range(3)]
        assert place[0] <= top1, (place[0], top1)
        place[0] = base1
        bm_m, bm_x, bm_c, bm_w, bm_a = (carve(128, 2 * ENDS).rearrange("p (h e) -> p h e", h=2) for _ in range(5))
        assert place[0] <= base1 + 4 * EG * W

        bank = [ctx.enter_context(nc.psum_tensor(f"bank{i}", [128, 512], F32)) for i in range(8)]

        s_const = sem("s_const")
        s_dload = sem("s_dload")
        s_zero = sem("s_zero")
        s_zeroed = sem("s_zeroed")
        s_zeroed_ft = sem("s_zeroed_ft")
        s_flag = sem("s_flag")
        s_flagst = sem("s_flagst")
        s_root0 = sem("s_root0")
        s_ones = sem("s_ones")
        s_pad = sem("s_pad")
        s_wsplit = sem("s_wsplit")
        s_wstack = sem("s_wstack")
        s_dve = sem("s_dve")
        s_act = sem("s_act")
        s_cols = sem("s_cols")
        s_rootl = sem("s_rootl")
        s_rootok = sem("s_rootok")
        s_wf = sem("s_wf")
        l0_x = sem2("l0_x")
        l0_in = sem2("l0_in")
        l0_got = sem2("l0_got")
        l0_z = sem("l0_z")
        l0_h = sem("l0_h")
        l0_w = sem("l0_w")
        l0_prod = sem("l0_prod")
        l0_hx = sem("l0_hx")
        l0_ht = sem("l0_ht")
        l0_htc = sem("l0_htc")
        l0_root = sem("l0_root")
        l0_rootc = sem("l0_rootc")
        l0_msg = sem("l0_msg")
        l0_seg = sem("l0_seg")
        l0_segc = sem("l0_segc")
        l0_sc = sem("l0_sc")
        l0_put = sem2("l0_put")
        l0_gate = sem("l0_gate")
        sp_in = sem("sp_in")
        sp_done = sem("sp_done")
        sp_out = sem("sp_out")
        l0_run = sem("l0_run")
        l0_runT = sem("l0_runT")
        l0_runc = sem("l0_runc")
        l0_end = sem("l0_end")
        n_in = sem2("n_in")
        n_xin = sem2("n_xin")
        n_row = sem("n_row")
        n_sq = sem("n_sq")
        n_y = sem("n_y")
        n_w = sem("n_w")
        n_z = sem("n_z")
        n_silu = sem("n_silu")
        n_x1 = sem("n_x1")
        n_out = sem("n_out")

        l1_in = sem2("l1_in")
        l1_got = sem2("l1_got")
        l1_gate = sem("l1_gate")
        l1_sp = sem("l1_sp")
        l1_ones = sem("l1_ones")
        l1_c = sem("l1_c")
        l1_q = sem("l1_q")
        l1_v = sem("l1_v")
        l1_y = sem("l1_y")
        l1_pre = sem("l1_pre")
        l1_A = sem("l1_A")
        l1_e = sem("l1_e")
        l1_T = sem("l1_T")
        l1_M = sem("l1_M")
        l1_MT = sem("l1_MT")
        l1_MTc = sem("l1_MTc")
        l1_B = sem("l1_B")
        l1_d = sem("l1_d")
        l1_ex = sem("l1_ex")
        l1_D = sem("l1_D")
        l1_ln = sem("l1_ln")
        l1_R = sem("l1_R")
        l1_at = sem("l1_at")
        l1_w = sem("l1_w")
        l1_F = sem("l1_F")
        l1_idx = sem2("l1_idx")
        l1_sc = sem("l1_sc")
        l1_S = sem("l1_S")
        l1_L = sem("l1_L")
        l1_ac = sem("l1_ac")
        l1_rowd = sem2("l1_rowd")
        l1_rowl = sem2("l1_rowl")
        l1_rowa = sem2("l1_rowa")
        b_in = sem("b_in")
        b_row = sem("b_row")
        b_T = sem("b_T")
        b_Tc = sem("b_Tc")
        l1_Fc = sem("l1_Fc")
        l1_put = sem2("l1_put")
        b_d = sem("b_d")
        b_x = sem("b_x")
        b_q = sem("b_q")
        b_f = sem("b_f")
        b_fc = sem("b_fc")
        b_x1 = sem("b_x1")
        b_s = sem("b_s")
        b_ln = sem("b_ln")
        b_r = sem("b_r")
        b_put = sem("b_put")
        f_in = [sem(f"f_in{k}") for k in range(3)]
        f_sum = sem("f_sum")
        f_out = [sem(f"f_out{k}") for k in range(3)]

        def wait_pos(eng, s, value):
            if not (isinstance(value, int) and value <= 0):
                eng.wait_ge(s, value)

        def valid(i, k):
            return not isinstance(i, int) or 0 <= 8 * i + k < STEPS

        def run_slots(eng, slot, chain=None, links=0):
            turns = STEPS // 8
            for k in range(16):
                slot(k // 8, k % 8)
            with eng.Fori(2, turns - 1) as i:
                if chain:
                    chain.enter(i, 2, links)
                for k in range(8):
                    slot(i, k)
            if chain:
                chain.leave(turns - 3)
            for k in range(8):
                slot(turns - 1, k)
            for k in range(6):
                slot(turns, k)

        def both(a):
            return a.rearrange("p (t w) -> p t w", t=2)

        block = ctx.enter_context(nc.Block())

        def bcast_rows(ap, rows, cols):
            return ap.rearrange("(a n) -> a n", a=1).broadcast_to([rows, cols])

        x_part = x.rearrange("(p n) c -> p (n c)", p=P)

        @block.sync
        def _(sp):
            def load(i, b):
                c = 2 * i + b
                if not (isinstance(i, int) and i == 0):
                    sp.wait_ge(l0_hx, c - 1)
                sp.dma_start(src0[b], src_cols[:, bass.ds(c * CT, CT)]).then_inc(l0_x[b], 16)
                sp.dma_start(xin[b][:, CT:, :].rearrange("p t c -> p (t c)"),
                             x_part[:, bass.ds(c * NS * C, NS * C)]).then_inc(l0_x[b], 16)
                if not (isinstance(i, int) and i == 0):
                    sp.wait_ge(l0_msg, c - 1)
                    sp.wait_ge(l0_z, c - 1)
                sp.dma_start(ea8[b], ea8T[:, bass.ds(c * CE, CE)]).then_inc(l0_in[b], 16)
                sp.dma_start(dstb[b], bcast_rows(dst[bass.ds(c * CE, CE)], P, CE)).then_inc(l0_in[b], 16)
                if b == 1:
                    if not (isinstance(i, int) and i == 0):
                        sp.wait_ge(sp_done, i)
                    sp.dma_start(spx, ea16T.rearrange("c (b n) -> (c b) n", b=8)[:, bass.ds(i * SPLITC, SPLITC)]
                                 ).then_inc(sp_in, 16)

            load(0, 0)
            for dst_ap, src_ap in (
                (d_i, dst_cols), (d_first, bcast_rows(dst_cols[0, :], P, T)),
                (d_last, bcast_rows(dst_cols[P - 1, :], P, T)), (dn, dst.rearrange("(p n) -> p n", p=100)),
                (e_b, bcast_rows(ends[0:ENDS], 128, ENDS)), (e_c, end_cols[0:EP, :]),
                (e_n, end_cols[EP:2 * EP, :]),
            ):
                sp.dma_start(dst_ap, src_ap).then_inc(s_dload, 16)
            sp.wait_ge(s_pad, 1)
            sp.dma_start(d_next[0:P - 1, :], dst_cols[1:P, :]).then_inc(s_dload, 16)
            for dst_ap, src_ap in (
                (w1_sb[:, :], W1), (b1_sb[:, :], b1.rearrange("(h a) -> h a", a=1)), (w2_sb[0:HID, :], W2),
                (w2_sb[HID:HID + 1, :], b2.rearrange("(a n) -> a n", a=1)), (lnb_sb[:, :], bcast_rows(ln_b, P, C)),
                (ident_sb[:, :], ident),
            ):
                sp.dma_start(dst_ap, src_ap).then_inc(s_const, 16)
            load(0, 1)

            with sp.Fori(1, NCH // 2) as i:
                load(i, 0)
                load(i, 1)

            sp.wait_ge(l0_put[0], 128 * (NCH // 2))
            sp.wait_ge(l0_put[1], 128 * (NCH // 2))
            sp.wait_ge(l0_end, 16 * EG)
            sp.wait_ge(l0_rootc, NCH)
            sp.wait_ge(sp_out, 96 * (NCH // 2))
            for k in range(NB + 2):
                if k < NB:
                    if k >= 2:
                        sp.wait_ge(n_row, k - 1)
                    sp.dma_start(ag[k % 2].rearrange("p n c -> p (n c)"),
                                 agg_tab.rearrange("(p n) c -> p (n c)", p=P)
                                 [:, k * NN * (C + 1):(k + 1) * NN * (C + 1)]).then_inc(n_in[k % 2], 16)
                if k >= 2:
                    j = k - 2
                    if j >= 2:
                        sp.wait_ge(n_x1, j - 1)
                    sp.dma_start(xn[j % 2].rearrange("p n c -> p (n c)"), x_part[:, j * NN * C:(j + 1) * NN * C]
                                 ).then_inc(n_xin[j % 2], 16)

            sp.wait_ge(n_x1, NB)
            sp.wait_ge(n_out, 16 * NB)

            def load1(i, k):
                c, b = 2 * i + k // 4, (k % 8) // 4
                wait_pos(sp, l1_A, 8 * (c - 1))
                sp.sem_inc(l1_sp, 1)
                wait_pos(sp, l1_M, 4 * (c - 1))
                sp.sem_inc(l1_sp, 1)
                sp.dma_start(stk[b][0:6 * C, :], stack_tab[:, bass.ds(c * CE, CE)]).then_inc(l1_in[b], 16)
                sp.dma_start(flg[b], bcast_rows(flag_tab[bass.ds(c * CE, CE)], 128, CE)).then_inc(l1_in[b], 16)
                sp.dma_start(dsb[b], bcast_rows(dst[bass.ds(c * CE, CE)], P, CE)).then_inc(l1_in[b], 16)

            def load_idx(i, k):
                c, b = 2 * i + k // 4, (k % 8) // 4
                wait_pos(sp, l1_pre, c - 1)
                sp.sem_inc(l1_sp, 1)
                sp.dma_start(src1[b], src_cols[:, bass.ds(c * CT, CT)]).then_inc(l1_idx[b], 16)

            def rows_of(m, i, k):
                return row_tab[m, bass.ds(16 * i + 2 * k, 2), :, :].rearrange("t q w -> q t w")

            def slot(i, k):
                if valid(i, k - 6):
                    n, q = 8 * i + k - 6, k % 2
                    sp.wait_ge(l1_ac, n + 1)
                    sp.sem_inc(l1_sp, 1)
                    sp.dma_start(rows_of(3, i, k - 6), both(asum[q][0:P:P - 1, :])).then_inc(l1_rowa[q], 16)
                if valid(i, k - 4):
                    n, q = 8 * i + k - 4, k % 2
                    sp.wait_ge(l1_ln, n + 1)
                    sp.sem_inc(l1_sp, 1)
                    sp.dma_start(rows_of(2, i, k - 4), lnd[q][0:P:P - 1, :, :]).then_inc(l1_rowl[q], 16)
                if valid(i, k - 2):
                    n, q = 8 * i + k - 2, k % 2
                    sp.wait_ge(l1_d, n + 1)
                    sp.sem_inc(l1_sp, 1)
                    sp.dma_start(rows_of(0, i, k - 2), En[(k - 2) % 8][0:P:P - 1, :, 1, :]).then_inc(l1_rowd[q], 16)
                    sp.dma_start(rows_of(1, i, k - 2), dd[q][0:P:P - 1, :, :]).then_inc(l1_rowd[q], 16)
                if k % 4 == 1 and valid(i, k + 3):
                    load1(i, k + 3)
                if k % 4 == 0 and valid(i, k + 8):
                    load_idx(i, k + 8)

            load_idx(0, 0)
            load_idx(0, 4)
            load1(0, 0)
            run_slots(sp, slot)
            for q in range(2):
                sp.wait_ge(l1_rowd[q], 16 * STEPS)
                sp.wait_ge(l1_rowl[q], 8 * STEPS)
                sp.wait_ge(l1_rowa[q], 8 * STEPS)
            sp.wait_ge(l1_F, STEPS)
            for m in range(4):
                sp.dma_start(rows4[m], row_tab[m, :, :, :].rearrange("t q w -> (t q) w")
                             .rearrange("(g p) w -> p g w", p=EP)).then_inc(b_in, 16)
            sp.wait_ge(l1_put[0], 128 * (NCH // 2))
            sp.wait_ge(l1_put[1], 128 * (NCH // 2))
            for k in range(NB + 2):
                if k < NB:
                    if k >= 3:
                        sp.wait_ge(f_out[k % 3], 16 * (k // 3))
                    sp.dma_start(fin[k % 3], ft_tab.rearrange("(p n) c -> p (n c)", p=P)[:, k * NN * C:(k + 1) * NN * C]
                                 ).then_inc(f_in[k % 3], 16)
                if k >= 2:
                    j = k - 2
                    sp.wait_ge(f_sum, j + 1)
                    sp.dma_start(out.rearrange("(p n) c -> p (n c)", p=P)[:, j * NN * C:(j + 1) * NN * C], fin[j % 3]
                                 ).then_inc(f_out[j % 3], 16)
            sp.wait_ge(b_put, 16 * EG)

        @block.gpsimd
        def _(pool):
            pool.memset(root_sb[:, :], 0.0).then_inc(s_root0, 1)
            pool.memset(zero, 0.0).then_inc(s_zero, 1)

            def gather(i, b):
                pool.wait_ge(l0_x[b], 32 * (i + 1))
                pool.sem_inc(l0_gate, 1)
                for t in range(CT):
                    pool.indirect_dma_start(out=xin[b][:, t, :], out_offset=None, in_=x,
                                            in_offset=bass.IndirectOffsetOnAxis(ap=src0[b][:, t:t + 1], axis=0)
                                            ).then_inc(l0_got[b], 16)

            def scatter(i, b):
                pool.wait_ge(s_zeroed, 128)
                pool.wait_ge(l0_segc, 2 * i + b + 1)
                pool.wait_ge(l0_sc, 2 * i + b + 1)
                pool.sem_inc(l0_gate, 1)
                for t in range(CT):
                    pool.indirect_dma_start(out=agg_tab, out_offset=bass.IndirectOffsetOnAxis(ap=sc0[b][:, t:t + 1], axis=0),
                                            in_=segs[b][:, t, :], in_offset=None,
                                            bounds_check=N - 1, oob_is_err=False).then_inc(l0_put[b], 16)

            gather(0, 0)
            gather(0, 1)
            with pool.Fori(1, NCH // 2) as i:
                gather(i, 0)
                scatter(i - 1, 0)
                gather(i, 1)
                scatter(i - 1, 1)
            scatter(NCH // 2 - 1, 0)
            scatter(NCH // 2 - 1, 1)
            pool.wait_ge(l0_runc, 1)
            for g in range(EG):
                pool.indirect_dma_start(out=agg_tab, out_offset=bass.IndirectOffsetOnAxis(ap=idx_e[:, g:g + 1], axis=0),
                                        in_=end_seg[:, g, :], in_offset=None,
                                        bounds_check=N - 1, oob_is_err=False).then_inc(l0_end, 16)

            def weigh(k):
                r = nt[k % 3]
                pool.wait_ge(n_y, k + 1)
                pool.tensor_tensor(r, r, lnw_sb[:, :].rearrange("p (a c) -> p a c", a=1).broadcast_to([P, NN, C]),
                                   ALU.mult).then_inc(n_w, 1)
                pool.wait_ge(n_w, k + 1)
                pool.tensor_tensor(r, r, hb[:, k * NN * C:(k + 1) * NN * C].rearrange("p (n c) -> p n c", c=C),
                                   ALU.add).then_inc(n_z, 1)

            def residual(k):
                pool.wait_ge(n_silu, k + 1)
                pool.wait_ge(n_xin[k % 2], 16 * (k // 2 + 1))
                pool.tensor_tensor(hb[:, k * NN * C:(k + 1) * NN * C], ns[k % 2],
                                   xn[k % 2].rearrange("p n c -> p (n c)"), ALU.add).then_inc(n_x1, 1)

            for k in range(NB):
                weigh(k)
                if k:
                    residual(k - 1)
            residual(NB - 1)

            pool.wait_ge(s_zeroed_ft, 128)
            pool.wait_ge(n_out, 16 * NB)

            def gather1(i, d):
                b = d % 2
                pool.wait_ge(l1_idx[b], 16 * (i + d // 2 + 1))
                wait_pos(pool, l1_pre, 2 * i + d - 1)
                pool.sem_inc(l1_gate, 1)
                for t in range(CT):
                    pool.indirect_dma_start(out=rows1[b][:, t, :], out_offset=None, in_=x1_tab,
                                            in_offset=bass.IndirectOffsetOnAxis(ap=src1[b][:, t:t + 1], axis=0)
                                            ).then_inc(l1_got[b], 16)

            def scatter1(i, d):
                b = d % 2
                pool.wait_ge(l1_Fc, 8 * i + 4 * d + 4)
                pool.wait_ge(l1_sc, 2 * i + d + 1)
                pool.sem_inc(l1_gate, 1)
                for t in range(CT):
                    pool.indirect_dma_start(out=ft_tab, out_offset=bass.IndirectOffsetOnAxis(ap=sc1[b][:, t:t + 1], axis=0),
                                            in_=fts[b][:, t, :], in_offset=None,
                                            bounds_check=N - 1, oob_is_err=False).then_inc(l1_put[b], 16)

            for c in range(4):
                gather1(0, c)
            with pool.Fori(1, NCH // 2 - 1) as i:
                gather1(i, 2)
                scatter1(i, -2)
                gather1(i, 3)
                scatter1(i, -1)
            for c in range(NCH - 4, NCH):
                scatter1(0, c)
            pool.wait_ge(l1_F, STEPS)
            for q in range(2):
                pool.wait_ge(l1_rowd[q], 16 * STEPS)
                pool.wait_ge(l1_rowl[q], 8 * STEPS)
                pool.wait_ge(l1_rowa[q], 8 * STEPS)
            for g in range(EG):
                pool.indirect_dma_start(out=end_x1[:, g, :], out_offset=None, in_=x1_tab,
                                        in_offset=bass.IndirectOffsetOnAxis(ap=idx_x[:, g:g + 1], axis=0)
                                        ).then_inc(b_x1, 16)
            for k in range(NB):
                pool.wait_ge(f_in[k % 3], 16 * (k // 3 + 1))
                pool.tensor_tensor(fin[k % 3], fin[k % 3], hb[:, k * NN * C:(k + 1) * NN * C], ALU.add
                                   ).then_inc(f_sum, 1)
            for k in range(3):
                pool.wait_ge(f_out[k], 16 * len(range(k, NB, 3)))
            pool.wait_ge(b_fc, 1)
            for g in range(EG):
                pool.indirect_dma_start(out=out, out_offset=bass.IndirectOffsetOnAxis(ap=idx_e[:, g:g + 1], axis=0),
                                        in_=end_ft[:, g, :], in_offset=None,
                                        bounds_check=N - 1, oob_is_err=False).then_inc(b_put, 16)

        @block.tensor
        def _(pe):
            pe.wait_ge(s_const, 16 * 6)
            pe.wait_ge(s_ones, 1)

            def weights(i, b, s):
                c = 2 * i + b
                if not (isinstance(i, int) and i == 0 and b == 0 and s < 2):
                    pe.wait_ge(l0_prod, 4 * c + s - 1)
                for k in range(2):
                    t = 2 * s + k
                    ins = pe.matmul(bank[s % 2][0:P, k * W:(k + 1) * W], hid[b][:, t * P:(t + 1) * P], w2_sb[:, :],
                                    start=True, stop=True)
                ins.then_inc(l0_w, 1)

            def hidden(i, d):
                b, c = d % 2, 2 * i + d
                pe.wait_ge(l0_in[b], 32 * (i + d // 2 + 1))
                wait_pos(pe, l0_h, c)
                for k in range(2):
                    ins = pe.matmul(bank[2 + k][0:HID, 0:CE // 2], w1_sb[:, :], ea8[b][:, k * CE // 2:(k + 1) * CE // 2],
                                    start=True, stop=True)
                ins.then_inc(l0_z, 1)

            def chunk(i, b, last=False):
                c = 2 * i + b
                pe.wait_ge(l0_h, c + 1)
                if b == 0 and isinstance(i, int) and i == 0:
                    pe.wait_ge(s_rootok, 1)
                for s in range(3):
                    weights(i, b, s)
                pe.wait_ge(l0_hx, c + 1)
                wait_pos(pe, l0_htc, c)
                for g in range(2):
                    ins = pe.transpose(bank[4][:, g * 128:g * 128 + P],
                                       hx[:, CT + 8 * g:CT + 8 * g + 8, :].rearrange("p t c -> p (t c)"),
                                       ident_sb[0:P, 0:P])
                ins.then_inc(l0_ht, 1)
                weights(i, b, 3)
                if not last:
                    hidden(i, b + 1)
                pe.wait_ge(l0_htc, c + 1)
                wait_pos(pe, l0_rootc, c)
                if b == 0 and isinstance(i, int) and i == 0:
                    pe.wait_ge(s_rootok, 3)
                for g in range(2):
                    pe.matmul(bank[5][0:P, g * 128:(g + 1) * 128], hT[:, g, :], root_sb[:, :], start=True, stop=False)
                    ins = pe.matmul(bank[5][0:P, g * 128:(g + 1) * 128], ones_row[:, :], bias_row[:, :],
                                    start=False, stop=True)
                ins.then_inc(l0_root, 1)
                pe.wait_ge(l0_msg, c + 1)
                wait_pos(pe, l0_segc, c)
                for t in range(CT):
                    pe.matmul(bank[6][0:P, t * (C + 1):(t + 1) * (C + 1)], S0[b][:, t, :], msg[b][:, t, :],
                              start=True, stop=True)
                    ins = pe.matmul(bank[7][0:C + 1, 2 * t:2 * t + 2], msg[b][:, t, :], S0[b][:, t, 0:P:P - 1],
                                    start=True, stop=True)
                ins.then_inc(l0_seg, 1)

            hidden(0, 0)
            chunk(0, 0)
            chunk(0, 1)
            with pe.Fori(1, NCH // 2 - 1) as i:
                chunk(i, 0)
                chunk(i, 1)
            chunk(NCH // 2 - 1, 0)
            chunk(NCH // 2 - 1, 1, last=True)
            pe.wait_ge(l0_run, 1)
            for g in range(EG):
                ins = pe.transpose(bank[6][0:EP, g * (C + 1):(g + 1) * (C + 1)], bound0[:, g * EP:(g + 1) * EP],
                                   ident_sb[0:C + 1, 0:C + 1])
            ins.then_inc(l0_runT, 1)

            pe.wait_ge(s_wstack, 16 * 9)
            pe.wait_ge(l1_ones, 1)
            pe.wait_ge(l0_runc, 1)

            def edge_weights(i, k, t):
                b, s = (k % 8) // 4, k % 4
                n = 8 * i + k
                if s == 0 and t == 0:
                    if isinstance(i, int):
                        pe.wait_ge(l1_in[b], 48 * (n // 8 + 1))
                    else:
                        pe.wait_ge(l1_in[b], 48 * (i + k // 8 + 1))
                wait_pos(pe, l1_e, 2 * n + t - 1)
                pe.matmul(bank[t][0:P, :], stk[b][:, (2 * s + t) * P:(2 * s + t + 1) * P], wstack[:, :],
                          start=True, stop=True).then_inc(l1_A, 1)

            def slot(i, k):
                if valid(i, k):
                    edge_weights(i, k, 0)
                if valid(i, k - 2):
                    n, q = 8 * i + k - 2, k % 2
                    pe.wait_ge(l1_M, n + 1)
                    wait_pos(pe, l1_MTc, n)
                    for t in range(2):
                        for h in range(2):
                            ins = pe.transpose(bank[3][0:P, (2 * t + h) * 128:(2 * t + h + 1) * 128],
                                               Mx[q][:, h, t * P:(t + 1) * P], ident_sb[:, :])
                    ins.then_inc(l1_MT, 1)
                if valid(i, k):
                    edge_weights(i, k, 1)
                if valid(i, k - 1):
                    n = 8 * i + k - 1
                    pe.wait_ge(l1_e, 2 * n + 2)
                    wait_pos(pe, l1_M, n)
                    for t in range(2):
                        for h in range(2):
                            ins = pe.transpose(bank[2][:, (2 * h + t) * P:(2 * h + t + 1) * P],
                                               En[(k - 1) % 8][:, t, 1, h * 128:(h + 1) * 128], ident_sb[0:P, 0:P])
                    ins.then_inc(l1_T, 1)
                if valid(i, k - 4):
                    n, q, b, s = 8 * i + k - 4, k % 2, ((k - 4) % 8) // 4, k % 4
                    pe.wait_ge(l1_ex, n + 1)
                    wait_pos(pe, l1_ln, n)
                    for t in range(2):
                        ins = pe.matmul(bank[5][0:P, t * W:(t + 1) * W], Sm[b][:, 2 * s + t, :], ex[q][:, t, :],
                                        start=True, stop=True)
                    ins.then_inc(l1_D, 1)
                if valid(i, k - 2):
                    n, q, b, s = 8 * i + k - 2, k % 2, ((k - 2) % 8) // 4, (k - 2) % 4
                    pe.wait_ge(l1_MTc, n + 1)
                    wait_pos(pe, l1_ex, n)
                    wait_pos(pe, l1_d, n)
                    pe.wait_ge(l1_L, n + 1)
                    alone = k % 4 in DVE_SUB
                    for t in range(2):
                        ins = pe.matmul(bank[4][0:P, t * W:(t + 1) * W], Lm[b][:, 2 * s + t, :], MT[q][:, t, :],
                                        start=True, stop=alone)
                        if not alone:
                            ins = pe.matmul(bank[4][0:P, t * W:(t + 1) * W], ident_sb[0:P, 0:P],
                                            En[(k - 2) % 8][:, t, 1, :], start=False, stop=True)
                    ins.then_inc(l1_B, 1)
                if valid(i, k - 5):
                    n, q, b, s = 8 * i + k - 5, (k - 5) % 2, ((k - 5) % 8) // 4, (k - 5) % 4
                    pe.wait_ge(l1_w, n + 1)
                    wait_pos(pe, l1_ac, n - 1)
                    for t in range(2):
                        ins = pe.matmul(bank[6 + q][0:P, t * W:(t + 1) * W], Sm[b][:, 2 * s + t, :], wv[q][:, t, :],
                                        start=True, stop=True)
                    ins.then_inc(l1_F, 1)

            run_slots(pe, slot)
            pe.wait_ge(b_row, 2)
            pe.wait_ge(l1_Fc, STEPS)
            for j in range(12):
                m, h, r = j // 4, j // 2 % 2, j % 2
                if j >= 8:
                    pe.wait_ge(b_Tc, j - 7)
                for g in range(4):
                    ins = pe.transpose(bank[j % 8][:, g * EP:(g + 1) * EP],
                                       rows4[(0, 2, 3)[m]][:, 4 * r + g, h * 128:(h + 1) * 128], ident_sb[0:EP, 0:EP])
                ins.then_inc(b_T, 1)
            pe.wait_ge(b_q, 1)
            for g in range(EG):
                for h in range(2):
                    ins = pe.matmul(bank[0][0:EP, g * C:(g + 1) * C], bm_a[:, h, g * EP:(g + 1) * EP], fold_sb[:, :],
                                    start=(h == 0), stop=(h == 1))
            ins.then_inc(b_f, 1)

        @block.scalar
        def _(act):
            def clear(tab, w, zeroed):
                eighth = NP * w // 8
                for k in range(8):
                    act.dma_start(tab.rearrange("(p n) c -> p (n c)", p=P)[:, k * eighth:(k + 1) * eighth],
                                  zero[:, 0:eighth]).then_inc(zeroed, 16)

            act.wait_ge(s_root0, 1)
            for n in range(8):
                act.dma_start(root_sb[n * C:(n + 1) * C, n * C:(n + 1) * C], root).then_inc(s_rootl, 16)
            act.dma_start(bias_row[0:1, :].rearrange("a (n c) -> a n c", c=C),
                          bias.rearrange("(a b n) -> a b n", a=1, b=1).broadcast_to([1, 8, C])).then_inc(s_rootl, 16)
            act.wait_ge(s_zero, 1)
            clear(agg_tab, C + 1, s_zeroed)
            for dst_ap, src_ap in (
                (lnw_sb[:, :], bcast_rows(ln_w, P, C)), (fold_sb[:, :], fold), (wf_sb[0:C, 0:W], Wm),
                (wf_sb[0:C, W:2 * W], Wa), (wf_sb[C:C + 1, 0:W], bm.rearrange("(a n) -> a n", a=1)),
                (wf_sb[C:C + 1, W:2 * W], ba.rearrange("(a n) -> a n", a=1)),
            ):
                act.dma_start(dst_ap, src_ap).then_inc(s_wf, 16)
            act.wait_ge(s_flag, 1)
            act.dma_start(flag_tab.rearrange("(p n) -> p n", p=100), dq).then_inc(s_flagst, 16)
            act.wait_ge(s_const, 16 * 6)
            act.wait_ge(s_cols, 1)
            act.wait_ge(s_flagst, 16)

            def hidden(i, d):
                b, c = d % 2, 2 * i + d
                act.wait_ge(l0_z, c + 1)
                wait_pos(act, l0_w, 4 * (c - 1))
                for k in range(2):
                    ins = nc.scalar.activation(hid[b][0:HID, k * CE // 2:(k + 1) * CE // 2],
                                               bank[2 + k][0:HID, 0:CE // 2], ACT.Silu, bias=b1_sb[:, 0:1])
                ins.then_inc(l0_h, 1)

            def chunk(i, b, last=False):
                c = 2 * i + b
                act.wait_ge(l0_ht, c + 1)
                wait_pos(act, l0_root, c)
                nc.scalar.activation(hT, bank[4][:, 0:256].rearrange("p (g e) -> p g e", g=2)[:, :, 0:P],
                                     ACT.Copy).then_inc(l0_htc, 1)
                if not last:
                    hidden(i, b + 1)
                act.wait_ge(l0_root, c + 1)
                nc.scalar.activation(rr[:, bass.ds(c * NS * C, NS * C)], bank[5][0:P, 0:NS * C],
                                     ACT.Copy).then_inc(l0_rootc, 1)
                act.wait_ge(l0_seg, c + 1)
                if not (isinstance(i, int) and i == 0):
                    act.wait_ge(l0_put[b], 128 * i)
                nc.scalar.activation(bound0[:, bass.ds(c * 2 * CT, 2 * CT)], bank[7][0:C + 1, 0:2 * CT], ACT.Copy)
                nc.scalar.activation(segs[b].rearrange("p t c -> p (t c)"), bank[6][0:P, 0:CT * (C + 1)],
                                     ACT.Copy).then_inc(l0_segc, 1)
                if b == 1:
                    act.wait_ge(sp_done, i + 1)
                    for j, k in enumerate((0, 0, 1, 1, 0, 2)):
                        act.dma_start(stack_tab[j * C:(j + 1) * C, :].rearrange("c (b n) -> (c b) n", b=8)
                                      [:, bass.ds(i * SPLITC, SPLITC)], spb[:, k, :]).then_inc(sp_out, 16)

            hidden(0, 0)
            chunk(0, 0)
            chunk(0, 1)
            clear(ft_tab, C, s_zeroed_ft)
            act.wait_ge(s_wsplit, 1)
            for j, k in enumerate((0, 1, 0, 1, 2, 0)):
                act.dma_start(wstack[j * C:(j + 1) * C, :], wpart[0:C, k, :]).then_inc(s_wstack, 16)
            for k in range(3):
                act.dma_start(wstack[6 * C + k:6 * C + k + 1, :], wpart[C:C + 1, k, :]).then_inc(s_wstack, 16)
            with act.Fori(1, NCH // 2 - 1) as i:
                chunk(i, 0)
                chunk(i, 1)
            chunk(NCH // 2 - 1, 0)
            chunk(NCH // 2 - 1, 1, last=True)
            act.wait_ge(l0_runT, 1)
            nc.scalar.activation(end_seg.rearrange("p g c -> p (g c)"), bank[6][0:EP, 0:EG * (C + 1)],
                                 ACT.Copy).then_inc(l0_runc, 1)

            for k in range(NB + 1):
                if k < NB:
                    act.wait_ge(n_row, k + 1)
                    if k:
                        act.wait_ge(n_y, k)
                    nc.scalar.activation(nq, nt[k % 3], ACT.Square).then_inc(n_sq, 1)
                if k:
                    act.wait_ge(n_z, k)
                    if k >= 3:
                        act.wait_ge(n_x1, k - 2)
                    nc.scalar.activation(ns[(k - 1) % 2], nt[(k - 1) % 3].rearrange("p n c -> p (n c)"),
                                         ACT.Silu).then_inc(n_silu, 1)
                if k >= 2:
                    act.wait_ge(n_x1, k - 1)
                    act.dma_start(x1_tab.rearrange("(p n) c -> p (n c)", p=P)[:, (k - 2) * NN * C:(k - 1) * NN * C],
                                  hb[:, (k - 2) * NN * C:(k - 1) * NN * C]).then_inc(n_out, 16)
            act.wait_ge(n_x1, NB)
            act.dma_start(x1_tab.rearrange("(p n) c -> p (n c)", p=P)[:, (NB - 1) * NN * C:],
                          hb[:, (NB - 1) * NN * C:]).then_inc(n_out, 16)
            act.preload_act_table_set("natural_log_exp_and_others")


            def rows_squared(i, d):
                act.wait_ge(l1_c, 2 * i + d + 1)
                wait_pos(act, l1_v, 2 * i + d)
                nc.scalar.activation(sq1, rows1[d % 2], ACT.Square).then_inc(l1_q, 1)

            def rows_rstd(i, d):
                c = 2 * i + d
                act.wait_ge(l1_v, c + 1)
                wait_pos(act, l1_pre, c)
                nc.scalar.activation(st1[:, 2, :], st1[:, 1, :], ACT.Ln).then_inc(s_act, 1)
                act.wait_ge(s_act, c + 1)
                nc.scalar.activation(st1[:, 2, :], st1[:, 2, :], ACT.Exp, scale=-0.5).then_inc(l1_y, 1)

            rows_squared(0, 0)
            rows_rstd(0, 0)

            def slot(i, k):
                if k == 0:
                    act.preload_act_table_set("natural_log_exp_and_others")
                if valid(i, k - 2):
                    n, q = 8 * i + k - 2, k % 2
                    act.wait_ge(l1_MT, n + 1)
                    wait_pos(act, l1_B, n - 1)
                    nc.scalar.activation(MT[q], both(bank[3][0:P, :]), ACT.Copy, scale=-1.0).then_inc(l1_MTc, 1)
                if valid(i, k - 4):
                    n, q = 8 * i + k - 4, k % 2
                    act.wait_ge(l1_D, n + 1)
                    wait_pos(act, l1_rowl[q], 8 * (n - k % 2))
                    wait_pos(act, l1_at, n - 1)
                    nc.scalar.activation(lnd[q], both(bank[5][0:P, :]), ACT.Ln).then_inc(l1_ln, 1)
                    act.wait_ge(l1_ln, n + 1)
                    nc.scalar.activation(Rd[q], lnd[q], ACT.Exp, scale=-1.0).then_inc(l1_R, 1)
                if valid(i, k - 6):
                    n, q = 8 * i + k - 6, (k - 6) % 2
                    act.wait_ge(l1_F, n + 1)
                    wait_pos(act, l1_rowa[q], 8 * (n - (k - 6) % 2))
                    wait_pos(act, l1_Fc, n - 1)
                    nc.scalar.activation(asum[q], bank[6 + q][0:P, :], ACT.Copy).then_inc(l1_ac, 1)
                if valid(i, k - 1):
                    n, b, s = 8 * i + k - 1, ((k - 1) % 8) // 4, (k - 1) % 4
                    act.wait_ge(l1_S, 2 * i + (k - 1) // 4 + 1)
                    wait_pos(act, l1_B, n - 7)
                    for t in range(2 * s, 2 * s + 2):
                        ins = nc.scalar.activation(Lm[b][:, t, :], Sm[b][:, t, :], ACT.Copy,
                                                   scale=dc1[b][:, 1, t:t + 1])
                    ins.then_inc(l1_L, 1)
                if valid(i, k - 2):
                    n, q = 8 * i + k - 2, k % 2
                    wait_pos(act, l1_at, n - 1)
                    if k % 4 in DVE_SUB:
                        act.wait_ge(l1_d, n + 1)
                        nc.scalar.activation(ex[q], dd[q], ACT.Exp).then_inc(l1_ex, 1)
                    else:
                        act.wait_ge(l1_B, n + 1)
                        nc.scalar.activation(ex[q], both(bank[4][0:P, :]), ACT.Exp).then_inc(l1_ex, 1)
                        wait_pos(act, l1_rowd[q], 16 * (n - k % 2))
                        nc.scalar.activation(dd[q], both(bank[4][0:P, :]), ACT.Copy).then_inc(l1_d, 1)
                if k % 4 == 1 and valid(i, k + 3):
                    rows_squared(i, k // 4 + 1)
                if k % 4 == 2 and valid(i, k + 2):
                    rows_rstd(i, k // 4 + 1)

            run_slots(act, slot)
            act.wait_ge(b_in, 64)
            nc.scalar.activation(rows4[2], rows4[2], ACT.Exp).then_inc(b_row, 1)
            for j in range(12):
                m, h, r = j // 4, j // 2 % 2, j % 2
                act.wait_ge(b_T, j + 1)
                nc.scalar.activation(bound1[:, m, h, r * 4 * EP:(r + 1) * 4 * EP], bank[j % 8][:, 0:4 * EP],
                                     ACT.Copy).then_inc(b_Tc, 1)
            act.wait_ge(b_d, 1)
            nc.scalar.activation(bm_c[:, :, :], bm_c[:, :, :], ACT.Exp).then_inc(b_x, 1)
            nc.scalar.activation(bm_w[:, :, :], bm_w[:, :, :], ACT.Exp).then_inc(b_x, 1)
            for h in range(2):
                act.wait_ge(b_s, h + 1)
                nc.scalar.activation(bm_r[:, h, :], bm_x[:, h, :], ACT.Ln).then_inc(b_ln, 1)
                act.wait_ge(b_ln, h + 1)
                nc.scalar.activation(bm_r[:, h, :], bm_r[:, h, :], ACT.Exp, scale=-1.0).then_inc(b_r, 1)

        @block.vector
        def _(dve):
            ch = Chain(s_dve)
            V = nc.vector

            def link(ins):
                ins.then_inc(s_dve, 1)
                dve.wait_ge(s_dve, ch.next())

            def rstd(y, v, t, total):
                link(V.tensor_scalar(v, total, 1.0 / C, EPS, ALU.mult, ALU.add))
                link(V.tensor_scalar(y.bitcast(I32), v.bitcast(I32), -0.5, 1597463007.0, ALU.mult, ALU.add))
                for _ in range(3):
                    link(V.scalar_tensor_tensor(t, y, -0.5, v, ALU.mult, ALU.mult))
                    link(V.tensor_tensor(t, t, y, ALU.mult))
                    link(V.scalar_tensor_tensor(y, t, 1.5, y, ALU.add, ALU.mult))

            def mark(ins):
                ins.then_inc(s_dve, 1)
                return ch.next()

            def wide(a, rows):
                return a.rearrange("p (n a) -> p n a", a=1).broadcast_to([P, rows, C])

            V.memset(d_next, -1).then_inc(s_pad, 1)
            for b in range(2):
                V.memset(hid[b][HID:HID + 1, :], 1.0)
                V.memset(msg[b][:, :, C:C + 1], 1.0)
            V.memset(ones_row[:, :], 1.0).then_inc(s_ones, 1)
            dve.wait_ge(s_dload, 16 * 8)
            link(V.tensor_copy(c1, d_i))
            link(V.tensor_copy(col_f[:, :, 0, :], c1.rearrange("p (c t) -> p c t", t=CT)))
            link(V.tensor_tensor(c2, d_i, d_next, ALU.not_equal))
            link(V.tensor_copy(col_f[:, :, 1, :], c2.rearrange("p (c t) -> p c t", t=CT)))
            V.tensor_tensor(c3, d_i, d_first, ALU.not_equal)
            link(V.tensor_tensor(c4, d_i, d_last, ALU.not_equal))
            link(V.tensor_tensor(c3, c3, c4, ALU.mult))
            link(V.tensor_tensor(c3, c3, c2, ALU.mult))
            link(V.scalar_tensor_tensor(c4, c1, -SKIP, c3, ALU.add, ALU.mult))
            link(V.tensor_scalar(col_i.rearrange("p c t -> p (c t)"), c4, SKIP, None, ALU.add))
            V.memset(same_e[:, 0:1], 0.0)
            V.memset(live_e[:, :], 1.0)
            link(V.tensor_tensor(same_e[:, 1:], e_b[:, 1:], e_b[:, :-1], ALU.is_equal))
            pairs = same_e[:, :].rearrange("p (t q) -> p t q", q=2)
            link(V.tensor_scalar(live_e[:, :].rearrange("p (t q) -> p t q", q=2)[:, :, 1:2], pairs[:, :, 1:2],
                                 -1.0, 1.0, ALU.mult, ALU.add))
            link(V.tensor_tensor(e_1, e_c, e_n, ALU.not_equal))
            link(V.tensor_copy(e_2, e_c))
            link(V.scalar_tensor_tensor(e_2, e_2, -SKIP, e_1, ALU.add, ALU.mult))
            link(V.tensor_scalar(idx_e[:, :], e_2, SKIP, None, ALU.add))
            link(V.tensor_scalar(idx_x[:, :], e_2, SKIP, float(N - 1), ALU.add, ALU.min))
            V.memset(dq.rearrange("p (t e) -> p t e", e=P)[:, :, 0:1], 0.0)
            d3 = dn.rearrange("p (t e) -> p t e", e=P)
            link(V.tensor_tensor(dq.rearrange("p (t e) -> p t e", e=P)[:, :, 1:], d3[:, :, 1:], d3[:, :, :-1],
                                 ALU.is_equal))
            link(V.tensor_scalar(dq, dq, 2.0, -1.0, ALU.mult, ALU.add))
            V.tensor_scalar(dq, dq, BIG, None, ALU.mult).then_inc(s_flag, 1)
            V.memset(sc0[0], 0).then_inc(s_cols, 1)

            def centre(a, rows, groups, nth):
                m = cen[0:rows, 0:groups]
                a3 = a.rearrange("p (g o) -> p g o", o=C)
                link(V.tensor_reduce(m, a3, X, ALU.add))
                V.scalar_tensor_tensor(a3, m.rearrange("p (g a) -> p g a", a=1).broadcast_to([rows, groups, C]),
                                       -1.0 / C, a3, ALU.mult, ALU.add).then_inc(s_rootok, 1)
                dve.wait_ge(s_rootok, nth)

            dve.wait_ge(s_const, 16 * 6)
            centre(w2_sb[:, :], HID + 1, C, 1)
            dve.wait_ge(s_rootl, 16 * 9)
            centre(root_sb[:, :], 128, 8, 2)
            centre(bias_row[:, :], 1, 8, 3)

            R = CT + NS

            def layernorm(xi):
                tot, v, y, t = (st[:, k, :] for k in range(4))
                link(V.tensor_reduce(tot, xi, X, ALU.add))
                link(V.scalar_tensor_tensor(xi, wide(tot, R), -1.0 / C, xi, ALU.mult, ALU.add))
                link(V.tensor_tensor(sq, xi, xi, ALU.mult))
                link(V.tensor_reduce(tot, sq, X, ALU.add))
                rstd(y, v, t, tot)
                return y

            def chunk(i, b):
                c = 2 * i + b
                dve.wait_ge(l0_got[b], 128 * (i + 1))
                dve.wait_ge(l0_x[b], 32 * (i + 1))
                y = layernorm(xin[b])
                if not (isinstance(i, int) and i == 0 and b == 0):
                    dve.wait_ge(l0_ht, c)
                V.scalar_tensor_tensor(hx, xin[b], 0.0, wide(y, R), ALU.max, ALU.mult).then_inc(l0_hx, 1)
                dve.wait_ge(l0_hx, c + 1)
                V.tensor_tensor(hb[:, bass.ds(c * NS * C, NS * C)].rearrange("p (n c) -> p n c", c=C), hx[:, CT:, :],
                                lnb_sb[:, :].rearrange("p (a c) -> p a c", a=1).broadcast_to([P, NS, C]), ALU.add)
                link(V.tensor_copy(dc0, col_f[:, bass.ds(c, 1), 0, :].rearrange("p a t -> p (a t)")))
                if not (isinstance(i, int) and i == 0):
                    dve.wait_ge(l0_seg, c - 1)
                dve.wait_ge(l0_in[b], 32 * (i + 1))
                V.tensor_tensor(S0[b], dstb[b].rearrange("p (t e) -> p t e", e=P),
                                dc0.rearrange("p (t a) -> p t a", a=1).broadcast_to([P, CT, P]), ALU.is_equal)
                for s in range(4):
                    dve.wait_ge(l0_w, 4 * c + s + 1)
                    V.tensor_tensor(prod[s % 2].rearrange("p (r o) -> p r o", o=C),
                                    bank[s % 2][0:P, :].rearrange("p (r o) -> p r o", o=C),
                                    hx[:, 2 * s:2 * s + 2, :].rearrange("p t (c a) -> p (t c) a", a=1)
                                    .broadcast_to([P, 2 * C, C]), ALU.mult).then_inc(l0_prod, 1)
                    dve.wait_ge(l0_prod, 4 * c + s + 1)
                    ins = V.tensor_reduce(msg[b][:, 2 * s:2 * s + 2, 0:C],
                                          prod[s % 2].rearrange("p (t i o) -> p t o i", t=2, i=C), X, ALU.add)
                ins.then_inc(l0_msg, 1)
                if not (isinstance(i, int) and i == 0):
                    dve.wait_ge(l0_put[b], 128 * i)
                V.tensor_copy(sc0[b], col_i[:, bass.ds(c, 1), :].rearrange("p a t -> p (a t)")).then_inc(l0_sc, 1)
                if b == 1:
                    dve.wait_ge(sp_in, 16 * (i + 1))
                    if not (isinstance(i, int) and i == 0):
                        dve.wait_ge(sp_out, 96 * i)
                    link(V.tensor_copy(spb[:, 0, :], spx))
                    link(V.tensor_tensor(spr, spx, spb[:, 0, :], ALU.subtract))
                    link(V.tensor_copy(spb[:, 1, :], spr))
                    link(V.tensor_tensor(spr, spr, spb[:, 1, :], ALU.subtract))
                    V.tensor_copy(spb[:, 2, :], spr).then_inc(sp_done, 1)

            before = ch.count
            chunk(0, 0)
            chunk(0, 1)
            per = ch.count - before
            dve.wait_ge(s_wf, 16 * 6)
            link(V.tensor_copy(wpart[:, 0, :], wf_sb[:, :]))
            link(V.tensor_tensor(wres[:, :], wf_sb[:, :], wpart[:, 0, :], ALU.subtract))
            link(V.tensor_copy(wpart[:, 1, :], wres[:, :]))
            link(V.tensor_tensor(wres[:, :], wres[:, :], wpart[:, 1, :], ALU.subtract))
            V.tensor_copy(wpart[:, 2, :], wres[:, :]).then_inc(s_wsplit, 1)
            with dve.Fori(1, NCH // 2) as i:
                ch.enter(i, 1, per)
                chunk(i, 0)
                chunk(i, 1)
            ch.leave(NCH // 2 - 1)
            dve.wait_ge(l0_segc, NCH)
            link(V.tensor_tensor(bound0[:, :], bound0[:, :], live_e[0:C + 1, :], ALU.mult))
            V.tensor_tensor_scan(bound0[:, :], same_e[0:C + 1, :], bound0[:, :], 0.0, ALU.mult, ALU.add
                                 ).then_inc(l0_run, 1)

            cnt, rc, tot, v, y, t = (nst[:, j, :] for j in range(6))

            def mean_and_root(k):
                a, r = ag[k % 2], nt[k % 3]
                dve.wait_ge(n_in[k % 2], 16 * (k // 2 + 1))
                link(V.tensor_scalar(cnt, a[:, :, C:C + 1].rearrange("p n a -> p (n a)"), 1.0, None, ALU.max))
                link(V.reciprocal(rc, cnt))
                if k >= 3:
                    dve.wait_ge(n_silu, k - 2)
                link(V.tensor_tensor(r, a[:, :, 0:C], wide(rc, NN), ALU.mult))
                V.tensor_tensor(r, r, rr[:, k * NN * C:(k + 1) * NN * C].rearrange("p (n c) -> p n c", c=C),
                                ALU.add).then_inc(n_row, 1)

            def normalise(k):
                dve.wait_ge(n_sq, k + 1)
                link(V.tensor_reduce(tot, nq, X, ALU.add))
                rstd(y, v, t, tot)
                V.tensor_tensor(nt[k % 3], nt[k % 3], wide(y, NN), ALU.mult).then_inc(n_y, 1)
                dve.wait_ge(n_y, k + 1)

            mean_and_root(0)
            for k in range(NB):
                if k + 1 < NB:
                    mean_and_root(k + 1)
                normalise(k)

            dve.wait_ge(n_x1, NB)
            for b in range(2):
                ins = V.memset(stk[b][6 * C:6 * C + 3, :], 1.0)
            ins.then_inc(l1_ones, 1)

            tot1, v1, y1, t1, u1 = (st1[:, j, :] for j in range(5))

            def rows_sum(i, d):
                dve.wait_ge(l1_got[d % 2], 128 * (i + d // 2 + 1))
                return mark(V.tensor_reduce(tot1, rows1[d % 2], X, ALU.add))

            def rows_centred(i, d, after):
                xi = rows1[d % 2]
                dve.wait_ge(s_dve, after)
                V.scalar_tensor_tensor(xi, wide(tot1, CT), -1.0 / C, xi, ALU.mult, ALU.add).then_inc(l1_c, 1)

            def rows_squares(i, d):
                dve.wait_ge(l1_q, 2 * i + d + 1)
                return mark(V.tensor_reduce(tot1, sq1, X, ALU.add))

            def rows_variance(i, d, after):
                dve.wait_ge(s_dve, after)
                V.tensor_scalar(v1, tot1, 1.0 / C, EPS, ALU.mult, ALU.add).then_inc(l1_v, 1)

            def newton_a(i, d):
                dve.wait_ge(l1_y, 2 * i + d + 1)
                return mark(V.scalar_tensor_tensor(t1, y1, -0.5, v1, ALU.mult, ALU.mult))

            def newton_b(after):
                dve.wait_ge(s_dve, after)
                return mark(V.tensor_tensor(t1, t1, y1, ALU.mult))

            def newton_c(after):
                dve.wait_ge(s_dve, after)
                return mark(V.scalar_tensor_tensor(u1, t1, 1.5, y1, ALU.add, ALU.mult))

            def rows_relu(i, d, after):
                c, b = 2 * i + d, d % 2
                dve.wait_ge(s_dve, after)
                V.scalar_tensor_tensor(h1[b], rows1[b], 0.0, wide(u1, CT), ALU.max, ALU.mult).then_inc(l1_pre, 1)
                wait_pos(dve, l1_L, 4 * (c - 1))
                link(V.tensor_copy(dc1[b], col_f[:, bass.ds(c, 1), :, :].rearrange("p a k t -> p (a k) t")))

            def same_segment(i, b):
                c = 2 * i + b
                wait_pos(dve, l1_F, 4 * (c - 1))
                V.tensor_tensor(Sm[b], dsb[b].rearrange("p (t e) -> p t e", e=P),
                                dc1[b][:, 0, :].rearrange("p (t a) -> p t a", a=1).broadcast_to([P, CT, P]),
                                ALU.is_equal).then_inc(l1_S, 1)

            def slot(i, k):
                if valid(i, k):
                    n, b, s = 8 * i + k, k // 4, k % 4
                    wait_pos(dve, l1_rowd[k % 2], 16 * (n - 6 - k % 2))
                    if k % 4 == 0:
                        dve.wait_ge(l1_pre, 2 * i + b + 1)
                for t in range(2):
                    if valid(i, k):
                        dve.wait_ge(l1_A, 2 * n + t + 1)
                        V.tensor_tensor(En[k % 8][:, t, :, :].rearrange("p m (i o) -> p m i o", o=C),
                                        bank[t][0:P, :].rearrange("p (m i o) -> p m i o", m=2, o=C),
                                        h1[b][:, 2 * s + t, :].rearrange("p (m i o) -> p m i o", m=1, o=1)
                                        .broadcast_to([P, 2, C, C]), ALU.mult).then_inc(l1_e, 1)
                    n5, q5 = 8 * i + k - 5, (k - 5) % 2
                    if t == 0 and valid(i, k - 5):
                        dve.wait_ge(l1_at, n5 + 1)
                        wait_pos(dve, l1_F, n5 - 1)
                        V.tensor_tensor(wv[q5], at, En[(k - 5) % 8][:, :, 0, :], ALU.mult).then_inc(l1_w, 1)
                if k % 4 == 1 and valid(i, k - 9):
                    c, b = 2 * i + (k - 9) // 4, ((k - 9) % 8) // 4
                    wait_pos(dve, l1_put[b], 128 * (i + (k - 9) // 8))
                    V.tensor_copy(sc1[b], col_i[:, bass.ds(c, 1), :].rearrange("p a t -> p (a t)")).then_inc(l1_sc, 1)
                ln, d = valid(i, k - k % 4 + 4), k // 4 + 1
                if ln and k % 4 == 1:
                    m = rows_sum(i, d)
                if ln and k % 4 == 2:
                    m = rows_squares(i, d)
                if ln and k % 4 == 3:
                    m = newton_a(i, d)
                if valid(i, k - 1):
                    n, b, s, q = 8 * i + k - 1, ((k - 1) % 8) // 4, (k - 1) % 4, (k - 1) % 2
                    dve.wait_ge(l1_T, n + 1)
                    wait_pos(dve, l1_MT, n - 1)
                    for h in range(2):
                        ins = V.tensor_tensor_scan(Mx[q][:, h, :], flg[b][:, 2 * s * P:(2 * s + 2) * P],
                                                   bank[2][:, h * 2 * P:(h + 1) * 2 * P], 0.0, ALU.min, ALU.max)
                    ins.then_inc(l1_M, 1)
                if ln and k % 4 == 1:
                    rows_centred(i, d, m)
                if ln and k % 4 == 2:
                    rows_variance(i, d, m)
                if ln and k % 4 == 3:
                    m = newton_b(m)
                if ln and k % 4 == 3:
                    m = newton_c(m)
                if k % 4 in DVE_SUB and valid(i, k - 2):
                    n, q = 8 * i + k - 2, k % 2
                    dve.wait_ge(l1_B, n + 1)
                    wait_pos(dve, l1_ex, n - 1)
                    wait_pos(dve, l1_rowd[q], 16 * (n - k % 2))
                    V.tensor_tensor(dd[q], En[(k - 2) % 8][:, :, 1, :], both(bank[4][0:P, :]), ALU.add
                                    ).then_inc(l1_d, 1)
                if valid(i, k - 4):
                    n, q = 8 * i + k - 4, k % 2
                    dve.wait_ge(l1_R, n + 1)
                    wait_pos(dve, l1_w, n)
                    V.tensor_tensor(at, ex[q], Rd[q], ALU.mult).then_inc(l1_at, 1)
                if valid(i, k - 6):
                    n, b, s, q = 8 * i + k - 6, ((k - 6) % 8) // 4, (k - 6) % 4, k % 2
                    dve.wait_ge(l1_ac, n + 1)
                    if s == 0:
                        wait_pos(dve, l1_put[b], 128 * (i + (k - 6) // 8))
                    V.tensor_reduce(fts[b][:, 2 * s:2 * s + 2, :],
                                    asum[q].rearrange("p (t i o) -> p t o i", t=2, i=C), X, ALU.add
                                    ).then_inc(l1_Fc, 1)
                if ln and k % 4 == 3:
                    rows_relu(i, d, m)
                if valid(i, k) and k % 4 == 0:
                    same_segment(i, k // 4)

            m = rows_sum(0, 0)
            rows_centred(0, 0, m)
            m = rows_squares(0, 0)
            rows_variance(0, 0, m)
            m = newton_a(0, 0)
            m = newton_b(m)
            m = newton_c(m)
            rows_relu(0, 0, m)
            run_slots(dve, slot, ch, LINKS1)

            dve.wait_ge(b_in, 64)
            V.tensor_tensor(rows4[0], rows4[0], rows4[1], ALU.subtract).then_inc(b_row, 1)
            V.tensor_scalar(bm_nf, live_e[:, :], 2.0, -1.0, ALU.mult, ALU.add)
            link(V.tensor_scalar(bm_sf, same_e[:, :], 2.0, -1.0, ALU.mult, ALU.add))
            V.tensor_scalar(bm_nf, bm_nf, BIG, None, ALU.mult)
            link(V.tensor_scalar(bm_sf, bm_sf, BIG, None, ALU.mult))
            dve.wait_ge(b_Tc, 12)
            V.memset(bm_c[:, :, 0:1], 0.0)
            for h in range(2):
                link(V.tensor_tensor(bm_m[:, h, :], bound1[:, 0, h, :], bm_nf, ALU.min))
                link(V.tensor_tensor_scan(bm_x[:, h, :], bm_sf, bm_m[:, h, :], 0.0, ALU.min, ALU.max))
                link(V.tensor_tensor(bm_c[:, h, 1:], bm_x[:, h, :-1], bm_x[:, h, 1:], ALU.subtract))
                link(V.tensor_scalar(bm_c[:, h, :], bm_c[:, h, :], 0.0, None, ALU.min))
                ins = V.tensor_tensor(bm_w[:, h, :], bm_m[:, h, :], bm_x[:, h, :], ALU.subtract)
            ins.then_inc(b_d, 1)
            dve.wait_ge(b_x, 2)
            for h in range(2):
                link(V.tensor_tensor(bm_c[:, h, :], bm_c[:, h, :], same_e[:, :], ALU.mult))
                link(V.tensor_tensor(bm_w[:, h, :], bm_w[:, h, :], bound1[:, 1, h, :], ALU.mult))
                link(V.tensor_tensor(bm_a[:, h, :], bm_w[:, h, :], bound1[:, 2, h, :], ALU.mult))
                V.tensor_tensor_scan(bm_x[:, h, :], bm_c[:, h, :], bm_w[:, h, :], 0.0, ALU.mult, ALU.add
                                     ).then_inc(b_s, 1)
                link(V.tensor_tensor_scan(bm_m[:, h, :], bm_c[:, h, :], bm_a[:, h, :], 0.0, ALU.mult, ALU.add))
            for h in range(2):
                dve.wait_ge(b_r, h + 1)
                ins = V.tensor_tensor(bm_a[:, h, :], bm_m[:, h, :], bm_r[:, h, :], ALU.mult)
            ins.then_inc(b_q, 1)
            dve.wait_ge(b_f, 1)
            dve.wait_ge(b_x1, 16 * EG)
            V.tensor_tensor(end_ft.rearrange("p g c -> p (g c)"), bank[0][0:EP, 0:EG * C],
                            end_x1.rearrange("p g c -> p (g c)"), ALU.add).then_inc(b_fc, 1)


_OUTS = [((N, C), 'float32')]


def kernel(**inputs):
    import numpy as _np
    import concourse.bacc as _bacc
    from concourse import mybir as _mybir
    from concourse.bass_utils import run_bass_kernel_spmd as _run

    nc = _bacc.Bacc("TRN2", target_bir_lowering=False, num_devices=1)
    a = {k: _np.asarray(v) for k, v in inputs.items()}
    dst_tiles = a["dst"].reshape(T, P)
    ends = _np.concatenate([dst_tiles[:, [0, P - 1]].reshape(-1), _np.full(1, -1, a["dst"].dtype)])
    sent = {
        "x": a["x"], "src_cols": a["src"].reshape(T, P).T, "dst": a["dst"], "dst_cols": dst_tiles.T,
        "ends": ends,
        "end_cols": _np.concatenate([ends[:-1].reshape(EG, EP).T, ends[1:].reshape(EG, EP).T]),
        "ea16T": a["edge_attr_16"].T, "ea8T": a["edge_attr_8"].T,
        "W1": a["L0_gnn_W1"], "b1": a["L0_gnn_b1"], "W2": a["L0_gnn_W2"], "b2": a["L0_gnn_b2"],
        "root": a["L0_gnn_root"], "bias": a["L0_gnn_bias"], "ln_w": a["L0_gnn_ln_w"], "ln_b": a["L0_gnn_ln_b"],
        "Wm": a["L1_gnn_W_msg"], "bm": a["L1_gnn_b_msg"], "Wa": a["L1_gnn_W_attn"], "ba": a["L1_gnn_b_attn"],
        "ident": _np.eye(128, dtype=_np.float32),
        "fold": _np.tile(_np.eye(C, dtype=_np.float32), (8, 1)),
    }
    arrays, args = {}, []
    for name, value in sent.items():
        value = _np.ascontiguousarray(value)
        arrays[f"in_{name}_dram"] = value
        args.append(nc.dram_tensor(f"in_{name}_dram", value.shape, _mybir.dt.from_np(value.dtype),
                                   kind="ExternalInput").ap())
    for i, (shape, dtype) in enumerate(_OUTS):
        args.append(nc.dram_tensor(f"out_{i}_dram", shape, _mybir.dt.from_np(_np.dtype(dtype)),
                                   kind="ExternalOutput").ap())
    gnn_kernel(nc, *args)
    r = _run(nc, [arrays], core_ids=[0])
    return r.results[0]["out_0_dram"]
```
